# Optimizing a Trainium2 kernel written in Bass

```python
import numpy as np
import jax
import jax.numpy as jnp

def _softmax(x, axis=-1):
    return jax.nn.softmax(x, axis=axis)

def _gelu(x):
    return jax.nn.gelu(x, approximate=True)

def _silu(x):
    return jax.nn.silu(x)

def _sigmoid(x):
    return jax.nn.sigmoid(x)

def _layernorm(x, axis=-1, eps=1e-05):
    m = jnp.mean(x, axis=axis, keepdims=True)
    v = jnp.var(x, axis=axis, keepdims=True)
    return (x - m) / jnp.sqrt(v + eps)

def _scatter_add(tgt, idx, src, axis=0):
    return tgt.at[idx].add(src)

def _segment_sum(src, seg, n):
    return jax.ops.segment_sum(src, seg, n)
kernel_name = 'mk_flamingo_gated_d2_seqx_r8_606c4e'

def setup_inputs(seed: int=0):
    np.random.seed(seed)
    _w = jnp.asarray

    def _rec_inputs():
        import jax
        import jax.numpy as jnp
        _rk = jax.random.key(seed)
        x = 7.22e-05 + 1 * jax.random.normal(jax.random.fold_in(_rk, 1), (128, 64, 128), jnp.float32)
        _lenS = 64 - jax.random.randint(jax.random.fold_in(_rk, 7), (128,), 0, max(1, 64 // 4) + 1, jnp.int32)
        _lenS2 = 64 - jax.random.randint(jax.random.fold_in(_rk, 8), (128,), 0, max(1, 64 // 4) + 1, jnp.int32)
        _ctx_1024P = jax.random.normal(jax.random.fold_in(_rk, 11), (128, 16, 128), jnp.float32)
        _ctx_1024c = jax.random.dirichlet(jax.random.fold_in(_rk, 511), 0.3 * jnp.ones((16,), jnp.float32), (128, 64))
        _ctx_1024t = jnp.einsum('bsk,bkd->bsd', _ctx_1024c, _ctx_1024P)
        _ctx_1024t = _ctx_1024t * jax.lax.rsqrt(jnp.mean(jnp.square(_ctx_1024t)) + 1e-12) * 0.953939
        ctx_1024 = 4.13588e-05 + 0.999923 * (_ctx_1024t + 0.3 * jax.random.normal(jax.random.fold_in(_rk, 611), (128, 64, 128), jnp.float32))
        _validS = jnp.arange(64)[None, :] < _lenS[:, None]
        _validS2 = jnp.arange(64)[None, :] < _lenS2[:, None]
        _causal = jnp.tril(jnp.ones((64, 64), dtype=bool))
        mask_1x1xSxS2_ff0 = jnp.where(jnp.ones((1, 1, 64, 64), dtype=bool), 0.0, -1000000000.0).astype(jnp.float32)
        mask_BxS2_bk1 = jnp.broadcast_to(_validS2[:, :], (128, 64))
        _g = jax.random.normal(jax.random.fold_in(_rk, 9001), (2, 2), jnp.float32)
        _g = jnp.sign(_g) * jnp.maximum(jnp.abs(_g), 1.0) + (_g == 0) * 1.0
        g_xattn = _g[0]
        g_ffn = _g[1]
        return (x, ctx_1024, mask_1x1xSxS2_ff0, mask_BxS2_bk1, g_xattn, g_ffn)
    x, ctx_1024, mask_1x1xSxS2_ff0, mask_BxS2_bk1, g_xattn, g_ffn = _rec_inputs()

    def _L0_xattn_setup():
        import jax, jax.numpy as jnp
        import numpy as np
        D_MODEL = 128
        NUM_HEADS = 16
        D_QKV = D_MODEL // NUM_HEADS
        B, S = (4, 256)
        FMAX = jnp.finfo(jnp.float32).max

        def _split_heads(x):
            b, s, _ = x.shape
            return x.reshape(b, s, NUM_HEADS, D_QKV).transpose(0, 2, 1, 3)
        key = jax.random.key(seed)
        ks = jax.random.split(key, 12)
        s = 1.0 / np.sqrt(D_MODEL)
        return {'q_in': jax.random.normal(ks[0], (B, S, D_MODEL), jnp.float32), 'k_in': jax.random.normal(ks[1], (B, S, D_MODEL), jnp.float32), 'v_in': jax.random.normal(ks[2], (B, S, D_MODEL), jnp.float32), 'mask': jnp.zeros((1, 1, S, S), jnp.float32), 'Wq': jax.random.normal(ks[3], (D_MODEL, D_MODEL), jnp.float32) * s, 'bq': jnp.zeros((D_MODEL,), jnp.float32), 'Wk': jax.random.normal(ks[4], (D_MODEL, D_MODEL), jnp.float32) * s, 'bk': jnp.zeros((D_MODEL,), jnp.float32), 'Wv': jax.random.normal(ks[5], (D_MODEL, D_MODEL), jnp.float32) * s, 'bv': jnp.zeros((D_MODEL,), jnp.float32), 'Wo': jax.random.normal(ks[6], (D_MODEL, D_MODEL), jnp.float32) * s, 'bo': jnp.zeros((D_MODEL,), jnp.float32)}
    _L0_xattn_all = _L0_xattn_setup()
    _L0_xattn_in = {k: v for k, v in _L0_xattn_all.items() if k in ('Wq', 'bq', 'Wk', 'bk', 'Wv', 'bv', 'Wo', 'bo')}
    del _L0_xattn_all

    def _L0_ffn_setup():
        import math
        import jax, jax.numpy as jnp
        import numpy as np
        TOP_K = 2
        _GELU_C = math.sqrt(2.0 / math.pi)

        def gelu_new(x):
            return 0.5 * x * (1.0 + jnp.tanh(_GELU_C * (x + 0.044715 * x * x * x)))
        key = jax.random.key(seed)
        ks = jax.random.split(key, 6)
        B, T, C, E, H = (2, 256, 128, 8, 512)
        s_in = 1.0 / math.sqrt(C)
        s_hid = 1.0 / math.sqrt(H)
        return {'x': jax.random.normal(ks[0], (B, T, C), dtype=jnp.float32), 'router_w': jax.random.normal(ks[1], (E, C), dtype=jnp.float32) * s_in, 'w_fc': jax.random.normal(ks[2], (E, C, H), dtype=jnp.float32) * s_in, 'b_fc': jax.random.normal(ks[3], (E, H), dtype=jnp.float32) * 0.02, 'w_proj': jax.random.normal(ks[4], (E, H, C), dtype=jnp.float32) * s_hid, 'b_proj': jax.random.normal(ks[5], (E, C), dtype=jnp.float32) * 0.02}
    _L0_ffn_all = _L0_ffn_setup()
    _L0_ffn_in = {k: v for k, v in _L0_ffn_all.items() if k in ('router_w', 'w_fc', 'b_fc', 'w_proj', 'b_proj')}
    del _L0_ffn_all

    def _L1_xattn_setup():
        import jax, jax.numpy as jnp
        import numpy as np
        B, SQ, SK, DQ, DKV, DH, DV = (8, 256, 256, 128, 128, 128, 128)
        ks = jax.random.split(jax.random.key(seed), 10)
        q = jax.random.normal(ks[0], (B, SQ, DQ), dtype=jnp.float32)
        k = jax.random.normal(ks[1], (B, SK, DKV), dtype=jnp.float32)
        v = jax.random.normal(ks[2], (B, SK, DKV), dtype=jnp.float32)
        mask = jax.random.randint(ks[3], (B, SK), 0, 2).astype(jnp.bool_)
        s = 1.0 / np.sqrt(DQ)
        Wq = jax.random.normal(ks[4], (DQ, DH), dtype=jnp.float32) * s
        bq = jnp.zeros((DH,), dtype=jnp.float32)
        Wk = jax.random.normal(ks[5], (DKV, DH), dtype=jnp.float32) * s
        bk = jnp.zeros((DH,), dtype=jnp.float32)
        Wv = jax.random.normal(ks[6], (DKV, DV), dtype=jnp.float32) * s
        bv = jnp.zeros((DV,), dtype=jnp.float32)
        return {'q': q, 'k': k, 'v': v, 'mask': mask, 'Wq': Wq, 'bq': bq, 'Wk': Wk, 'bk': bk, 'Wv': Wv, 'bv': bv}
    _L1_xattn_all = _L1_xattn_setup()
    _L1_xattn_in = {k: v for k, v in _L1_xattn_all.items() if k in ('Wq', 'bq', 'Wk', 'bk', 'Wv', 'bv')}
    del _L1_xattn_all

    def _L1_ffn_setup():
        import jax, jax.numpy as jnp
        import numpy as np
        QMIN, QMAX = (-128.0, 127.0)

        def _affine_quantize(x):
            amin, amax = (jnp.min(x), jnp.max(x))
            scale = jnp.maximum((amax - amin) / 255.0, 1e-08)
            zp = jnp.clip(jnp.round(-amin / scale) + QMIN, QMIN, QMAX)
            q = jnp.clip(jnp.round(x / scale) + zp, QMIN, QMAX)
            return (q, scale, zp)

        def _sym_quantize(w):
            scale = jnp.maximum(jnp.max(jnp.abs(w)) / 127.0, 1e-08)
            q = jnp.clip(jnp.round(w / scale), -127.0, 127.0)
            return (q, scale)

        def _qlinear(x, W, b):
            xq, sx, zx = _affine_quantize(x)
            wq, sw = _sym_quantize(W)
            acc = jnp.einsum('bsh,oh->bso', xq - zx, wq)
            return acc * (sx * sw) + b
        key = jax.random.key(seed)
        k1, k2, k3, k4, k5 = jax.random.split(key, 5)
        d, h = (128, 512)
        x = jax.random.normal(k1, (4, 512, d), dtype=jnp.float32)
        W1 = jax.random.normal(k2, (h, d), dtype=jnp.float32) * (1.0 / np.sqrt(d))
        b1 = jax.random.normal(k3, (h,), dtype=jnp.float32) * 0.02
        W2 = jax.random.normal(k4, (d, h), dtype=jnp.float32) * (1.0 / np.sqrt(h))
        b2 = jax.random.normal(k5, (d,), dtype=jnp.float32) * 0.02
        return {'x': x, 'W1': W1, 'b1': b1, 'W2': W2, 'b2': b2}
    _L1_ffn_all = _L1_ffn_setup()
    _L1_ffn_in = {k: v for k, v in _L1_ffn_all.items() if k in ('W1', 'b1', 'W2', 'b2')}
    del _L1_ffn_all
    return {'x': x, 'ctx_1024': ctx_1024, 'mask_1x1xSxS2_ff0': mask_1x1xSxS2_ff0, 'mask_BxS2_bk1': mask_BxS2_bk1, 'g_xattn': g_xattn, 'g_ffn': g_ffn, 'L0_xattn_Wq': _L0_xattn_in['Wq'], 'L0_xattn_bq': _L0_xattn_in['bq'], 'L0_xattn_Wk': _L0_xattn_in['Wk'], 'L0_xattn_bk': _L0_xattn_in['bk'], 'L0_xattn_Wv': _L0_xattn_in['Wv'], 'L0_xattn_bv': _L0_xattn_in['bv'], 'L0_xattn_Wo': _L0_xattn_in['Wo'], 'L0_xattn_bo': _L0_xattn_in['bo'], 'L0_ffn_router_w': _L0_ffn_in['router_w'], 'L0_ffn_w_fc': _L0_ffn_in['w_fc'], 'L0_ffn_b_fc': _L0_ffn_in['b_fc'], 'L0_ffn_w_proj': _L0_ffn_in['w_proj'], 'L0_ffn_b_proj': _L0_ffn_in['b_proj'], 'L1_xattn_Wq': _L1_xattn_in['Wq'], 'L1_xattn_bq': _L1_xattn_in['bq'], 'L1_xattn_Wk': _L1_xattn_in['Wk'], 'L1_xattn_bk': _L1_xattn_in['bk'], 'L1_xattn_Wv': _L1_xattn_in['Wv'], 'L1_xattn_bv': _L1_xattn_in['bv'], 'L1_ffn_W1': _L1_ffn_in['W1'], 'L1_ffn_b1': _L1_ffn_in['b1'], 'L1_ffn_W2': _L1_ffn_in['W2'], 'L1_ffn_b2': _L1_ffn_in['b2']}

def reference(x, ctx_1024, mask_1x1xSxS2_ff0, mask_BxS2_bk1, g_xattn, g_ffn, L0_xattn_Wq, L0_xattn_bq, L0_xattn_Wk, L0_xattn_bk, L0_xattn_Wv, L0_xattn_bv, L0_xattn_Wo, L0_xattn_bo, L0_ffn_router_w, L0_ffn_w_fc, L0_ffn_b_fc, L0_ffn_w_proj, L0_ffn_b_proj, L1_xattn_Wq, L1_xattn_bq, L1_xattn_Wk, L1_xattn_bk, L1_xattn_Wv, L1_xattn_bv, L1_ffn_W1, L1_ffn_b1, L1_ffn_W2, L1_ffn_b2):
    import jax
    import jax.numpy as jnp

    def _L0_xattn_ref(q_in, k_in, v_in, mask, Wq, bq, Wk, bk, Wv, bv, Wo, bo):
        import jax, jax.numpy as jnp
        import numpy as np
        D_MODEL = 128
        NUM_HEADS = 16
        D_QKV = D_MODEL // NUM_HEADS
        B, S = (4, 256)
        FMAX = jnp.finfo(jnp.float32).max

        def _split_heads(x):
            b, s, _ = x.shape
            return x.reshape(b, s, NUM_HEADS, D_QKV).transpose(0, 2, 1, 3)
        q = _split_heads(q_in @ Wq + bq)
        k = _split_heads(k_in @ Wk + bk)
        v = _split_heads(v_in @ Wv + bv)
        logits = jnp.einsum('bhqd,bhkd->bhqk', q, k) / jnp.sqrt(jnp.asarray(D_QKV, jnp.float32))
        logits = logits - mask * FMAX
        w = jax.nn.softmax(logits, axis=-1)
        o = jnp.einsum('bhqk,bhkd->bhqd', w, v)
        o = o.transpose(0, 2, 1, 3).reshape(q_in.shape[0], q_in.shape[1], D_MODEL)
        return o @ Wo + bo

    def _L0_ffn_ref(x, router_w, w_fc, b_fc, w_proj, b_proj):
        import math
        import jax, jax.numpy as jnp
        import numpy as np
        TOP_K = 2
        _GELU_C = math.sqrt(2.0 / math.pi)

        def gelu_new(x):
            return 0.5 * x * (1.0 + jnp.tanh(_GELU_C * (x + 0.044715 * x * x * x)))
        B, T, C = x.shape
        E = router_w.shape[0]
        N = B * T
        xf = x.reshape(N, C)
        logits = xf @ router_w.T
        probs = jax.nn.softmax(logits, axis=-1)
        topk_probs, topk_idx = jax.lax.top_k(probs, TOP_K)
        topk_probs = topk_probs / jnp.sum(topk_probs, axis=-1, keepdims=True)
        combine = jnp.zeros((N, E), dtype=x.dtype).at[jnp.arange(N)[:, None], topk_idx].add(topk_probs)
        h = gelu_new(jnp.einsum('nc,ech->neh', xf, w_fc) + b_fc)
        out = jnp.einsum('neh,ehc->nec', h, w_proj) + b_proj
        y = jnp.einsum('nec,ne->nc', out, combine)
        return y.reshape(B, T, C)

    def _L1_xattn_ref(q, k, v, mask, Wq, bq, Wk, bk, Wv, bv):
        import jax, jax.numpy as jnp
        import numpy as np
        B, SQ, SK, DQ, DKV, DH, DV = (8, 256, 256, 128, 128, 128, 128)
        Qp = q @ Wq + bq
        Kp = k @ Wk + bk
        Vp = jnp.tanh(v @ Wv + bv)
        qk = jnp.einsum('bqd,bkd->bqk', Qp, Kp)
        qk = qk + mask[:, None, :].astype(qk.dtype)
        attn = jax.nn.softmax(qk, axis=-1)
        out = jnp.einsum('bqk,bkd->bqd', attn, Vp)
        return out

    def _L1_ffn_ref(x, W1, b1, W2, b2):
        import jax, jax.numpy as jnp
        import numpy as np
        QMIN, QMAX = (-128.0, 127.0)

        def _affine_quantize(x):
            amin, amax = (jnp.min(x), jnp.max(x))
            scale = jnp.maximum((amax - amin) / 255.0, 1e-08)
            zp = jnp.clip(jnp.round(-amin / scale) + QMIN, QMIN, QMAX)
            q = jnp.clip(jnp.round(x / scale) + zp, QMIN, QMAX)
            return (q, scale, zp)

        def _sym_quantize(w):
            scale = jnp.maximum(jnp.max(jnp.abs(w)) / 127.0, 1e-08)
            q = jnp.clip(jnp.round(w / scale), -127.0, 127.0)
            return (q, scale)

        def _qlinear(x, W, b):
            xq, sx, zx = _affine_quantize(x)
            wq, sw = _sym_quantize(W)
            acc = jnp.einsum('bsh,oh->bso', xq - zx, wq)
            return acc * (sx * sw) + b
        h = _qlinear(x, W1, b1)
        h = jax.nn.gelu(h, approximate=False)
        out = _qlinear(h, W2, b2)
        return out
    x = x + jnp.tanh(g_xattn[0]) * _L0_xattn_ref(_layernorm(x, axis=-1), ctx_1024, ctx_1024, mask_1x1xSxS2_ff0, L0_xattn_Wq, L0_xattn_bq, L0_xattn_Wk, L0_xattn_bk, L0_xattn_Wv, L0_xattn_bv, L0_xattn_Wo, L0_xattn_bo)
    x = x + jnp.tanh(g_ffn[0]) * _L0_ffn_ref(_layernorm(x, axis=-1), L0_ffn_router_w, L0_ffn_w_fc, L0_ffn_b_fc, L0_ffn_w_proj, L0_ffn_b_proj)
    x = x + jnp.tanh(g_xattn[1]) * _L1_xattn_ref(_layernorm(x, axis=-1), ctx_1024, ctx_1024, mask_BxS2_bk1, L1_xattn_Wq, L1_xattn_bq, L1_xattn_Wk, L1_xattn_bk, L1_xattn_Wv, L1_xattn_bv)
    x = x + jnp.tanh(g_ffn[1]) * _L1_ffn_ref(_layernorm(x, axis=-1), L1_ffn_W1, L1_ffn_b1, L1_ffn_W2, L1_ffn_b2)
    return x

_drawn_inputs = setup_inputs


def setup_inputs(seed=0):
    import zlib

    import numpy as np

    out = dict(_drawn_inputs(seed))
    spreads = {'g_ffn': (-1.0, 0.563),
     'L0_xattn_bq': (0.0, 0.1),
     'L0_xattn_bk': (0.0, 0.1),
     'L0_xattn_bv': (0.0, 0.1),
     'L0_xattn_bo': (0.0, 0.1),
     'L1_xattn_bq': (0.0, 0.1),
     'L1_xattn_bk': (0.0, 0.8),
     'L1_xattn_bv': (0.0, 0.1)}
    factors = {'L0_ffn_b_fc': 5.604, 'L0_ffn_b_proj': 4.204, 'L1_ffn_b1': 6.019, 'L1_ffn_b2': 5.134}
    for name, (base, spread) in spreads.items():
        noise = np.random.default_rng([zlib.crc32(name.encode()), seed]).standard_normal(out[name].shape)
        drawn = base * np.exp(spread * noise) if base else spread * noise
        out[name] = jnp.asarray(drawn.astype(out[name].dtype))
    for name, factor in factors.items():
        out[name] = (out[name] * factor).astype(out[name].dtype)
    return out
```

```python
from contextlib import ExitStack

import concourse.bass as bass
from concourse import mybir

ALU = mybir.AluOpType
ACT = mybir.ActivationFunctionType
AX_X = mybir.AxisListType.X
F32 = mybir.dt.float32
F32R = mybir.dt.float32r
BF16 = mybir.dt.bfloat16
U8 = mybir.dt.uint8
U32 = mybir.dt.uint32

P = 128
BATCH, SEQ, DM = 128, 64, 128
NTOK = BATCH * SEQ
TILES = NTOK // P
QUAD = 4
SUPERS = TILES // QUAD
ST = QUAD * P
HEADS, DH = 16, 8
GROUPS = HEADS // 2
VW = 9
VB = 2 * GROUPS * VW
FMAX = 3.4028234663852886e38
LN_EPS = 1e-5
Q_SLOTS = (0, 0, 1, 1, 0, 2, 1, 2)
K_SLOTS = (0, 1, 0, 1, 2, 0, 2, 1)


def layer0_attention(nc, ctx, d, g, sb, sem):
    x_sb = g["x_sb"]
    ident, tg = g["ident"], g["tanh_gates"]

    wq = sb("a_wq", [P, DM], F32)
    wk = sb("a_wk", [P, DM], F32)
    wv = sb("a_wv", [P, DM], F32)
    wo = sb("a_wo", [P, DM], F32)
    bq = sb("a_bq", [P, 1], F32)
    bk = sb("a_bk", [P, 1], F32)
    bv = sb("a_bv", [P, DM], F32)
    bo = sb("a_bo", [P, DM], F32)
    mask = sb("a_mask", [P, SEQ], F32)
    ctx_in = sb("a_ctx_in", [P, 2, QUAD, DM], F32)
    stats, mean, rstd = g["stats"], g["mean"], g["rstd"]
    xn = sb("a_xn", [P, QUAD, DM], F32)
    xn_t = sb("a_xn_t", [P, ST], F32)
    ctx_t = sb("a_ctx_t", [P, 2, ST // SEQ, 2, SEQ], F32)
    qk = sb("a_qk", [P, 2, 2, ST], F32)
    parts = sb("a_parts", [P, 2, 2, 3, ST], BF16)
    stack = sb("a_stack", [P, 2, 2, GROUPS, ST], BF16)
    VALL = QUAD * 2 * VB
    vals = [sb(f"a_vals{u}", [P, VALL + SEQ], F32) for u in range(2)]
    probs = sb("a_probs", [P, 4, GROUPS, 2, SEQ], F32)
    top = sb("a_top", [P, 4, HEADS], F32)
    probs_t = sb("a_probs_t", [P, 2, GROUPS, P], F32)
    rsum = sb("a_rsum", [P, HEADS], F32)
    heads = sb("a_heads", [P, HEADS, DH], F32)
    heads_t = sb("a_heads_t", [P, P], F32)

    parked = nc.dram_tensor("a_parked", (2, 2, 3, P, ST), BF16, kind="Internal").ap()
    ps_s = [ctx.enter_context(nc.psum_tensor(f"a_ps_s{j}", [P, GROUPS, SEQ], F32)) for j in range(2)]
    ps_pt = [ctx.enter_context(nc.psum_tensor(f"a_ps_pt{j}", [P, 4, P], F32)) for j in range(2)]
    ps_1 = [ctx.enter_context(nc.psum_tensor(f"a_ps_1{j}", [P, ST], F32)) for j in range(2)]
    ps_o = ctx.enter_context(nc.psum_tensor("a_ps_o", [P, 2, 256], F32))
    ps_y = ctx.enter_context(nc.psum_tensor("a_ps_y", [P, 4, P], F32))

    w_in = sem("a_w_in")
    held = sem("a_held")
    consts = sem("a_consts")
    loaded = sem("a_loaded")
    xn_ready = sem("a_xn_ready")
    bo_added = sem("a_bo_added")
    xt_ps, ct_ps = sem("a_xt_ps"), sem("a_ct_ps")
    xt_sb, ct_sb = sem("a_xt_sb"), sem("a_ct_sb")
    q_ps, k_ps, qk_sb = sem("a_q_ps"), sem("a_k_ps"), sem("a_qk_sb")
    hi_cut, hi_off, mid_cut, split = (sem(f"a_{n}") for n in ("hi_cut", "hi_off", "mid_cut", "split"))
    parts_parked = sem("a_parts_parked")
    stacked = sem("a_stacked")
    v_ps, v_sb = sem("a_v_ps"), sem("a_v_sb")
    s_ps, s_sb = sem("a_s_ps"), sem("a_s_sb")
    top_ready, shifted, p_ready = sem("a_top_ready"), sem("a_shifted"), sem("a_p_ready")
    pt_ps, pt_sb = sem("a_pt_ps"), sem("a_pt_sb")
    o_ps, rsum_ready, o_sb = sem("a_o_ps"), sem("a_rsum_ready"), sem("a_o_sb")
    ot_ps, ot_sb = sem("a_ot_ps"), sem("a_ot_sb")
    y_ps, x_out, stats_out = sem("a_y_ps"), sem("a_x_out"), sem("a_stats_out")

    ctx_view = d["ctx_1024"].rearrange("(a b) s c -> (b s) a c", b=2)
    N_W = 12

    def sweep(eng, step):
        for s in range(-3, 1):
            step(s, s % 2)
        with eng.Fori(0, (SUPERS - 4) // 2) as i:
            step(i * 2 + 1, 1)
            step(i * 2 + 2, 0)
        for s in range(SUPERS - 3, SUPERS + 1):
            step(s, s % 2)

    def hold(eng):
        eng.sem_inc(held, 1)

    def known(n):
        return isinstance(n, int)

    def there(n, count):
        return not known(n) or 0 <= n < count

    def later(n, least):
        return not known(n) or n >= least

    block = ctx.enter_context(nc.Block())

    @block.sync
    def _(sp):
        for dst, src in ((wq, "L0_xattn_Wq"), (wk, "L0_xattn_Wk"), (wv, "L0_xattn_Wv"), (wo, "L0_xattn_Wo")):
            sp.dma_start(dst[:], d[src]).then_inc(w_in, 16)
        for dst, src in ((bq, "L0_xattn_bq"), (bk, "L0_xattn_bk")):
            sp.dma_start(dst[:], d[src].rearrange("(p a) -> p a", a=1)).then_inc(w_in, 16)
        for dst, src in ((bv, "L0_xattn_bv"), (bo, "L0_xattn_bo")):
            sp.dma_start(dst[:], d[src].partition_broadcast(P)).then_inc(w_in, 16)
        for b in range(2):
            sp.dma_start(mask[SEQ * b:SEQ * b + SEQ, :],
                         d["mask_1x1xSxS2_ff0"].rearrange("a b q k -> (a b q) k")).then_inc(w_in, 16)

        def step(s, u):
            nxt = s + 3
            if there(nxt, SUPERS):
                if later(nxt, 1):
                    sp.wait_ge(loaded, nxt * 16)
                    hold(sp)
                if later(nxt, 2):
                    sp.wait_ge(ct_ps, nxt - 1)
                    hold(sp)
                sp.dma_start(ctx_in[:, 1 - u], ctx_view[:, bass.ds(nxt * QUAD, QUAD), :]).then_inc(loaded, 16)
            nxt = s + 1
            if there(nxt, SUPERS):
                if later(nxt, 1):
                    sp.wait_ge(stacked, nxt * 512)
                    hold(sp)
                if later(nxt, 2):
                    sp.wait_ge(s_ps, (nxt - 1) * QUAD)
                    hold(sp)
                sp.wait_ge(parts_parked, nxt * 16 + 16)
                hold(sp)
                for x in range(2):
                    for slot, part in enumerate((Q_SLOTS, K_SLOTS)[x]):
                        rows = parked[1 - u, x, part].rearrange("(g j e) t -> j e g t", g=GROUPS, j=2)
                        for j in range(2):
                            sp.dma_start(stack[64 * j + DH * slot:64 * j + DH * slot + DH, 1 - u, x], rows[j])\
                              .then_inc(stacked, 16)
            nxt = s + 2
            if there(nxt, SUPERS):
                sp.wait_ge(split, nxt + 1)
                hold(sp)
                if later(nxt, 2):
                    sp.wait_ge(stacked, nxt * 512 - 512)
                    hold(sp)
                sp.dma_start(parked[u].rearrange("x r p t -> p x r t"), parts[:, u]).then_inc(parts_parked, 16)

        sweep(sp, step)

    @block.gpsimd
    def _(pool):
        for u in range(2):
            pool.memset(vals[u][:], 0.0).then_inc(consts, 1)
        pool.wait_ge(consts, 2)
        for u in range(2):
            for j in range(2):
                ones = vals[u][64 * j:64 * j + 64, 0:VALL].rearrange("p (n w) -> p n w", w=2 * VW)
                pool.memset(ones[:, :, VW * j + DH], 1.0).then_inc(consts, 1)
        pool.wait_ge(consts, 6)
        pool.wait_ge(w_in, 16 * 10)
        pool.tensor_scalar(mask[:], mask[:], FMAX, None, ALU.mult).then_inc(consts, 1)
        pool.tensor_scalar(bo[:], bo[:], tg[:, 0:1], None, ALU.mult).then_inc(consts, 1)
        pool.wait_ge(consts, 8)

        def step(s, u):
            if there(s + 1, SUPERS):
                n = s + 1
                pool.wait_ge(xn_ready, n * QUAD + QUAD)
                xs = x_sb[:, bass.ds(n * QUAD, QUAD), :]
                pool.tensor_tensor(xs, xs, bo[:].unsqueeze(1).broadcast_to([P, QUAD, DM]), ALU.add)\
                    .then_inc(bo_added, 1)
            n = s + 2
            for j in range(QUAD):
                t = s * QUAD + j
                if j == 2 and there(n, SUPERS):
                    pool.wait_ge(hi_cut, n * 2 + 2)
                    pool.tensor_tensor(qk[:, u], qk[:, u], parts[:, u, :, 0, :], ALU.subtract).then_inc(hi_off, 1)
                if j == 3 and there(n, SUPERS):
                    pool.wait_ge(mid_cut, n + 1)
                    pool.tensor_tensor(parts[:, u, :, 2, :], qk[:, u], parts[:, u, :, 1, :],
                                       ALU.subtract).then_inc(split, 1)
                if there(t, TILES):
                    pool.wait_ge(top_ready, t + 1)
                    p = probs[:, j].rearrange("p g j k -> p (g j) k")
                    pool.tensor_tensor(p, p, top[:, j].unsqueeze(2).broadcast_to([P, HEADS, SEQ]),
                                       ALU.subtract).then_inc(shifted, 1)

        sweep(pool, step)

    @block.scalar
    def _(act):
        act.wait_ge(w_in, 16 * 10)

        def step(s, u):
            n = s + 2
            for j in range(QUAD):
                t = s * QUAD + j
                if there(t - 2, TILES):
                    if later(t - 2, 2):
                        act.wait_ge(o_ps, t - 3)
                    for h in range(2):
                        act.wait_ge(pt_ps, t * 2 - 3 + h)
                        act.activation(probs_t[:, j % 2, 4 * h:4 * h + 4, :], ps_pt[h][:], ACT.Copy)\
                            .then_inc(pt_sb, 1)
                if there(n, SUPERS) and j == 3:
                    act.wait_ge(hi_off, n + 1)
                    act.activation(parts[:, u, :, 1, :], qk[:, u], ACT.Copy).then_inc(mid_cut, 1)
                if there(t - 1, TILES):
                    act.wait_ge(shifted, t)
                    act.activation(probs[:, (j + 3) % 4], probs[:, (j + 3) % 4], ACT.Exp).then_inc(p_ready, 1)
                if there(t - 3, TILES):
                    act.wait_ge(ot_ps, t - 2)
                    act.activation(heads_t[:], ps_y[:, 0, :], ACT.Copy).then_inc(ot_sb, 1)
                if there(n, SUPERS) and j == 0:
                    act.wait_ge(xt_ps, n + 1)
                    act.activation(xn_t[:], ps_1[0][:], ACT.Copy).then_inc(xt_sb, 1)
                    act.wait_ge(ct_ps, n + 1)
                    if later(n, 2):
                        act.wait_ge(v_ps, n * 2 - 2)
                    act.activation(ctx_t[:, u], ps_1[1][:].rearrange("p (b k) -> p b k", k=SEQ).unsqueeze(2)
                                   .broadcast_to([P, ST // SEQ, 2, SEQ]), ACT.Copy).then_inc(ct_sb, 1)
                if there(n, SUPERS) and j == 1:
                    if later(n, 2):
                        act.wait_ge(split, n - 1)
                        act.wait_ge(parts_parked, n * 16 - 16)
                    for x, ps, bias in ((0, q_ps, bq), (1, k_ps, bk)):
                        act.wait_ge(ps, n + 1)
                        act.activation(qk[:, u, x], ps_1[x][:], ACT.Identity, bias=bias[:, 0:1]).then_inc(qk_sb, 1)
                        act.activation(parts[:, u, x, 0], ps_1[x][:], ACT.Identity, bias=bias[:, 0:1])\
                            .then_inc(hi_cut, 1)

        sweep(act, step)

    @block.tensor
    def _(pe):
        pe.wait_ge(w_in, 16 * 10)

        def step(s, u):
            n, nv = s + 2, s + 1
            for j in range(QUAD):
                t = s * QUAD + j
                if there(t - 2, TILES):
                    pe.wait_ge(p_ready, t - 1)
                    for h in range(2):
                        if later(t - 2, 1):
                            pe.wait_ge(pt_sb, t * 2 - 5 + h)
                        for k in range(4):
                            mm = pe.transpose(ps_pt[h][:, k, :],
                                              probs[:, (j + 2) % 4, 4 * h + k].rearrange("p j k -> p (j k)"),
                                              ident[:])
                        mm.then_inc(pt_ps, 1)
                if there(t, TILES):
                    if j == 0:
                        pe.wait_ge(stacked, (s + 1) * 512)
                    if later(t, 1):
                        pe.wait_ge(s_sb, t * 2)
                    hold(pe)
                    for gr in range(GROUPS):
                        for h in range(2):
                            for b in range(2):
                                at = slice(P * j + SEQ * b, P * j + SEQ * b + SEQ)
                                rows = slice(64 * h, 64 * h + 64)
                                mm = pe.matmul(ps_s[h][SEQ * b:SEQ * b + SEQ, gr, :],
                                               stack[rows, u, 0, gr, at], stack[rows, u, 1, gr, at],
                                               start=True, stop=True)
                    mm.then_inc(s_ps, 1)
                if there(t - 3, TILES):
                    if later(t - 3, 1):
                        pe.wait_ge(x_out, t - 3)
                    pe.wait_ge(o_sb, t * 2 - 4)
                    pe.transpose(ps_y[:, 0, :], heads[:].rearrange("p h e -> p (h e)"), ident[:])\
                        .then_inc(ot_ps, 1)
                if there(n, SUPERS) and j == 0:
                    pe.wait_ge(xn_ready, n * QUAD + QUAD)
                    if later(n, 2):
                        pe.wait_ge(v_sb, n * 4 - 4)
                    elif n == 1:
                        pe.wait_ge(hi_cut, 2)
                    for k in range(QUAD):
                        mm = pe.transpose(ps_1[0][:, P * k:P * k + P], xn[:, k, :], ident[:])
                    mm.then_inc(xt_ps, 1)
                    pe.wait_ge(loaded, n * 16 + 16)
                    for k in range(QUAD):
                        mm = pe.transpose(ps_1[1][:, P * k:P * k + P], ctx_in[:, u, k, :], ident[:])
                    mm.then_inc(ct_ps, 1)
                if there(n, SUPERS) and j == 1:
                    pe.wait_ge(xt_sb, n + 1)
                    pe.matmul(ps_1[0][:], wq[:], xn_t[:], start=True, stop=True).then_inc(q_ps, 1)
                    pe.wait_ge(ct_sb, n + 1)
                    pe.matmul(ps_1[1][:], wk[:], ctx_t[:, u, :, 0, :], start=True, stop=True).then_inc(k_ps, 1)
                if there(nv, SUPERS) and j == 2:
                    for h in range(2):
                        if there(n, SUPERS):
                            pe.wait_ge(hi_cut, n * 2 + 1 + h)
                        else:
                            pe.wait_ge(v_sb, nv * 4)
                        for b in range(4):
                            mm = pe.matmul(ps_1[h][:, P * b:P * b + P],
                                           ctx_t[:, 1 - u, 4 * h + b].rearrange("p a k -> p (a k)"), wv[:],
                                           start=True, stop=True)
                        mm.then_inc(v_ps, 1)
                if there(t - 2, TILES):
                    sv = s if j >= 2 else s - 1
                    pe.wait_ge(v_sb, (sv + 1) * 4)
                    if later(t - 2, 1):
                        pe.wait_ge(o_sb, t * 2 - 4)
                    v0 = 2 * VB * ((j + 2) % 4)
                    vv = vals[u if j >= 2 else 1 - u]
                    for gr in range(GROUPS):
                        if gr % 4 == 0:
                            pe.wait_ge(pt_sb, t * 2 - 3 + gr // 4)
                        c = v0 + 2 * VW * gr
                        rhs = vv[:, c:c + 2 * VB].rearrange("p (b w) -> p b w", b=2)[:, :, 0:SEQ] if \
                            c + 2 * VB <= VALL + SEQ else None
                        if rhs is None:
                            rhs = vv[:, c - 2 * VB + VB + SEQ:c + VB + SEQ].rearrange(
                                "p (b w) -> p b w", b=2)[:, :, VB - SEQ:VB]
                        mm = pe.matmul(ps_o[:, :, 2 * VW * gr:2 * VW * gr + SEQ], probs_t[:, j % 2, gr, :],
                                       rhs, start=True, stop=True)
                    mm.then_inc(o_ps, 1)
                if there(t - 3, TILES):
                    pe.wait_ge(ot_sb, t - 2)
                    pe.matmul(ps_y[:, 1, :], heads_t[:], wo[:], start=True, stop=True).then_inc(y_ps, 1)

        sweep(pe, step)

    @block.vector
    def _(dve):
        dve.wait_ge(w_in, 16 * 10)
        dve.wait_ge(consts, 8)

        def step(s, u):
            for j in range(QUAD):
                t = s * QUAD + j
                if there(t - 3, TILES):
                    dve.wait_ge(o_ps, t - 2)
                    if later(t - 3, 1):
                        dve.wait_ge(ot_ps, t - 3)
                    for b in range(2):
                        o = ps_o[SEQ * b:SEQ * b + SEQ, b, 0:VB].rearrange("p (h w) -> p h w", w=VW)
                        dve.reciprocal(rsum[SEQ * b:SEQ * b + SEQ, :], o[:, :, DH]).then_inc(rsum_ready, 1)
                    for b in range(2):
                        rows = slice(SEQ * b, SEQ * b + SEQ)
                        o = ps_o[rows, b, 0:VB].rearrange("p (h w) -> p h w", w=VW)
                        dve.wait_ge(rsum_ready, t * 2 - 5 + b)
                        dve.tensor_tensor(heads[rows], o[:, :, 0:DH],
                                          rsum[rows, :].unsqueeze(2).broadcast_to([SEQ, HEADS, DH]),
                                          ALU.mult).then_inc(o_sb, 1)
                if there(t - 4, TILES):
                    dve.wait_ge(y_ps, t - 3)
                    if j == 0:
                        dve.wait_ge(bo_added, s)
                    xs = x_sb[:, bass.ds(t - 4, 1), :].rearrange("p a c -> p (a c)")
                    dve.scalar_tensor_tensor(out=xs, in0=ps_y[:, 1, :], scalar=tg[:, 0:1], in1=xs,
                                             op0=ALU.mult, op1=ALU.add).then_inc(x_out, 1)
                    if j % 2:
                        for k in range(2):
                            dve.wait_ge(x_out, t - 4 + k)
                            tile = t - 5 + k
                            xs = x_sb[:, bass.ds(tile, 1), :].rearrange("p a c -> p (a c)")
                            dve.bn_stats(stats[:, bass.ds(tile, 1), :].rearrange("p a c -> p (a c)"), xs)\
                                .then_inc(stats_out, 1)
                n = s + 3
                if there(n, SUPERS) and j == 1:
                    if later(n, 1):
                        dve.wait_ge(xt_ps, n)
                    for k in range(QUAD):
                        tile = n * QUAD + k
                        xs = x_sb[:, bass.ds(tile, 1), :].rearrange("p a c -> p (a c)")
                        dve.tensor_scalar(xn[:, k, :], xs, mean[:, bass.ds(tile, 1)], rstd[:, bass.ds(tile, 1)],
                                          ALU.subtract, ALU.mult).then_inc(xn_ready, 1)
                nv = s + 1
                if there(nv, SUPERS) and j == 3:
                    for h in range(2):
                        dve.wait_ge(v_ps, nv * 2 + h + 1)
                        if later(nv, 2):
                            dve.wait_ge(o_ps, (nv - 1) * QUAD)
                        for r in range(2):
                            rows = slice(64 * r, 64 * r + 64)
                            out = vals[1 - u][rows, 4 * VB * h:4 * VB * h + 4 * VB].rearrange(
                                "p (n g w) -> p n g w", n=4, g=GROUPS)[:, :, :, VW * r:VW * r + DH]
                            src = ps_1[h][rows, :].rearrange("p (n g w) -> p n g w", n=4, g=GROUPS)
                            bias = bv[rows, :].rearrange("p (g w) -> p g w", g=GROUPS)
                            dve.tensor_tensor(out, src[:, :, :, DH * r:DH * r + DH],
                                              bias[:, :, DH * r:DH * r + DH].unsqueeze(1)
                                              .broadcast_to([64, 4, GROUPS, DH]), ALU.add).then_inc(v_sb, 1)
                if there(t, TILES):
                    dve.wait_ge(s_ps, t + 1)
                    if later(t, 4):
                        dve.wait_ge(pt_ps, t * 2 - 6)
                    for h in range(2):
                        dve.scalar_tensor_tensor(
                            out=probs[:, j, :, h, :], in0=ps_s[h][:], scalar=DH ** -0.5,
                            in1=mask[:].unsqueeze(1).broadcast_to([P, GROUPS, SEQ]),
                            op0=ALU.mult, op1=ALU.subtract).then_inc(s_sb, 1)
                    dve.wait_ge(s_sb, t * 2 + 2)
                    dve.tensor_reduce(top[:, j], probs[:, j].rearrange("p g j k -> p (g j) k"),
                                      AX_X, ALU.max).then_inc(top_ready, 1)

        sweep(dve, step)


def sweep(eng, step):
    for s in range(-2, 2):
        step(s, s % 2)
    with eng.Fori(0, (SUPERS - 4) // 2) as i:
        step(i * 2 + 2, 0)
        step(i * 2 + 3, 1)
    for s in range(SUPERS - 2, SUPERS + 2):
        step(s, s % 2)


def there(n, count):
    return not isinstance(n, int) or 0 <= n < count


def later(n, least):
    return not isinstance(n, int) or n >= least


def row(x, tile):
    return x[:, bass.ds(tile, 1), :].rearrange("p a c -> p (a c)")


def layer1_attention(nc, ctx, d, g, sb, sem):
    x_sb, ident, tg = g["x_sb"], g["ident"], g["tanh_gates"]
    stats, mean, rstd = g["stats"], g["mean"], g["rstd"]

    wq, wk, wv = (sb(f"c_w{n}", [P, DM], F32) for n in "qkv")
    bq, bk = (sb(f"c_b{n}", [P, 1], F32) for n in "qk")
    bv = sb("c_bv", [P, DM], F32)
    mask_u8 = sb("c_mask_u8", [1, NTOK], U8)
    term_k = sb("c_term_k", [3, TILES, 2, SEQ], BF16)
    term_q = sb("c_term_q", [3, P], BF16)
    ctx_in = sb("c_ctx_in", [P, 2, QUAD, DM], F32)
    xn = sb("c_xn", [P, QUAD, DM], F32)
    xn_t = sb("c_xn_t", [P, ST], F32)
    ctx_t = sb("c_ctx_t", [P, ST], F32)
    qk = sb("c_qk", [P, 2, ST], F32)
    v_raw = sb("c_v_raw", [P, QUAD, DM], F32)
    vals = sb("c_vals", [P, 2, QUAD, DM], F32)
    ntop = sb("c_ntop", [P, 2, QUAD], F32)
    probs = sb("c_probs", [P, 2, QUAD, P], F32)
    rsum = sb("c_rsum", [P, 2, QUAD], F32)
    gain = sb("c_gain", [P, 2, QUAD], F32)
    probs_t = sb("c_probs_t", [P, QUAD, P], F32)

    def bank(name):
        return ctx.enter_context(nc.psum_tensor(name, [P, QUAD, P], F32))

    ps_a, ps_b, ps_v, ps_s, ps_pt, ps_o = (bank(f"c_ps_{n}") for n in ("a", "b", "v", "s", "pt", "o"))

    w_in, m_in, held, loaded, terms = (sem(f"c_{n}") for n in ("w_in", "m_in", "held", "loaded", "terms"))
    xn_ready, xt_ps, ct_ps, xt_sb, ct_sb = (sem(f"c_{n}") for n in ("xn_ready", "xt_ps", "ct_ps", "xt_sb", "ct_sb"))
    q_ps, k_ps, qk_sb = (sem(f"c_{n}") for n in ("q_ps", "k_ps", "qk_sb"))
    v_ps, v_raw_sb, v_sb = (sem(f"c_{n}") for n in ("v_ps", "v_raw_sb", "v_sb"))
    s_ps, top_step, top_ready, p_ready = (sem(f"c_{n}") for n in ("s_ps", "top_step", "top_ready", "p_ready"))
    pt_ps, pt_sb, o_ps, gain_step, x_out, stats_out = (
        sem(f"c_{n}") for n in ("pt_ps", "pt_sb", "o_ps", "gain_step", "x_out", "stats_out"))

    ctx_view = d["ctx_1024"].rearrange("(a b) s c -> (b s) a c", b=2)

    def hold(eng):
        eng.sem_inc(held, 1)

    block = ctx.enter_context(nc.Block())

    @block.sync
    def _(sp):
        for dst, src in ((wq, "Wq"), (wk, "Wk"), (wv, "Wv")):
            sp.dma_start(dst[:], d["L1_xattn_" + src]).then_inc(w_in, 16)
        for dst, src in ((bq, "bq"), (bk, "bk")):
            sp.dma_start(dst[:], d["L1_xattn_" + src].rearrange("(p a) -> p a", a=1)).then_inc(w_in, 16)
        sp.dma_start(bv[:], d["L1_xattn_bv"].partition_broadcast(P)).then_inc(w_in, 16)
        sp.dma_start(mask_u8[:], d["mask_BxS2_bk1"].rearrange("(a b) k -> a (b k)", a=1)).then_inc(m_in, 16)

        def step(s, u):
            nxt = s + 2
            if there(nxt, SUPERS):
                if later(nxt, 1):
                    sp.wait_ge(loaded, nxt * 16)
                    hold(sp)
                if later(nxt, 2):
                    sp.wait_ge(ct_ps, nxt - 1)
                    hold(sp)
                sp.dma_start(ctx_in[:, u], ctx_view[:, bass.ds(nxt * QUAD, QUAD), :]).then_inc(loaded, 16)

        sweep(sp, step)

    @block.gpsimd
    def _(pool):
        def select(x, pattern, base, fill, n):
            pool.wait_ge(terms, n)
            pool.affine_select(out=x, in_=x, compare_op=ALU.not_equal, fill=fill, base=base,
                               pattern=pattern, channel_multiplier=1).then_inc(terms, 1)

        pool.memset(term_k[:], 0.0).then_inc(terms, 1)
        pool.memset(term_q[:], 0.0).then_inc(terms, 1)
        select(term_k[:, :, 1, :], [[0, TILES], [0, SEQ]], -1, -1e30, 2)
        select(term_k[:, :, 0, :], [[0, TILES], [0, SEQ]], -2, -1e30, 3)
        select(term_q[:], [[0, P]], 0, 1.0, 4)
        select(term_q[:, 0:SEQ], [[0, SEQ]], -1, 1.0, 5)
        select(term_q[:, SEQ:P], [[0, SEQ]], -2, 1.0, 6)
        pool.wait_ge(terms, 7)
        pool.wait_ge(m_in, 16)
        pool.tensor_copy(term_k[0:1].rearrange("p t b k -> p (t b k)"), mask_u8[:]).then_inc(terms, 1)

    @block.scalar
    def _(act):
        act.wait_ge(w_in, 96)

        def step(s, u):
            n = s + 1
            if there(n, SUPERS):
                act.wait_ge(xt_ps, n + 1)
                act.activation(xn_t[:], ps_a[:].rearrange("p a b -> p (a b)"), ACT.Copy).then_inc(xt_sb, 1)
                act.wait_ge(ct_ps, n + 1)
                act.activation(ctx_t[:], ps_b[:].rearrange("p a b -> p (a b)"), ACT.Copy).then_inc(ct_sb, 1)
            if there(s - 1, SUPERS):
                act.wait_ge(pt_ps, s)
                act.activation(probs_t[:], ps_pt[:], ACT.Copy).then_inc(pt_sb, 1)
            if there(s, SUPERS):
                act.wait_ge(top_ready, s + 1)
                for k in range(QUAD):
                    act.activation(probs[:, u, k], ps_s[:, k], ACT.Exp, bias=ntop[:, u, k:k + 1],
                                   accum_out=rsum[:, u, k:k + 1]).then_inc(p_ready, 1)
            if there(n, SUPERS):
                for h, (ready, ps, bias) in enumerate(((q_ps, ps_a, bq), (k_ps, ps_b, bk))):
                    act.wait_ge(ready, n + 1)
                    act.activation(qk[:, h], ps[:].rearrange("p a b -> p (a b)"), ACT.Identity,
                                   bias=bias[:, 0:1]).then_inc(qk_sb, 1)
                act.wait_ge(v_raw_sb, n + 1)
                if later(n, 2):
                    act.wait_ge(o_ps, n - 1)
                act.activation(vals[:, 1 - u], v_raw[:], ACT.Tanh).then_inc(v_sb, 1)

        sweep(act, step)

    @block.tensor
    def _(pe):
        pe.wait_ge(w_in, 96)
        pe.wait_ge(terms, 8)

        def step(s, u):
            n = s + 1
            if there(s, SUPERS):
                pe.wait_ge(qk_sb, s * 2 + 2)
                if later(s, 1):
                    pe.wait_ge(p_ready, s * 4)
                for k in range(QUAD):
                    tok = slice(P * k, P * k + P)
                    pe.matmul(ps_s[:, k], qk[:, 0, tok], qk[:, 1, tok], start=True, stop=False)
                    mm = pe.matmul(ps_s[:, k], term_q[:],
                                   term_k[:, bass.ds(s * QUAD + k, 1)].rearrange("p a b k -> p (a b k)"),
                                   start=False, stop=True)
                mm.then_inc(s_ps, 1)
            if there(n, SUPERS):
                pe.wait_ge(xn_ready, n * QUAD + QUAD)
                if later(n, 1):
                    pe.wait_ge(qk_sb, n * 2)
                for k in range(QUAD):
                    mm = pe.transpose(ps_a[:, k], xn[:, k], ident[:])
                mm.then_inc(xt_ps, 1)
                pe.wait_ge(loaded, n * 16 + 16)
                for k in range(QUAD):
                    mm = pe.transpose(ps_b[:, k], ctx_in[:, 1 - u, k], ident[:])
                mm.then_inc(ct_ps, 1)
            if there(s - 1, SUPERS):
                pe.wait_ge(p_ready, s * 4)
                if later(s - 1, 1):
                    pe.wait_ge(pt_sb, s - 1)
                for k in range(QUAD):
                    mm = pe.transpose(ps_pt[:, k], probs[:, 1 - u, k], ident[:])
                mm.then_inc(pt_ps, 1)
            if there(n, SUPERS):
                pe.wait_ge(xt_sb, n + 1)
                pe.matmul(ps_a[:].rearrange("p a b -> p (a b)"), wq[:], xn_t[:], start=True, stop=True)\
                    .then_inc(q_ps, 1)
                pe.wait_ge(ct_sb, n + 1)
                pe.matmul(ps_b[:].rearrange("p a b -> p (a b)"), wk[:], ctx_t[:], start=True, stop=True)\
                    .then_inc(k_ps, 1)
                if later(n, 1):
                    pe.wait_ge(v_raw_sb, n)
                for k in range(QUAD):
                    mm = pe.matmul(ps_v[:, k], ctx_t[:, P * k:P * k + P], wv[:], start=True, stop=True)
                mm.then_inc(v_ps, 1)
            if there(s - 1, SUPERS):
                pe.wait_ge(pt_sb, s)
                pe.wait_ge(v_sb, s)
                if later(s - 1, 1):
                    pe.wait_ge(x_out, s * 4 - 4)
                for k in range(QUAD):
                    mm = pe.matmul(ps_o[:, k], probs_t[:, k], vals[:, 1 - u, k], start=True, stop=True)
                mm.then_inc(o_ps, 1)

        sweep(pe, step)

    @block.vector
    def _(dve):
        dve.wait_ge(w_in, 96)

        def step(s, u):
            if there(s, SUPERS):
                dve.wait_ge(s_ps, s + 1)
                dve.tensor_reduce(ntop[:, u], ps_s[:], AX_X, ALU.max).then_inc(top_step, 1)
                dve.wait_ge(top_step, s + 1)
                dve.tensor_scalar(ntop[:, u], ntop[:, u], -1.0, None, ALU.mult).then_inc(top_ready, 1)
            n2 = s + 2
            if there(n2, SUPERS):
                if later(n2, 1):
                    dve.wait_ge(xt_ps, n2)
                for k in range(QUAD):
                    tile = n2 * QUAD + k
                    dve.tensor_scalar(xn[:, k], row(x_sb, tile), mean[:, bass.ds(tile, 1)],
                                      rstd[:, bass.ds(tile, 1)], ALU.subtract, ALU.mult).then_inc(xn_ready, 1)
            n = s + 1
            if there(n, SUPERS):
                dve.wait_ge(v_ps, n + 1)
                if later(n, 1):
                    dve.wait_ge(v_sb, n)
                dve.tensor_tensor(v_raw[:], ps_v[:], bv[:].unsqueeze(1).broadcast_to([P, QUAD, DM]), ALU.add)\
                    .then_inc(v_raw_sb, 1)
            if there(s - 1, SUPERS):
                dve.wait_ge(p_ready, s * 4)
                dve.reciprocal(gain[:, 1 - u], rsum[:, 1 - u]).then_inc(gain_step, 1)
                dve.wait_ge(gain_step, s * 2 - 1)
                dve.tensor_scalar(gain[:, 1 - u], gain[:, 1 - u], tg[:, 2:3], None, ALU.mult).then_inc(gain_step, 1)
                dve.wait_ge(gain_step, s * 2)
                dve.wait_ge(o_ps, s)
                for k in range(QUAD):
                    xs = row(x_sb, (s - 1) * QUAD + k)
                    dve.scalar_tensor_tensor(out=xs, in0=ps_o[:, k], scalar=gain[:, 1 - u, k:k + 1], in1=xs,
                                             op0=ALU.mult, op1=ALU.add).then_inc(x_out, 1)
                for k in range(QUAD):
                    dve.wait_ge(x_out, s * 4 - 3 + k)
                    tile = (s - 1) * QUAD + k
                    dve.bn_stats(row(stats, tile), row(x_sb, tile)).then_inc(stats_out, 1)

        sweep(dve, step)


MAGIC = 12582912.0
QMIN, QMAX = -128.0, 127.0
HID = 512
CHUNKS = HID // P


def layer1_ffn(nc, ctx, d, g, sb, sem):
    x_sb, ident, tg = g["x_sb"], g["ident"], g["tanh_gates"]
    mean, rstd = g["mean"], g["rstd"]

    hid = sb("d_hid", [P, SUPERS, CHUNKS, ST], F32)
    w1 = sb("d_w1", [P, CHUNKS, P], F32)
    w2 = sb("d_w2", [P, CHUNKS, P], F32)
    wq = [sb(f"d_wq{n}", [P, CHUNKS, P], BF16) for n in range(2)]
    wqt = [sb(f"d_wqt{n}", [P, CHUNKS, P], BF16) for n in range(2)]
    b1 = sb("d_b1", [P, CHUNKS], F32)
    b2 = sb("d_b2", [P, DM], F32)
    ident16 = sb("d_ident16", [P, P], BF16)
    ext = sb("d_ext", [P, 2, TILES], F32)
    peak = sb("d_peak", [P, 4], F32)
    peaks = sb("d_peaks", [P, 4], F32)
    hpeak = sb("d_hpeak", [P, 2, SUPERS], F32)
    hp = sb("d_hp", [P, 2], F32)
    hps = sb("d_hps", [P, 2], F32)
    wscale = sb("d_wscale", [P, 2], F32)
    winv = sb("d_winv", [P, 2], F32)
    qs = [sb(f"d_qs{n}", [P, 8], F32) for n in range(2)]
    outscale = sb("d_outscale", [P, 2], F32)
    xq32 = sb("d_xq32", [P, QUAD, DM], F32)
    xq = sb("d_xq", [P, QUAD, DM], BF16)
    xqt = sb("d_xqt", [P, 2, ST], BF16)
    hq = sb("d_hq", [P, 2, CHUNKS, ST], BF16)

    def qscale(dve, q, amax, namin, step, at):
        def then(ins, wait=True):
            nonlocal at
            at += 1
            ins.then_inc(step, 1)
            if wait:
                dve.wait_ge(step, at)

        then(dve.tensor_tensor(q[:, 0:1], amax, namin, ALU.add))
        then(dve.tensor_scalar(q[:, 0:1], q[:, 0:1], 1.0 / 255.0, 1e-8, ALU.mult, ALU.max))
        then(dve.reciprocal(q[:, 1:2], q[:, 0:1]))
        then(dve.tensor_scalar(q[:, 2:3], namin, q[:, 1:2], MAGIC, ALU.mult, ALU.add))
        then(dve.tensor_scalar(q[:, 3:4], q[:, 2:3], MAGIC, QMIN, ALU.subtract, ALU.add))
        then(dve.tensor_scalar(q[:, 4:5], q[:, 3:4], QMIN, QMAX, ALU.max, ALU.min))
        then(dve.tensor_scalar(q[:, 5:6], q[:, 4:5], -1.0, QMIN + MAGIC, ALU.mult, ALU.add))
        then(dve.tensor_scalar(q[:, 6:7], q[:, 4:5], -1.0, QMAX + MAGIC, ALU.mult, ALU.add))
        return at

    def bank(name, dt=F32):
        return ctx.enter_context(nc.psum_tensor(name, [P, CHUNKS, P], dt))

    ps_t = bank("d_ps_t", BF16)
    ps_h = [bank(f"d_ps_h{n}") for n in range(CHUNKS)]
    ps_y = [bank(f"d_ps_y{n}") for n in range(2)]

    names = ("w_in", "held", "id16", "ext", "peak_ready", "peaks_ready", "step", "x_scale", "wq_sb", "wq32", "wt_ps", "wt_sb",
             "n_ready", "q_step", "xq_ready", "xt_ps", "xt_sb", "h_ps", "h_sb", "hpeak_ready", "hp_ready", "hps_ready",
             "h_scale", "b2_added", "t_ready", "c_ready", "hq_ready", "y_ps", "x_out", "stored")
    (w_in, held, id16, ext_ready, peak_ready, peaks_ready, qstep, x_scale, wq_sb, wq32, wt_ps, wt_sb,
     n_ready, q_step, xq_ready, xt_ps, xt_sb, h_ps, h_sb, hpeak_ready, hp_ready, hps_ready,
     h_scale, b2_added, t_ready, c_ready, hq_ready, y_ps, x_out, stored) = (sem("d_" + n) for n in names)

    def hold(eng):
        eng.sem_inc(held, 1)

    out_view = d["out"].rearrange("(a b) s c -> (b s) a c", b=2)
    flat_x = x_sb[:].rearrange("p t c -> p (t c)")

    def tokens(s):
        return flat_x[:, bass.ds(s * ST, ST)]

    block = ctx.enter_context(nc.Block())

    @block.sync
    def _(sp):
        sp.dma_start(w1[:], d["L1_ffn_W1"].rearrange("(a p) c -> p a c", p=P)).then_inc(w_in, 16)
        sp.dma_start(w2[:], d["L1_ffn_W2"].rearrange("c (a p) -> c a p", p=P)).then_inc(w_in, 16)
        sp.dma_start(b1[:], d["L1_ffn_b1"].rearrange("(a p) -> p a", p=P), allow_slow_non_contiguous=True).then_inc(w_in, 16)
        sp.dma_start(b2[:], d["L1_ffn_b2"].partition_broadcast(P)).then_inc(w_in, 16)
        with sp.Fori(0, SUPERS) as s:
            sp.wait_ge(x_out, s * 4 + 4)
            hold(sp)
            sp.dma_start(out_view[:, bass.ds(s * QUAD, QUAD), :], x_sb[:, bass.ds(s * QUAD, QUAD), :])\
                .then_inc(stored, 16)
        sp.wait_ge(stored, 16 * SUPERS)

    @block.gpsimd
    def _(pool):
        pool.tensor_copy(ident16[:], ident[:]).then_inc(id16, 1)
        pool.wait_ge(w_in, 64)
        pool.tensor_scalar(b2[:], b2[:], tg[:, 3:4], None, ALU.mult).then_inc(id16, 1)
        pool.wait_ge(peak_ready, 4)
        pool.partition_all_reduce(peaks[:], peak[:], P, bass.bass_isa.ReduceOp.max).then_inc(peaks_ready, 1)
        pool.wait_ge(id16, 2)
        with pool.Fori(0, SUPERS) as s:
            pool.wait_ge(n_ready, s * 4 + 4)
            xs = x_sb[:, bass.ds(s * QUAD, QUAD), :]
            pool.tensor_tensor(xs, xs, b2[:].unsqueeze(1).broadcast_to([P, QUAD, DM]), ALU.add).then_inc(b2_added, 1)
        pool.wait_ge(hp_ready, 2)
        pool.partition_all_reduce(hps[:], hp[:], P, bass.bass_isa.ReduceOp.max).then_inc(hps_ready, 1)

    @block.scalar
    def _(act):
        for n in range(2):
            act.wait_ge(wt_ps, n + 1)
            act.activation(wqt[n][:], ps_t[:], ACT.Copy).then_inc(wt_sb, 1)
        act.wait_ge(x_scale, 1)

        def step(s, u):
            if there(s + 1, SUPERS):
                n = s + 1
                act.wait_ge(xt_ps, n + 1)
                if later(n, 2):
                    act.wait_ge(h_ps, n * 4 - 4)
                act.activation(xqt[:, 1 - u], ps_t[:].rearrange("p a b -> p (a b)"), ACT.Copy).then_inc(xt_sb, 1)
            if there(s, SUPERS):
                for c in range(CHUNKS):
                    act.wait_ge(h_ps, s * 4 + c + 1)
                    act.activation(hid[:, bass.ds(s, 1), c, :].rearrange("p a t -> p (a t)"),
                                   ps_h[c][:].rearrange("p a b -> p (a b)"), ACT.Gelu,
                                   bias=b1[:, c:c + 1], scale=outscale[:, 0:1]).then_inc(h_sb, 1)

        sweep(act, step)
        act.wait_ge(h_scale, 1)
        with act.Fori(0, SUPERS) as s:
            h = hid[:, bass.ds(s, 1)].rearrange("p a c t -> p (a c t)")
            act.activation(h, h, ACT.Identity, scale=qs[1][:, 1:2], bias=qs[1][:, 7:8]).then_inc(t_ready, 1)

    @block.tensor
    def _(pe):
        pe.wait_ge(id16, 1)
        for n in range(2):
            pe.wait_ge(wq_sb, n + 1)
            if n:
                pe.wait_ge(wt_sb, n)
            for c in range(CHUNKS):
                mm = pe.transpose(ps_t[:, c], wq[n][:, c], ident16[:])
            mm.then_inc(wt_ps, 1)

        pe.wait_ge(wt_sb, 2)

        def step(s, u):
            if there(s + 1, SUPERS):
                n = s + 1
                pe.wait_ge(xq_ready, n + 1)
                if later(n, 1):
                    pe.wait_ge(xt_sb, n)
                for k in range(QUAD):
                    mm = pe.transpose(ps_t[:, k], xq[:, k], ident16[:])
                mm.then_inc(xt_ps, 1)
            if there(s, SUPERS):
                pe.wait_ge(xt_sb, s + 1)
                for c in range(CHUNKS):
                    if later(s, 1):
                        pe.wait_ge(h_sb, s * 4 - 3 + c)
                    pe.matmul(ps_h[c][:].rearrange("p a b -> p (a b)"), wqt[0][:, c], xqt[:, u],
                              start=True, stop=True).then_inc(h_ps, 1)

        sweep(pe, step)

        def second(s, u):
            pe.wait_ge(hq_ready, s + 1)
            if later(s, 2):
                pe.wait_ge(x_out, s * 4 - 4)
            for k in range(QUAD):
                for c in range(CHUNKS):
                    mm = pe.matmul(ps_y[u][:, k], hq[:, u, c, P * k:P * k + P], wqt[1][:, c],
                                   start=(c == 0), stop=(c == CHUNKS - 1))
            mm.then_inc(y_ps, 1)

        for s in range(2):
            second(s, s)
        with pe.Fori(0, SUPERS // 2 - 1) as i:
            for u in range(2):
                second(i * 2 + 2 + u, u)

    @block.vector
    def _(dve):
        dve.tensor_reduce(ext[:, 0], x_sb[:], AX_X, ALU.max).then_inc(ext_ready, 1)
        dve.tensor_reduce(ext[:, 1], x_sb[:], AX_X, ALU.min).then_inc(ext_ready, 1)
        dve.wait_ge(ext_ready, 2)
        for e in range(2):
            dve.tensor_tensor(ext[:, e], ext[:, e], mean[:], ALU.subtract).then_inc(ext_ready, 1)
        dve.wait_ge(ext_ready, 4)
        for e in range(2):
            dve.tensor_tensor(ext[:, e], ext[:, e], rstd[:], ALU.mult).then_inc(ext_ready, 1)
        dve.wait_ge(ext_ready, 6)
        dve.tensor_scalar(ext[:, 1], ext[:, 1], -1.0, None, ALU.mult).then_inc(ext_ready, 1)
        dve.wait_ge(ext_ready, 7)
        for e in range(2):
            dve.tensor_reduce(peak[:, e:e + 1], ext[:, e], AX_X, ALU.max).then_inc(peak_ready, 1)
        dve.wait_ge(w_in, 64)
        for e, w in enumerate((w1, w2)):
            dve.tensor_reduce(peak[:, 2 + e:3 + e], w[:].rearrange("p a b -> p (a b)"), AX_X, ALU.max,
                              apply_absolute_value=True).then_inc(peak_ready, 1)
        dve.wait_ge(peaks_ready, 1)
        at = qscale(dve, qs[0], peaks[:, 0:1], peaks[:, 1:2], qstep, 0)
        dve.tensor_scalar(wscale[:], peaks[:, 2:4], 1.0 / 127.0, 1e-8, ALU.mult, ALU.max).then_inc(qstep, 1)
        dve.wait_ge(qstep, at + 1)
        dve.reciprocal(winv[:], wscale[:]).then_inc(qstep, 1)
        dve.tensor_scalar(outscale[:, 0:1], wscale[:, 0:1], qs[0][:, 0:1], None, ALU.mult).then_inc(x_scale, 1)
        dve.wait_ge(qstep, at + 2)
        at += 2
        for n, w in enumerate((w1, w2)):
            dve.tensor_scalar(w[:], w[:], winv[:, n:n + 1], MAGIC, ALU.mult, ALU.add).then_inc(wq32, 1)
            dve.wait_ge(wq32, 3 * n + 1)
            dve.tensor_scalar(w[:], w[:], MAGIC, -127.0, ALU.subtract, ALU.max).then_inc(wq32, 1)
            dve.wait_ge(wq32, 3 * n + 2)
            dve.tensor_scalar(wq[n][:], w[:], 127.0, None, ALU.min).then_inc(wq_sb, 1)
            dve.sem_inc(wq32, 1)

        def step(s, u):
            n = s + 1
            if there(n, SUPERS):
                if later(n, 1):
                    dve.wait_ge(xq_ready, n)
                for k in range(QUAD):
                    tile = n * QUAD + k
                    dve.tensor_scalar(xq32[:, k], row(x_sb, tile), mean[:, bass.ds(tile, 1)],
                                      rstd[:, bass.ds(tile, 1)], ALU.subtract, ALU.mult).then_inc(n_ready, 1)
                dve.wait_ge(n_ready, n * 4 + 4)
                dve.tensor_scalar(xq32[:], xq32[:], qs[0][:, 1:2], MAGIC, ALU.mult, ALU.add).then_inc(q_step, 1)
                dve.wait_ge(q_step, n * 2 + 1)
                dve.tensor_scalar(xq32[:], xq32[:], qs[0][:, 5:6], qs[0][:, 6:7], ALU.max, ALU.min)\
                    .then_inc(q_step, 1)
                dve.wait_ge(q_step, n * 2 + 2)
                if later(n, 1):
                    dve.wait_ge(xt_ps, n)
                dve.tensor_scalar(xq[:], xq32[:], MAGIC, None, ALU.subtract).then_inc(xq_ready, 1)
            p = s - 1
            if there(p, SUPERS):
                dve.wait_ge(h_sb, p * 4 + 4)
                h = hid[:, bass.ds(p, 1)].rearrange("p a c t -> p (a c t)")
                for e, op in enumerate((ALU.max, ALU.min)):
                    dve.tensor_reduce(hpeak[:, e, bass.ds(p, 1)], h, AX_X, op).then_inc(hpeak_ready, 1)

        sweep(dve, step)
        dve.wait_ge(hpeak_ready, 2 * SUPERS)
        dve.tensor_reduce(hp[:, 0:1], hpeak[:, 0], AX_X, ALU.max).then_inc(hp_ready, 1)
        dve.tensor_reduce(hp[:, 1:2], hpeak[:, 1], AX_X, ALU.min).then_inc(hpeak_ready, 1)
        dve.wait_ge(hpeak_ready, 2 * SUPERS + 1)
        dve.tensor_scalar(hp[:, 1:2], hp[:, 1:2], -1.0, None, ALU.mult).then_inc(hp_ready, 1)
        dve.wait_ge(hps_ready, 1)
        at = qscale(dve, qs[1], hps[:, 0:1], hps[:, 1:2], qstep, at)
        dve.memset(qs[1][:, 7:8], MAGIC).then_inc(h_scale, 1)
        dve.tensor_scalar(outscale[:, 1:2], wscale[:, 1:2], qs[1][:, 0:1], tg[:, 3:4], ALU.mult, ALU.mult)\
            .then_inc(qstep, 1)
        dve.wait_ge(qstep, at + 1)

        def second(s, u):
            dve.wait_ge(t_ready, s + 1)
            h = hid[:, bass.ds(s, 1)].rearrange("p a c t -> p (a c t)")
            dve.tensor_scalar(h, h, qs[1][:, 5:6], qs[1][:, 6:7], ALU.max, ALU.min).then_inc(c_ready, 1)
            dve.wait_ge(c_ready, s + 1)
            if later(s, 2):
                dve.wait_ge(y_ps, s - 1)
            dve.tensor_scalar(hq[:, u].rearrange("p c t -> p (c t)"), h, MAGIC, None, ALU.subtract)\
                .then_inc(hq_ready, 1)

        def finish(s, u):
            dve.wait_ge(y_ps, s + 1)
            dve.wait_ge(b2_added, s + 1)
            for k in range(QUAD):
                xs = row(x_sb, s * QUAD + k)
                dve.scalar_tensor_tensor(out=xs, in0=ps_y[u][:, k], scalar=outscale[:, 1:2], in1=xs,
                                         op0=ALU.mult, op1=ALU.add).then_inc(x_out, 1)

        second(0, 0)
        second(1, 1)
        finish(0, 0)
        with dve.Fori(0, SUPERS // 2 - 1) as i:
            second(i * 2 + 2, 0)
            finish(i * 2 + 1, 1)
            second(i * 2 + 3, 1)
            finish(i * 2 + 2, 0)
        finish(SUPERS - 1, 1)


EXPERTS = 8
RT = ST
REGION = NTOK + RT
ETILES = (2 * NTOK + EXPERTS * (RT - 1)) // RT
RW = DM + 4
SPARE = ETILES - 2 * NTOK // RT
PADDED = EXPERTS + SPARE


def mixture(nc, ctx, d, g, sb, sem):
    tokens_to = nc.dram_tensor("m_rows", (EXPERTS * REGION + SPARE * RT, RW), F32, kind="Internal").ap()
    results = nc.dram_tensor("m_results", (2 * NTOK + PADDED * RT, DM), F32, kind="Internal").ap()
    wall = sb("m_wall", [P, EXPERTS, 4, HID], F32R)
    ball = sb("m_ball", [P, EXPERTS, CHUNKS + 1], F32)
    tables = sb("m_tables", [1, 2, ETILES], U32)
    ends = sb("m_ends", [1, EXPERTS], U32)
    with ExitStack() as inner:
        route(nc, inner, d, g, sem, tokens_to, wall, ball, tables, ends)
    with ExitStack() as inner:
        experts(nc, inner, d, g, sem, tokens_to, results, wall, ball, tables)
    with ExitStack() as inner:
        gather(nc, inner, d, g, sem, results)


def route(nc, ctx, d, g, sem, tokens_to, wall, ball, tables, ends):
    x_sb, ident, tg, mean, rstd = g["x_sb"], g["ident"], g["tanh_gates"], g["mean"], g["rstd"]

    def sb(name, shape, dt):
        return ctx.enter_context(nc.sbuf_tensor(name, shape, dt))

    rows = sb("r_rows", [P, TILES, 2, RW], F32)
    xn = sb("r_xn", [P, 2, QUAD, DM], F32)
    xn_t = sb("r_xn_t", [P, QUAD, P], F32)
    rw = sb("r_rw", [EXPERTS, DM], F32)
    rw_t = sb("r_rw_t", [P, EXPERTS], F32)
    raw = sb("r_raw", [P, 2, 2, HID], F32)
    bias_rows = sb("r_bias_rows", [EXPERTS * (CHUNKS + 1), P], F32)
    TE = [P, TILES, EXPERTS]
    logits, work, first, second = (sb(f"r_{n}", TE, F32) for n in ("logits", "work", "first", "second"))
    chosen = sb("r_chosen", TE, BF16)
    order = sb("r_order", TE, F32)
    top = sb("r_top", [P, 2, TILES], F32)
    pick = sb("r_pick", [P, TILES], F32)
    gate = sb("r_gate", [P, 2, TILES], F32)
    place = sb("r_place", [P, 2, TILES], F32)
    place_u = sb("r_place_u", [P, 2, TILES], U32)
    before = sb("r_before", [P, P], BF16)
    ones = sb("r_ones", [P, P], BF16)
    total = sb("r_total", [P, EXPERTS, TILES], F32)
    upto = sb("r_upto", [P, EXPERTS, TILES], F32)
    resets = sb("r_resets", [P, EXPERTS, TILES], F32)
    base = sb("r_base", [P, EXPERTS], F32)
    count = sb("r_count", [P, EXPERTS], F32)
    ntile = sb("r_ntile", [P, EXPERTS], F32)
    tile_end = sb("r_tile_end", [P, EXPERTS], F32)
    eones = sb("r_eones", [P, EXPERTS], F32)
    tnum = sb("r_tnum", [P, ETILES], F32)
    trow = sb("r_trow", [P, ETILES], F32)
    texp = sb("r_texp", [P, ETILES], F32)
    past = sb("r_past", [P, ETILES], F32)
    skip = sb("r_skip", [P, EXPERTS], F32)
    pad = sb("r_pad", [P, RT // P, RW], F32)

    def bank(name, shape, dt=F32):
        return ctx.enter_context(nc.psum_tensor(name, shape, dt))

    ps_t = bank("r_ps_t", [P, QUAD, P])
    ps_l = [bank(f"r_ps_l{n}", [P, QUAD, P]) for n in range(2)]
    ps_c = bank("r_ps_c", [P, TILES, EXPERTS])
    ps_n = bank("r_ps_n", [P, TILES, EXPERTS])
    ps_w = bank("r_ps_w", [P, 4, P])

    names = ("w_in", "b_in", "xn_ready", "xt_ps", "xt_sb", "copied", "l_ps", "l_sb", "rwt_ps", "rwt_sb", "bias_ps",
             "bias_sb", "raw_in", "hi", "lo", "consts", "step", "diff", "ratio", "chosen", "cn_ps", "tables_ready",
             "ids", "place_ready", "sent", "padded", "held", "pad_ready")
    (w_in, b_in, xn_ready, xt_ps, xt_sb, copied, l_ps, l_sb, rwt_ps, rwt_sb, bias_ps,
     bias_sb, raw_in, hi_done, lo_done, consts, step_done, diff, ratio, chosen_ready, cn_ps, tables_ready,
     ids, place_ready, sent, padded, held, pad_ready) = (sem("r_" + n) for n in names)

    def hold(eng):
        eng.sem_inc(held, 1)

    with nc.Block() as block:
        @block.sync
        def _(sp):
            sp.dma_start(rw[:], d["L0_ffn_router_w"]).then_inc(w_in, 16)
            sp.dma_start(bias_rows[0:EXPERTS * CHUNKS, :], d["L0_ffn_b_fc"].rearrange("e (a p) -> (e a) p", p=P))\
                .then_inc(b_in, 16)
            sp.dma_start(bias_rows[EXPERTS * CHUNKS:, :], d["L0_ffn_b_proj"]).then_inc(b_in, 16)
            for e in range(EXPERTS):
                if e >= 1:
                    sp.wait_ge(raw_in, 32 * e)
                if e >= 2:
                    sp.wait_ge(lo_done, e - 1)
                sp.dma_start(raw[:, e % 2, 0], d["L0_ffn_w_fc"][e]).then_inc(raw_in, 16)
                sp.dma_start(raw[:, e % 2, 1].rearrange("p (a c) -> p a c", c=DM),
                             d["L0_ffn_w_proj"][e].rearrange("(a p) c -> p a c", p=P)).then_inc(raw_in, 16)
            for n in range(PADDED):
                first = EXPERTS * REGION + n * RT
                if n >= SPARE:
                    e = n - SPARE
                    if e == 0:
                        sp.wait_ge(tables_ready, 3)
                    first = sp.value_load(ends[0:1, e:e + 1], min_val=e * REGION, max_val=e * REGION + NTOK)
                sp.wait_ge(pad_ready, n + 1)
                sp.dma_start(tokens_to[bass.ds(first, RT), :].rearrange("(p r) w -> p r w", p=P), pad[:])\
                    .then_inc(padded, 16)
            sp.wait_ge(padded, 16 * PADDED)

        @block.gpsimd
        def _(pool):
            pool.memset(before[:], 1.0).then_inc(consts, 1)
            pool.memset(ones[:], 1.0).then_inc(consts, 1)
            pool.memset(pad[:], 0.0).then_inc(consts, 1)
            pool.wait_ge(consts, 3)
            pool.affine_select(out=before[:], in_=before[:], compare_op=ALU.is_gt, fill=0.0, base=0,
                               pattern=[[1, P]], channel_multiplier=-1).then_inc(consts, 1)
            pool.iota(pad[:, :, DM], pattern=[[1, RT // P]], base=2 * NTOK, channel_multiplier=RT // P,
                      allow_small_or_imprecise_dtypes=True).then_inc(consts, 1)
            pool.iota(order[:], pattern=[[0, TILES], [-1, EXPERTS]], base=EXPERTS, channel_multiplier=0,
                      allow_small_or_imprecise_dtypes=True).then_inc(consts, 1)
            pool.iota(tnum[:], pattern=[[1, ETILES]], base=0, channel_multiplier=0,
                      allow_small_or_imprecise_dtypes=True).then_inc(consts, 1)
            pool.iota(base[:], pattern=[[REGION, EXPERTS]], base=0, channel_multiplier=0,
                      allow_small_or_imprecise_dtypes=True).then_inc(consts, 1)
            for k in range(2):
                pool.iota(rows[:, :, k, DM], pattern=[[2 * P, TILES]], base=k, channel_multiplier=2,
                          allow_small_or_imprecise_dtypes=True).then_inc(ids, 1)
                pool.memset(rows[:, :, k, DM + 2:RW], 0.0).then_inc(ids, 1)
            pool.wait_ge(ids, 4)
            pool.wait_ge(place_ready, 2)
            pool.wait_ge(copied, SUPERS)
            for t in range(TILES):
                for k in range(2):
                    pool.indirect_dma_start(
                        tokens_to, bass.IndirectOffsetOnAxis(ap=place_u[:, k, t:t + 1], axis=0),
                        rows[:, t, k, :], None).then_inc(sent, 16)
            pool.wait_ge(sent, 32 * TILES)

        @block.scalar
        def _(act):
            act.wait_ge(rwt_ps, 1)
            act.activation(rw_t[:], ps_w[:, 0, 0:EXPERTS], ACT.Copy).then_inc(rwt_sb, 1)
            act.wait_ge(bias_ps, 1)
            act.activation(ball[:, :, 0:CHUNKS], ps_w[:, 1, 0:EXPERTS * CHUNKS].rearrange("p (e a) -> p e a", e=EXPERTS),
                           ACT.Copy).then_inc(bias_sb, 1)
            act.activation(ball[:, :, CHUNKS], ps_w[:, 1, EXPERTS * CHUNKS:EXPERTS * (CHUNKS + 1)], ACT.Copy)\
                .then_inc(bias_sb, 1)

            def step(s, u):
                if there(s, SUPERS):
                    act.wait_ge(xt_ps, s + 1)
                    act.activation(xn_t[:], ps_t[:], ACT.Copy).then_inc(xt_sb, 1)
                    act.wait_ge(xn_ready, s * QUAD + QUAD)
                    act.activation(rows[:, bass.ds(s * QUAD, QUAD), :, 0:DM],
                                   xn[:, u].unsqueeze(2).broadcast_to([P, QUAD, 2, DM]), ACT.Copy).then_inc(copied, 1)

            sweep(act, step)
            for e in range(EXPERTS):
                act.wait_ge(raw_in, 32 * e + 32)
                for k in range(2):
                    act.activation(wall[:, e, 2 * k], raw[:, e % 2, k], ACT.Copy).then_inc(hi_done, 1)
            act.wait_ge(diff, 1)
            act.activation(gate[:, 1], pick[:], ACT.Exp).then_inc(ratio, 1)

        @block.tensor
        def _(pe):
            pe.wait_ge(w_in, 16)
            pe.transpose(ps_w[:, 0, 0:EXPERTS], rw[:], ident[0:EXPERTS, 0:EXPERTS]).then_inc(rwt_ps, 1)
            pe.wait_ge(b_in, 32)
            pe.wait_ge(rwt_sb, 1)
            n = EXPERTS * (CHUNKS + 1)
            pe.transpose(ps_w[:, 1, 0:n], bias_rows[:], ident[0:n, 0:n]).then_inc(bias_ps, 1)

            def step(s, u):
                if there(s, SUPERS):
                    pe.wait_ge(xn_ready, s * QUAD + QUAD)
                    if later(s, 1):
                        pe.wait_ge(xt_sb, s)
                    for k in range(QUAD):
                        mm = pe.transpose(ps_t[:, k], xn[:, u, k], ident[:])
                    mm.then_inc(xt_ps, 1)
                    pe.wait_ge(xt_sb, s + 1)
                    if later(s, 2):
                        pe.wait_ge(l_sb, s - 1)
                    for k in range(QUAD):
                        mm = pe.matmul(ps_l[u][:, k, 0:EXPERTS], xn_t[:, k], rw_t[:], start=True, stop=True)
                    mm.then_inc(l_ps, 1)

            sweep(pe, step)
            pe.wait_ge(consts, 4)
            pe.wait_ge(chosen_ready, 1)
            flat = chosen[:].rearrange("p t e -> p (t e)")
            pe.matmul(ps_c[:].rearrange("p t e -> p (t e)"), before[:], flat, start=True, stop=True).then_inc(cn_ps, 1)
            pe.matmul(ps_n[:].rearrange("p t e -> p (t e)"), ones[:], flat, start=True, stop=True).then_inc(cn_ps, 1)

        @block.vector
        def _(dve):
            def step(s, u):
                if there(s, SUPERS):
                    if later(s, 2):
                        dve.wait_ge(xt_ps, s - 1)
                        dve.wait_ge(copied, s - 1)
                    for k in range(QUAD):
                        tile = s * QUAD + k
                        dve.tensor_scalar(xn[:, u, k], row(x_sb, tile), mean[:, bass.ds(tile, 1)],
                                          rstd[:, bass.ds(tile, 1)], ALU.subtract, ALU.mult).then_inc(xn_ready, 1)
                if there(s - 1, SUPERS):
                    dve.wait_ge(l_ps, s)
                    dve.tensor_copy(logits[:, bass.ds((s - 1) * QUAD, QUAD), :], ps_l[1 - u][:, :, 0:EXPERTS])\
                        .then_inc(l_sb, 1)

            sweep(dve, step)
            for e in range(EXPERTS):
                dve.wait_ge(hi_done, 2 * e + 2)
                dve.tensor_tensor(wall[:, e].rearrange("p (k w) n -> p k w n", w=2)[:, :, 1], raw[:, e % 2],
                                  wall[:, e].bitcast(F32).rearrange("p (k w) n -> p k w n", w=2)[:, :, 0],
                                  ALU.subtract).then_inc(lo_done, 1)

            at = 0

            def then(ins):
                nonlocal at
                at += 1
                ins.then_inc(step_done, 1)
                dve.wait_ge(step_done, at)

            def wide(x):
                return x.unsqueeze(2).broadcast_to(TE)

            dve.wait_ge(l_sb, SUPERS)
            dve.wait_ge(consts, 8)
            for k, (src, hot) in enumerate(((logits, first), (work, second))):
                then(dve.tensor_reduce(top[:, k], src[:], AX_X, ALU.max))
                then(dve.tensor_tensor(hot[:], src[:], wide(top[:, k]), ALU.is_equal))
                then(dve.tensor_tensor(hot[:], hot[:], order[:], ALU.mult))
                then(dve.tensor_reduce(pick[:], hot[:], AX_X, ALU.max))
                then(dve.tensor_tensor(hot[:], order[:], wide(pick[:]), ALU.is_equal))
                if k == 0:
                    then(dve.scalar_tensor_tensor(out=work[:], in0=first[:], scalar=-FMAX, in1=logits[:],
                                                  op0=ALU.mult, op1=ALU.add))
            then(dve.tensor_tensor(chosen[:], first[:], second[:], ALU.add))
            dve.sem_inc(chosen_ready, 1)
            dve.tensor_tensor(pick[:], top[:, 1], top[:, 0], ALU.subtract).then_inc(diff, 1)
            dve.wait_ge(ratio, 1)
            then(dve.tensor_scalar(gate[:, 0], gate[:, 1], 1.0, None, ALU.add))
            then(dve.reciprocal(gate[:, 0], gate[:, 0]))
            then(dve.tensor_scalar(gate[:, 0], gate[:, 0], tg[:, 1:2], None, ALU.mult))
            then(dve.tensor_tensor(gate[:, 1], gate[:, 1], gate[:, 0], ALU.mult))
            dve.wait_ge(ids, 4)
            for k in range(2):
                then(dve.tensor_copy(rows[:, :, k, DM + 1], gate[:, k]))
            dve.wait_ge(cn_ps, 2)
            then(dve.tensor_copy(total[:].rearrange("p e t -> p t e"), ps_n[:]))
            then(dve.memset(resets[:], 1.0))
            then(dve.memset(resets[:, :, 0], 0.0))
            then(dve.memset(eones[:], 1.0))
            then(dve.tensor_tensor_scan(upto[:].rearrange("p e t -> p (e t)"), resets[:].rearrange("p e t -> p (e t)"),
                                        total[:].rearrange("p e t -> p (e t)"), 0.0, ALU.mult, ALU.add))
            then(dve.tensor_copy(count[:], upto[:, :, TILES - 1]))
            then(dve.tensor_tensor(upto[:], upto[:], total[:], ALU.subtract))
            then(dve.tensor_tensor(upto[:], upto[:], base[:].unsqueeze(2).broadcast_to([P, EXPERTS, TILES]), ALU.add))
            then(dve.tensor_tensor(work[:], ps_c[:], upto[:].rearrange("p e t -> p t e"), ALU.add))
            for k, hot in enumerate((first, second)):
                then(dve.tensor_tensor(hot[:], hot[:], work[:], ALU.mult))
                then(dve.tensor_reduce(place[:, k], hot[:], AX_X, ALU.add))
                dve.tensor_copy(place_u[:, k], place[:, k]).then_inc(place_ready, 1)
            then(dve.tensor_scalar(ntile[:], count[:], 1.0 / RT, (RT - 1.0) / RT - 0.5 + 0.5 / RT, ALU.mult, ALU.add))
            then(dve.tensor_scalar(ntile[:], ntile[:], MAGIC, MAGIC, ALU.add, ALU.subtract))
            then(dve.tensor_tensor_scan(tile_end[:], eones[:], ntile[:], 0.0, ALU.mult, ALU.add))
            then(dve.tensor_scalar(skip[:], ntile[:], -float(RT), float(REGION), ALU.mult, ALU.add))
            then(dve.tensor_scalar(trow[:], tnum[:], float(RT), None, ALU.mult))
            then(dve.memset(texp[:], 0.0))
            for e in range(EXPERTS):
                then(dve.tensor_scalar(past[:], tnum[:], tile_end[:, e:e + 1], None, ALU.is_ge))
                then(dve.scalar_tensor_tensor(out=trow[:], in0=past[:], scalar=skip[:, e:e + 1], in1=trow[:],
                                              op0=ALU.mult, op1=ALU.add))
                then(dve.tensor_tensor(texp[:], texp[:], past[:], ALU.add))
            then(dve.tensor_scalar(texp[:], texp[:], EXPERTS - 1.0, None, ALU.min))
            then(dve.tensor_tensor(count[:], count[:], base[:], ALU.add))
            dve.tensor_copy(tables[0:1, 0], trow[0:1, :]).then_inc(tables_ready, 1)
            dve.tensor_copy(tables[0:1, 1], texp[0:1, :]).then_inc(tables_ready, 1)
            dve.tensor_copy(ends[:], count[0:1, :]).then_inc(tables_ready, 1)
            dve.sem_inc(pad_ready, 1)
            for n in range(1, PADDED):
                dve.wait_ge(padded, 16 * n)
                dve.tensor_scalar(pad[:, :, DM], pad[:, :, DM], float(RT), None, ALU.add).then_inc(pad_ready, 1)


def experts(nc, ctx, d, g, sem, tokens_to, results, wall, ball, tables):
    ident = g["ident"]

    def sb(name, shape, dt):
        return ctx.enter_context(nc.sbuf_tensor(name, shape, dt))

    NR = RT // P
    w = sb("e_w", [P, 2, 4, HID], F32R)
    b = sb("e_b", [P, 2, CHUNKS + 1], F32)
    rows_in = sb("e_rows", [P, 2, NR, RW], F32)
    xt = sb("e_xt", [P, 2, 2, RT], F32R)
    h = sb("e_h", [P, 2, RT], F32)
    hp = sb("e_hp", [P, 2, 2, RT], F32R)
    yt = sb("e_yt", [P, RT], F32)
    y = sb("e_y", [P, 2, NR, DM], F32)
    to = sb("e_to", [P, 2, NR], U32)
    to_all = sb("e_to_all", [P, ETILES, NR], U32)
    weight = sb("e_weight", [P, ETILES, NR], F32)

    ps_x = ctx.enter_context(nc.psum_tensor("e_ps_x", [P, NR, P], F32))
    ps_h = [ctx.enter_context(nc.psum_tensor(f"e_ps_h{n}", [P, RT], F32)) for n in range(2)]
    ps_y = ctx.enter_context(nc.psum_tensor("e_ps_y", [P, RT], F32))
    ps_r = ctx.enter_context(nc.psum_tensor("e_ps_r", [P, NR, P], F32))

    names = ("held", "w_in", "rows_in", "xt_ps", "xt_hi", "xt_lo", "h_ps", "h_sb", "h_hi", "h_lo", "h_used", "meta_ready", "yt_sb",
             "yr_ps", "to_ready", "y_sb")
    (held, w_in, r_in, xt_ps, xt_hi, xt_lo, h_ps, h_sb, h_hi, h_lo, h_used, meta_ready, yt_sb, yr_ps, to_ready, y_sb) = (
        sem("e_" + n) for n in names)
    sent = [sem(f"e_sent{v}") for v in range(2)]

    def hold(eng):
        eng.sem_inc(held, 1)

    def tiles(eng, step):
        for t in range(-2, 4):
            step(t, t % 2)
        pairs = (ETILES - 6) // 2
        with eng.Fori(0, pairs) as i:
            step(i * 2 + 4, 0)
            step(i * 2 + 5, 1)
        for t in range(4 + 2 * pairs, ETILES + 1):
            step(t, t % 2)

    with nc.Block() as block:
        @block.sync
        def _(sp):
            def step(t, u):
                n = t + 1
                if there(n, ETILES):
                    v = 1 - u
                    if later(n, 1):
                        sp.wait_ge(w_in, n * 32)
                        hold(sp)
                    if later(n, 2):
                        sp.wait_ge(yt_sb, n - 1)
                        hold(sp)
                    expert = sp.value_load(tables[0:1, 1, bass.ds(n, 1)], min_val=0, max_val=EXPERTS - 1)
                    sp.dma_start(w[:, v].bitcast(F32),
                                 wall[:, bass.ds(expert, 1)].rearrange("p a k n -> p (a k) n").bitcast(F32))\
                        .then_inc(w_in, 16)
                    sp.dma_start(b[:, v], ball[:, bass.ds(expert, 1)].rearrange("p a k -> p (a k)")).then_inc(w_in, 16)
                n = t + 2
                if there(n, ETILES):
                    if later(n, 1):
                        sp.wait_ge(r_in, n * 16)
                        hold(sp)
                    if later(n, 2):
                        sp.wait_ge(xt_ps, n - 1)
                        hold(sp)
                        sp.wait_ge(meta_ready, n * 2 - 2)
                        hold(sp)
                    first = sp.value_load(tables[0:1, 0, bass.ds(n, 1)], min_val=0, max_val=EXPERTS * REGION + (SPARE - 1) * RT)
                    sp.dma_start(rows_in[:, u], tokens_to[bass.ds(first, RT), :].rearrange("(p r) w -> p r w", p=P))\
                        .then_inc(r_in, 16)

            tiles(sp, step)

        @block.gpsimd
        def _(pool):
            def step(t, u):
                n = t - 1
                if there(n, ETILES):
                    v = 1 - u
                    pool.wait_ge(meta_ready, n * 2 + 2)
                    if later(n, 2):
                        pool.wait_ge(sent[v], (n - v) * 32)
                    hold(pool)
                    pool.tensor_copy(to[:, v], to_all[:, bass.ds(n, 1)].rearrange("p a r -> p (a r)"))\
                        .then_inc(to_ready, 1)
                    pool.wait_ge(to_ready, n + 1)
                    for r in range(NR):
                        pool.wait_ge(y_sb, n * NR + r + 1)
                        hold(pool)
                        pool.indirect_dma_start(
                            results, bass.IndirectOffsetOnAxis(ap=to[:, v, r:r + 1], axis=0),
                            y[:, v, r], None).then_inc(sent[v], 16)

            tiles(pool, step)
            for v in range(2):
                pool.wait_ge(sent[v], 16 * NR * ((ETILES + 1 - v) // 2))

        @block.scalar
        def _(act):
            def step(t, u):
                n = t + 1

                def gelu(c):
                    act.wait_ge(h_ps, t * 4 + c + 1)
                    if c >= 2 or later(t, 1):
                        act.wait_ge(h_lo, t * 4 + c - 1)
                    act.activation(h[:, c % 2], ps_h[c % 2][:], ACT.Gelu_apprx_tanh,
                                   bias=b[:, u, c:c + 1]).then_inc(h_sb, 1)

                if there(t, ETILES):
                    act.wait_ge(w_in, t * 32 + 32)
                    gelu(0)
                if there(n, ETILES):
                    act.wait_ge(xt_ps, n + 1)
                    if later(n, 2):
                        act.wait_ge(h_ps, n * 4 - 4)
                    act.activation(xt[:, 1 - u, 0], ps_x[:].rearrange("p r t -> p (r t)"), ACT.Copy).then_inc(xt_hi, 1)
                if there(t, ETILES):
                    for c in range(1, CHUNKS):
                        gelu(c)
                    act.wait_ge(h_used, t * 4 + 4)
                    if later(t, 1):
                        act.wait_ge(yr_ps, t)
                    act.activation(yt[:], ps_y[:], ACT.Identity, bias=b[:, u, CHUNKS:CHUNKS + 1]).then_inc(yt_sb, 1)

            tiles(act, step)

        @block.tensor
        def _(pe):
            def step(t, u):
                n = t + 1

                def up(c):
                    if later(t, 1) or c >= 2:
                        pe.wait_ge(h_sb, t * 4 + c - 1)
                    at = slice(P * c, P * c + P)
                    pe.matmul(ps_h[c % 2][:], w[:, u, 0, at], xt[:, u, 0], start=True, stop=False)
                    pe.matmul(ps_h[c % 2][:], w[:, u, 1, at], xt[:, u, 0], start=False, stop=False)
                    if c == 0:
                        pe.wait_ge(xt_lo, t + 1)
                    pe.matmul(ps_h[c % 2][:], w[:, u, 0, at], xt[:, u, 1], start=False, stop=True).then_inc(h_ps, 1)

                def down(c):
                    pe.wait_ge(h_hi, t * 4 + c + 1)
                    if c == 0 and later(t, 1):
                        pe.wait_ge(yt_sb, t)
                    at = slice(P * c, P * c + P)
                    pe.matmul(ps_y[:], w[:, u, 2, at], hp[:, c % 2, 0], start=(c == 0), stop=False)
                    pe.matmul(ps_y[:], w[:, u, 3, at], hp[:, c % 2, 0], start=False, stop=False)
                    pe.wait_ge(h_lo, t * 4 + c + 1)
                    mm = pe.matmul(ps_y[:], w[:, u, 2, at], hp[:, c % 2, 1], start=False, stop=(c == CHUNKS - 1))
                    mm.then_inc(h_used, 1)

                if there(t, ETILES):
                    pe.wait_ge(w_in, t * 32 + 32)
                    pe.wait_ge(xt_hi, t + 1)
                    up(0)
                    up(1)
                if there(n, ETILES):
                    pe.wait_ge(r_in, n * 16 + 16)
                    if later(n, 1):
                        pe.wait_ge(xt_lo, n)
                    for r in range(NR):
                        mm = pe.transpose(ps_x[:, r], rows_in[:, 1 - u, r, 0:DM], ident[:])
                    mm.then_inc(xt_ps, 1)
                if there(t - 1, ETILES):
                    pe.wait_ge(yt_sb, t)
                    if later(t - 1, 1):
                        pe.wait_ge(y_sb, t * 4 - 4)
                    for r in range(NR):
                        mm = pe.transpose(ps_r[:, r], yt[:, P * r:P * r + P], ident[:])
                    mm.then_inc(yr_ps, 1)
                if there(t, ETILES):
                    for c in range(CHUNKS):
                        down(c)
                        if c + 2 < CHUNKS:
                            up(c + 2)

            tiles(pe, step)

        @block.vector
        def _(dve):
            def step(t, u):
                n = t + 1

                def split(c):
                    dve.wait_ge(h_sb, t * 4 + c + 1)
                    if c >= 2 or later(t, 1):
                        dve.wait_ge(h_used, t * 4 + c - 1)
                    dve.tensor_copy(hp[:, c % 2, 0], h[:, c % 2]).then_inc(h_hi, 1)
                    dve.wait_ge(h_hi, t * 4 + c + 1)
                    dve.tensor_tensor(hp[:, c % 2, 1], h[:, c % 2], hp[:, c % 2, 0].bitcast(F32),
                                      ALU.subtract).then_inc(h_lo, 1)

                if there(t, ETILES):
                    split(0)
                if there(n, ETILES):
                    dve.wait_ge(r_in, n * 16 + 16)
                    hold(dve)
                    dve.tensor_copy(to_all[:, bass.ds(n, 1)].rearrange("p a r -> p (a r)"), rows_in[:, 1 - u, :, DM])\
                        .then_inc(meta_ready, 1)
                    dve.tensor_copy(weight[:, bass.ds(n, 1)].rearrange("p a r -> p (a r)"),
                                    rows_in[:, 1 - u, :, DM + 1]).then_inc(meta_ready, 1)
                    dve.wait_ge(xt_hi, n + 1)
                    if later(n, 2):
                        dve.wait_ge(h_ps, n * 4 - 4)
                    dve.tensor_tensor(xt[:, 1 - u, 1], ps_x[:].rearrange("p r t -> p (r t)"),
                                      xt[:, 1 - u, 0].bitcast(F32), ALU.subtract).then_inc(xt_lo, 1)
                if there(t, ETILES):
                    split(1)
                if there(t - 1, ETILES):
                    v = 1 - u
                    if later(t - 1, 2):
                        dve.wait_ge(sent[v], (t - 1 - v) * 32)
                    dve.wait_ge(yr_ps, t)
                    for r in range(NR):
                        dve.tensor_scalar(y[:, v, r], ps_r[:, r], weight[:, bass.ds(t - 1, 1), r], None,
                                          ALU.mult).then_inc(y_sb, 1)
                if there(t, ETILES):
                    split(2)
                    split(3)

            tiles(dve, step)


def gather(nc, ctx, d, g, sem, results):
    x_sb, stats = g["x_sb"], g["stats"]
    two = ctx.enter_context(nc.sbuf_tensor("f_two", [P, 2, QUAD, 2, DM], F32))
    two_in = [sem(f"f_two_in{u}") for u in range(2)]
    added, x_out, stats_out, held = sem("f_added"), sem("f_x_out"), sem("f_stats_out"), sem("f_held")
    view = results[0:2 * NTOK, :].rearrange("(t p k) c -> p t k c", p=P, k=2)

    with nc.Block() as block:
        @block.sync
        def _(sp):
            for u in range(2):
                sp.dma_start(two[:, u], view[:, QUAD * u:QUAD * u + QUAD]).then_inc(two_in[u], 16)
            with sp.Fori(0, SUPERS // 2 - 1) as i:
                for u in range(2):
                    s = i * 2 + 2 + u
                    sp.wait_ge(x_out, s - 1)
                    sp.sem_inc(held, 1)
                    sp.dma_start(two[:, u], view[:, bass.ds(s * QUAD, QUAD)]).then_inc(two_in[u], 16)

        @block.vector
        def _(dve):
            with dve.Fori(0, SUPERS // 2) as i:
                for u in range(2):
                    s = i * 2 + u
                    dve.wait_ge(two_in[u], i * 16 + 16)
                    xs = x_sb[:, bass.ds(s * QUAD, QUAD), :]
                    dve.tensor_tensor(two[:, u, :, 0], two[:, u, :, 0], two[:, u, :, 1], ALU.add).then_inc(added, 1)
                    dve.wait_ge(added, s + 1)
                    dve.tensor_tensor(xs, xs, two[:, u, :, 0], ALU.add).then_inc(x_out, 1)
                    dve.wait_ge(x_out, s + 1)
                    for k in range(QUAD):
                        tile = s * QUAD + k
                        dve.bn_stats(row(stats, tile), row(x_sb, tile)).then_inc(stats_out, 1)


def setup(nc, ctx, d, g, sb, sem):
    x_sb, stats, ident, tg = g["x_sb"], g["stats"], g["ident"], g["tanh_gates"]
    CHUNKS = 8
    CT = TILES // CHUNKS
    x_view = d["x"].rearrange("(a b) s c -> (b s) a c", b=2)
    x_in = [sem(f"x_in{n}") for n in range(CHUNKS)]
    gates_in, ident_step, gates_ready = sem("gates_in"), sem("ident_step"), sem("gates_ready")
    stats_out = sem("stats_out")
    block = ctx.enter_context(nc.Block())

    @block.sync
    def _(sp):
        for n in range(CHUNKS):
            sp.dma_start(x_sb[:, CT * n:CT * n + CT, :], x_view[:, CT * n:CT * n + CT, :]).then_inc(x_in[n], 16)
        for n, (name, at) in enumerate((("g_xattn", 0), ("g_ffn", 0), ("g_xattn", 1), ("g_ffn", 1))):
            sp.dma_start(tg[:, n:n + 1], d[name][at:at + 1].partition_broadcast(P)).then_inc(gates_in, 16)

    @block.gpsimd
    def _(pool):
        pool.memset(ident[:], 0.0).then_inc(ident_step, 1)
        pool.wait_ge(ident_step, 1)
        pool.affine_select(out=ident[:], in_=ident[:], compare_op=ALU.not_equal, fill=1.0, base=0,
                           pattern=[[-1, P]], channel_multiplier=1).then_inc(ident_step, 1)

    @block.scalar
    def _(act):
        act.wait_ge(gates_in, 64)
        act.activation(tg[:], tg[:], ACT.Tanh).then_inc(gates_ready, 1)

    @block.vector
    def _(dve):
        for t in range(TILES):
            if t % CT == 0:
                dve.wait_ge(x_in[t // CT], 16)
            dve.bn_stats(stats[:, t], x_sb[:, t]).then_inc(stats_out, 1)


def layernorm_scales(nc, ctx, d, g, sb, sem):
    stats, mean, rstd = g["stats"], g["mean"], g["rstd"]
    uid = g["uid"] = g["uid"] + 1
    diff = sb(f"ln_diff{uid}", [P, TILES], F32)
    var = sb(f"ln_var{uid}", [P, TILES], F32)
    step, var_ready, std_ready = sem(f"ln_step{uid}"), sem(f"ln_var_ready{uid}"), sem(f"ln_std_ready{uid}")
    done = sem(f"ln_done{uid}")
    block = ctx.enter_context(nc.Block())

    @block.vector
    def _(dve):
        dve.tensor_tensor(mean[:], stats[:, :, 1], stats[:, :, 4], ALU.add).then_inc(step, 1)
        dve.tensor_tensor(diff[:], stats[:, :, 1], stats[:, :, 4], ALU.subtract).then_inc(step, 1)
        dve.tensor_tensor(var[:], stats[:, :, 2], stats[:, :, 5], ALU.add).then_inc(step, 1)
        dve.wait_ge(step, 1)
        dve.tensor_scalar(mean[:], mean[:], 0.5, None, ALU.mult).then_inc(step, 1)
        dve.wait_ge(step, 2)
        dve.tensor_tensor(diff[:], diff[:], diff[:], ALU.mult).then_inc(step, 1)
        dve.wait_ge(step, 3)
        dve.tensor_scalar(var[:], var[:], 1.0 / DM, LN_EPS, ALU.mult, ALU.add).then_inc(step, 1)
        dve.wait_ge(step, 6)
        dve.scalar_tensor_tensor(out=var[:], in0=diff[:], scalar=0.25, in1=var[:],
                                 op0=ALU.mult, op1=ALU.add).then_inc(var_ready, 1)
        dve.wait_ge(std_ready, 1)
        dve.reciprocal(rstd[:], var[:]).then_inc(done, 1)

    @block.scalar
    def _(act):
        act.wait_ge(var_ready, 1)
        act.activation(var[:], var[:], ACT.Sqrt).then_inc(std_ready, 1)


def store_x(nc, ctx, d, g, sb, sem):
    stored = sem("stored")
    block = ctx.enter_context(nc.Block())

    @block.sync
    def _(sp):
        sp.dma_start(d["out"].rearrange("(a b) s c -> (b s) a c", b=2), g["x_sb"][:]).then_inc(stored, 16)
        sp.wait_ge(stored, 16)


STAGES = (layernorm_scales, layer0_attention, layernorm_scales, mixture,
          layernorm_scales, layer1_attention, layernorm_scales, layer1_ffn)


def flamingo(nc, d, stages=None):
    with ExitStack() as whole:
        g = {
            "x_sb": whole.enter_context(nc.sbuf_tensor("x_sb", [P, TILES, DM], F32)),
            "stats": whole.enter_context(nc.sbuf_tensor("stats", [P, TILES, 6], F32)),
            "mean": whole.enter_context(nc.sbuf_tensor("mean", [P, TILES], F32)),
            "rstd": whole.enter_context(nc.sbuf_tensor("rstd", [P, TILES], F32)),
            "uid": 0,
            "ident": whole.enter_context(nc.sbuf_tensor("ident", [P, P], F32)),
            "tanh_gates": whole.enter_context(nc.sbuf_tensor("tanh_gates", [P, 4], F32)),
        }
        for stage in (setup, *(stages or STAGES)):
            with ExitStack() as ctx:
                def sb(name, shape, dt):
                    return ctx.enter_context(nc.sbuf_tensor(name, shape, dt))

                def sem(name):
                    stage_sems.append(nc.alloc_semaphore(name=name))
                    return stage_sems[-1]

                stage_sems = []
                stage(nc, ctx, d, g, sb, sem)
            nc.clear_and_free_semaphores(stage_sems)
            nc.all_engine_barrier()


_INS = ["x", "ctx_1024", "mask_1x1xSxS2_ff0", "mask_BxS2_bk1", "g_xattn", "g_ffn",
        "L0_xattn_Wq", "L0_xattn_bq", "L0_xattn_Wk", "L0_xattn_bk", "L0_xattn_Wv", "L0_xattn_bv",
        "L0_xattn_Wo", "L0_xattn_bo", "L0_ffn_router_w", "L0_ffn_w_fc", "L0_ffn_b_fc", "L0_ffn_w_proj",
        "L0_ffn_b_proj", "L1_xattn_Wq", "L1_xattn_bq", "L1_xattn_Wk", "L1_xattn_bk", "L1_xattn_Wv",
        "L1_xattn_bv", "L1_ffn_W1", "L1_ffn_b1", "L1_ffn_W2", "L1_ffn_b2"]


def kernel(**inputs):
    import numpy as _np
    import concourse.bacc as _bacc
    from concourse import mybir as _mybir
    from concourse.bass_utils import run_bass_kernel_spmd as _run

    nc = _bacc.Bacc("TRN2", target_bir_lowering=False, num_devices=1)
    arrays, d = {}, {}
    for name in _INS:
        a = _np.ascontiguousarray(inputs[name])
        arrays[f"in_{name}_dram"] = a
        d[name] = nc.dram_tensor(f"in_{name}_dram", a.shape, _mybir.dt.from_np(a.dtype), kind="ExternalInput").ap()
    d["out"] = nc.dram_tensor("out_dram", (BATCH, SEQ, DM), F32, kind="ExternalOutput").ap()
    flamingo(nc, d)
    r = _run(nc, [arrays], core_ids=[0])
    return r.results[0]["out_dram"]
```

```python
from contextlib import ExitStack

import concourse.bass as bass
from concourse import mybir

ALU = mybir.AluOpType
ACT = mybir.ActivationFunctionType
AX_X = mybir.AxisListType.X
F32 = mybir.dt.float32
F32R = mybir.dt.float32r
BF16 = mybir.dt.bfloat16
U8 = mybir.dt.uint8
U32 = mybir.dt.uint32

P = 128
BATCH, SEQ, DM = 128, 64, 128
NTOK = BATCH * SEQ
TILES = NTOK // P
QUAD = 4
SUPERS = TILES // QUAD
ST = QUAD * P
HEADS, DH = 16, 8
GROUPS = HEADS // 2
VW = 9
VB = 2 * GROUPS * VW
FMAX = 3.4028234663852886e38
LN_EPS = 1e-5
Q_SLOTS = (0, 0, 1, 1, 0, 2, 1, 2)
K_SLOTS = (0, 1, 0, 1, 2, 0, 2, 1)


def layer0_attention(nc, ctx, d, g, sb, sem):
    x_sb = g["x_sb"]
    ident, tg = g["ident"], g["tanh_gates"]

    wq = sb("a_wq", [P, DM], F32)
    wk = sb("a_wk", [P, DM], F32)
    wv = sb("a_wv", [P, DM], F32)
    wo = sb("a_wo", [P, DM], F32)
    bq = sb("a_bq", [P, 1], F32)
    bk = sb("a_bk", [P, 1], F32)
    bv = sb("a_bv", [P, DM], F32)
    bo = sb("a_bo", [P, DM], F32)
    mask = sb("a_mask", [P, SEQ], F32)
    ctx_in = sb("a_ctx_in", [P, 2, QUAD, DM], F32)
    stats, mean, rstd = g["stats"], g["mean"], g["rstd"]
    xn = sb("a_xn", [P, QUAD, DM], F32)
    xn_t = sb("a_xn_t", [P, ST], F32)
    ctx_t = sb("a_ctx_t", [P, 2, ST // SEQ, 2, SEQ], F32)
    qk = sb("a_qk", [P, 2, 2, ST], F32)
    parts = sb("a_parts", [P, 2, 2, 3, ST], BF16)
    stack = sb("a_stack", [P, 2, 2, GROUPS, ST], BF16)
    VALL = QUAD * 2 * VB
    vals = [sb(f"a_vals{u}", [P, VALL + SEQ], F32) for u in range(2)]
    probs = sb("a_probs", [P, 4, GROUPS, 2, SEQ], F32)
    top = sb("a_top", [P, 4, HEADS], F32)
    probs_t = sb("a_probs_t", [P, 2, GROUPS, P], F32)
    rsum = sb("a_rsum", [P, HEADS], F32)
    heads = sb("a_heads", [P, HEADS, DH], F32)
    heads_t = sb("a_heads_t", [P, P], F32)

    parked = nc.dram_tensor("a_parked", (2, 2, 3, P, ST), BF16, kind="Internal").ap()
    ps_s = [ctx.enter_context(nc.psum_tensor(f"a_ps_s{j}", [P, GROUPS, SEQ], F32)) for j in range(2)]
    ps_pt = [ctx.enter_context(nc.psum_tensor(f"a_ps_pt{j}", [P, 4, P], F32)) for j in range(2)]
    ps_1 = [ctx.enter_context(nc.psum_tensor(f"a_ps_1{j}", [P, ST], F32)) for j in range(2)]
    ps_o = ctx.enter_context(nc.psum_tensor("a_ps_o", [P, 2, 256], F32))
    ps_y = ctx.enter_context(nc.psum_tensor("a_ps_y", [P, 4, P], F32))

    w_in = sem("a_w_in")
    held = sem("a_held")
    consts = sem("a_consts")
    loaded = sem("a_loaded")
    xn_ready = sem("a_xn_ready")
    bo_added = sem("a_bo_added")
    xt_ps, ct_ps = sem("a_xt_ps"), sem("a_ct_ps")
    xt_sb, ct_sb = sem("a_xt_sb"), sem("a_ct_sb")
    q_ps, k_ps, qk_sb = sem("a_q_ps"), sem("a_k_ps"), sem("a_qk_sb")
    hi_cut, hi_off, mid_cut, split = (sem(f"a_{n}") for n in ("hi_cut", "hi_off", "mid_cut", "split"))
    parts_parked = sem("a_parts_parked")
    stacked = sem("a_stacked")
    v_ps, v_sb = sem("a_v_ps"), sem("a_v_sb")
    s_ps, s_sb = sem("a_s_ps"), sem("a_s_sb")
    top_ready, shifted, p_ready = sem("a_top_ready"), sem("a_shifted"), sem("a_p_ready")
    pt_ps, pt_sb = sem("a_pt_ps"), sem("a_pt_sb")
    o_ps, rsum_ready, o_sb = sem("a_o_ps"), sem("a_rsum_ready"), sem("a_o_sb")
    ot_ps, ot_sb = sem("a_ot_ps"), sem("a_ot_sb")
    y_ps, x_out, stats_out = sem("a_y_ps"), sem("a_x_out"), sem("a_stats_out")

    ctx_view = d["ctx_1024"].rearrange("(a b) s c -> (b s) a c", b=2)
    N_W = 12

    def sweep(eng, step):
        for s in range(-3, 1):
            step(s, s % 2)
        with eng.Fori(0, (SUPERS - 4) // 2) as i:
            step(i * 2 + 1, 1)
            step(i * 2 + 2, 0)
        for s in range(SUPERS - 3, SUPERS + 1):
            step(s, s % 2)

    def hold(eng):
        eng.sem_inc(held, 1)

    def known(n):
        return isinstance(n, int)

    def there(n, count):
        return not known(n) or 0 <= n < count

    def later(n, least):
        return not known(n) or n >= least

    block = ctx.enter_context(nc.Block())

    @block.sync
    def _(sp):
        for dst, src in ((wq, "L0_xattn_Wq"), (wk, "L0_xattn_Wk"), (wv, "L0_xattn_Wv"), (wo, "L0_xattn_Wo")):
            sp.dma_start(dst[:], d[src]).then_inc(w_in, 16)
        for dst, src in ((bq, "L0_xattn_bq"), (bk, "L0_xattn_bk")):
            sp.dma_start(dst[:], d[src].rearrange("(p a) -> p a", a=1)).then_inc(w_in, 16)
        for dst, src in ((bv, "L0_xattn_bv"), (bo, "L0_xattn_bo")):
            sp.dma_start(dst[:], d[src].partition_broadcast(P)).then_inc(w_in, 16)
        for b in range(2):
            sp.dma_start(mask[SEQ * b:SEQ * b + SEQ, :],
                         d["mask_1x1xSxS2_ff0"].rearrange("a b q k -> (a b q) k")).then_inc(w_in, 16)

        def step(s, u):
            nxt = s + 3
            if there(nxt, SUPERS):
                if later(nxt, 1):
                    sp.wait_ge(loaded, nxt * 16)
                    hold(sp)
                if later(nxt, 2):
                    sp.wait_ge(ct_ps, nxt - 1)
                    hold(sp)
                sp.dma_start(ctx_in[:, 1 - u], ctx_view[:, bass.ds(nxt * QUAD, QUAD), :]).then_inc(loaded, 16)
            nxt = s + 1
            if there(nxt, SUPERS):
                if later(nxt, 1):
                    sp.wait_ge(stacked, nxt * 512)
                    hold(sp)
                if later(nxt, 2):
                    sp.wait_ge(s_ps, (nxt - 1) * QUAD)
                    hold(sp)
                sp.wait_ge(parts_parked, nxt * 16 + 16)
                hold(sp)
                for x in range(2):
                    for slot, part in enumerate((Q_SLOTS, K_SLOTS)[x]):
                        rows = parked[1 - u, x, part].rearrange("(g j e) t -> j e g t", g=GROUPS, j=2)
                        for j in range(2):
                            sp.dma_start(stack[64 * j + DH * slot:64 * j + DH * slot + DH, 1 - u, x], rows[j])\
                              .then_inc(stacked, 16)
            nxt = s + 2
            if there(nxt, SUPERS):
                sp.wait_ge(split, nxt + 1)
                hold(sp)
                if later(nxt, 2):
                    sp.wait_ge(stacked, nxt * 512 - 512)
                    hold(sp)
                sp.dma_start(parked[u].rearrange("x r p t -> p x r t"), parts[:, u]).then_inc(parts_parked, 16)

        sweep(sp, step)

    @block.gpsimd
    def _(pool):
        for u in range(2):
            pool.memset(vals[u][:], 0.0).then_inc(consts, 1)
        pool.wait_ge(consts, 2)
        for u in range(2):
            for j in range(2):
                ones = vals[u][64 * j:64 * j + 64, 0:VALL].rearrange("p (n w) -> p n w", w=2 * VW)
                pool.memset(ones[:, :, VW * j + DH], 1.0).then_inc(consts, 1)
        pool.wait_ge(consts, 6)
        pool.wait_ge(w_in, 16 * 10)
        pool.tensor_scalar(mask[:], mask[:], FMAX, None, ALU.mult).then_inc(consts, 1)
        pool.tensor_scalar(bo[:], bo[:], tg[:, 0:1], None, ALU.mult).then_inc(consts, 1)
        pool.wait_ge(consts, 8)

        def step(s, u):
            if there(s + 1, SUPERS):
                n = s + 1
                pool.wait_ge(xn_ready, n * QUAD + QUAD)
                xs = x_sb[:, bass.ds(n * QUAD, QUAD), :]
                pool.tensor_tensor(xs, xs, bo[:].unsqueeze(1).broadcast_to([P, QUAD, DM]), ALU.add)\
                    .then_inc(bo_added, 1)
            n = s + 2
            for j in range(QUAD):
                t = s * QUAD + j
                if j == 2 and there(n, SUPERS):
                    pool.wait_ge(hi_cut, n * 2 + 2)
                    pool.tensor_tensor(qk[:, u], qk[:, u], parts[:, u, :, 0, :], ALU.subtract).then_inc(hi_off, 1)
                if j == 3 and there(n, SUPERS):
                    pool.wait_ge(mid_cut, n + 1)
                    pool.tensor_tensor(parts[:, u, :, 2, :], qk[:, u], parts[:, u, :, 1, :],
                                       ALU.subtract).then_inc(split, 1)
                if there(t, TILES):
                    pool.wait_ge(top_ready, t + 1)
                    p = probs[:, j].rearrange("p g j k -> p (g j) k")
                    pool.tensor_tensor(p, p, top[:, j].unsqueeze(2).broadcast_to([P, HEADS, SEQ]),
                                       ALU.subtract).then_inc(shifted, 1)

        sweep(pool, step)

    @block.scalar
    def _(act):
        act.wait_ge(w_in, 16 * 10)

        def step(s, u):
            n = s + 2
            for j in range(QUAD):
                t = s * QUAD + j
                if there(t - 2, TILES):
                    if later(t - 2, 2):
                        act.wait_ge(o_ps, t - 3)
                    for h in range(2):
                        act.wait_ge(pt_ps, t * 2 - 3 + h)
                        act.activation(probs_t[:, j % 2, 4 * h:4 * h + 4, :], ps_pt[h][:], ACT.Copy)\
                            .then_inc(pt_sb, 1)
                if there(n, SUPERS) and j == 3:
                    act.wait_ge(hi_off, n + 1)
                    act.activation(parts[:, u, :, 1, :], qk[:, u], ACT.Copy).then_inc(mid_cut, 1)
                if there(t - 1, TILES):
                    act.wait_ge(shifted, t)
                    act.activation(probs[:, (j + 3) % 4], probs[:, (j + 3) % 4], ACT.Exp).then_inc(p_ready, 1)
                if there(t - 3, TILES):
                    act.wait_ge(ot_ps, t - 2)
                    act.activation(heads_t[:], ps_y[:, 0, :], ACT.Copy).then_inc(ot_sb, 1)
                if there(n, SUPERS) and j == 0:
                    act.wait_ge(xt_ps, n + 1)
                    act.activation(xn_t[:], ps_1[0][:], ACT.Copy).then_inc(xt_sb, 1)
                    act.wait_ge(ct_ps, n + 1)
                    if later(n, 2):
                        act.wait_ge(v_ps, n * 2 - 2)
                    act.activation(ctx_t[:, u], ps_1[1][:].rearrange("p (b k) -> p b k", k=SEQ).unsqueeze(2)
                                   .broadcast_to([P, ST // SEQ, 2, SEQ]), ACT.Copy).then_inc(ct_sb, 1)
                if there(n, SUPERS) and j == 1:
                    if later(n, 2):
                        act.wait_ge(split, n - 1)
                        act.wait_ge(parts_parked, n * 16 - 16)
                    for x, ps, bias in ((0, q_ps, bq), (1, k_ps, bk)):
                        act.wait_ge(ps, n + 1)
                        act.activation(qk[:, u, x], ps_1[x][:], ACT.Identity, bias=bias[:, 0:1]).then_inc(qk_sb, 1)
                        act.activation(parts[:, u, x, 0], ps_1[x][:], ACT.Identity, bias=bias[:, 0:1])\
                            .then_inc(hi_cut, 1)

        sweep(act, step)

    @block.tensor
    def _(pe):
        pe.wait_ge(w_in, 16 * 10)

        def step(s, u):
            n, nv = s + 2, s + 1
            for j in range(QUAD):
                t = s * QUAD + j
                if there(t - 2, TILES):
                    pe.wait_ge(p_ready, t - 1)
                    for h in range(2):
                        if later(t - 2, 1):
                            pe.wait_ge(pt_sb, t * 2 - 5 + h)
                        for k in range(4):
                            mm = pe.transpose(ps_pt[h][:, k, :],
                                              probs[:, (j + 2) % 4, 4 * h + k].rearrange("p j k -> p (j k)"),
                                              ident[:])
                        mm.then_inc(pt_ps, 1)
                if there(t, TILES):
                    if j == 0:
                        pe.wait_ge(stacked, (s + 1) * 512)
                    if later(t, 1):
                        pe.wait_ge(s_sb, t * 2)
                    hold(pe)
                    for gr in range(GROUPS):
                        for h in range(2):
                            for b in range(2):
                                at = slice(P * j + SEQ * b, P * j + SEQ * b + SEQ)
                                rows = slice(64 * h, 64 * h + 64)
                                mm = pe.matmul(ps_s[h][SEQ * b:SEQ * b + SEQ, gr, :],
                                               stack[rows, u, 0, gr, at], stack[rows, u, 1, gr, at],
                                               start=True, stop=True)
                    mm.then_inc(s_ps, 1)
                if there(t - 3, TILES):
                    if later(t - 3, 1):
                        pe.wait_ge(x_out, t - 3)
                    pe.wait_ge(o_sb, t * 2 - 4)
                    pe.transpose(ps_y[:, 0, :], heads[:].rearrange("p h e -> p (h e)"), ident[:])\
                        .then_inc(ot_ps, 1)
                if there(n, SUPERS) and j == 0:
                    pe.wait_ge(xn_ready, n * QUAD + QUAD)
                    if later(n, 2):
                        pe.wait_ge(v_sb, n * 4 - 4)
                    elif n == 1:
                        pe.wait_ge(hi_cut, 2)
                    for k in range(QUAD):
                        mm = pe.transpose(ps_1[0][:, P * k:P * k + P], xn[:, k, :], ident[:])
                    mm.then_inc(xt_ps, 1)
                    pe.wait_ge(loaded, n * 16 + 16)
                    for k in range(QUAD):
                        mm = pe.transpose(ps_1[1][:, P * k:P * k + P], ctx_in[:, u, k, :], ident[:])
                    mm.then_inc(ct_ps, 1)
                if there(n, SUPERS) and j == 1:
                    pe.wait_ge(xt_sb, n + 1)
                    pe.matmul(ps_1[0][:], wq[:], xn_t[:], start=True, stop=True).then_inc(q_ps, 1)
                    pe.wait_ge(ct_sb, n + 1)
                    pe.matmul(ps_1[1][:], wk[:], ctx_t[:, u, :, 0, :], start=True, stop=True).then_inc(k_ps, 1)
                if there(nv, SUPERS) and j == 2:
                    for h in range(2):
                        if there(n, SUPERS):
                            pe.wait_ge(hi_cut, n * 2 + 1 + h)
                        else:
                            pe.wait_ge(v_sb, nv * 4)
                        for b in range(4):
                            mm = pe.matmul(ps_1[h][:, P * b:P * b + P],
                                           ctx_t[:, 1 - u, 4 * h + b].rearrange("p a k -> p (a k)"), wv[:],
                                           start=True, stop=True)
                        mm.then_inc(v_ps, 1)
                if there(t - 2, TILES):
                    sv = s if j >= 2 else s - 1
                    pe.wait_ge(v_sb, (sv + 1) * 4)
                    if later(t - 2, 1):
                        pe.wait_ge(o_sb, t * 2 - 4)
                    v0 = 2 * VB * ((j + 2) % 4)
                    vv = vals[u if j >= 2 else 1 - u]
                    for gr in range(GROUPS):
                        if gr % 4 == 0:
                            pe.wait_ge(pt_sb, t * 2 - 3 + gr // 4)
                        c = v0 + 2 * VW * gr
                        rhs = vv[:, c:c + 2 * VB].rearrange("p (b w) -> p b w", b=2)[:, :, 0:SEQ] if \
                            c + 2 * VB <= VALL + SEQ else None
                        if rhs is None:
                            rhs = vv[:, c - 2 * VB + VB + SEQ:c + VB + SEQ].rearrange(
                                "p (b w) -> p b w", b=2)[:, :, VB - SEQ:VB]
                        mm = pe.matmul(ps_o[:, :, 2 * VW * gr:2 * VW * gr + SEQ], probs_t[:, j % 2, gr, :],
                                       rhs, start=True, stop=True)
                    mm.then_inc(o_ps, 1)
                if there(t - 3, TILES):
                    pe.wait_ge(ot_sb, t - 2)
                    pe.matmul(ps_y[:, 1, :], heads_t[:], wo[:], start=True, stop=True).then_inc(y_ps, 1)

        sweep(pe, step)

    @block.vector
    def _(dve):
        dve.wait_ge(w_in, 16 * 10)
        dve.wait_ge(consts, 8)

        def step(s, u):
            for j in range(QUAD):
                t = s * QUAD + j
                if there(t - 3, TILES):
                    dve.wait_ge(o_ps, t - 2)
                    if later(t - 3, 1):
                        dve.wait_ge(ot_ps, t - 3)
                    for b in range(2):
                        o = ps_o[SEQ * b:SEQ * b + SEQ, b, 0:VB].rearrange("p (h w) -> p h w", w=VW)
                        dve.reciprocal(rsum[SEQ * b:SEQ * b + SEQ, :], o[:, :, DH]).then_inc(rsum_ready, 1)
                    for b in range(2):
                        rows = slice(SEQ * b, SEQ * b + SEQ)
                        o = ps_o[rows, b, 0:VB].rearrange("p (h w) -> p h w", w=VW)
                        dve.wait_ge(rsum_ready, t * 2 - 5 + b)
                        dve.tensor_tensor(heads[rows], o[:, :, 0:DH],
                                          rsum[rows, :].unsqueeze(2).broadcast_to([SEQ, HEADS, DH]),
                                          ALU.mult).then_inc(o_sb, 1)
                if there(t - 4, TILES):
                    dve.wait_ge(y_ps, t - 3)
                    if j == 0:
                        dve.wait_ge(bo_added, s)
                    xs = x_sb[:, bass.ds(t - 4, 1), :].rearrange("p a c -> p (a c)")
                    dve.scalar_tensor_tensor(out=xs, in0=ps_y[:, 1, :], scalar=tg[:, 0:1], in1=xs,
                                             op0=ALU.mult, op1=ALU.add).then_inc(x_out, 1)
                    if j % 2:
                        for k in range(2):
                            dve.wait_ge(x_out, t - 4 + k)
                            tile = t - 5 + k
                            xs = x_sb[:, bass.ds(tile, 1), :].rearrange("p a c -> p (a c)")
                            dve.bn_stats(stats[:, bass.ds(tile, 1), :].rearrange("p a c -> p (a c)"), xs)\
                                .then_inc(stats_out, 1)
                n = s + 3
                if there(n, SUPERS) and j == 1:
                    if later(n, 1):
                        dve.wait_ge(xt_ps, n)
                    for k in range(QUAD):
                        tile = n * QUAD + k
                        xs = x_sb[:, bass.ds(tile, 1), :].rearrange("p a c -> p (a c)")
                        dve.tensor_scalar(xn[:, k, :], xs, mean[:, bass.ds(tile, 1)], rstd[:, bass.ds(tile, 1)],
                                          ALU.subtract, ALU.mult).then_inc(xn_ready, 1)
                nv = s + 1
                if there(nv, SUPERS) and j == 3:
                    for h in range(2):
                        dve.wait_ge(v_ps, nv * 2 + h + 1)
                        if later(nv, 2):
                            dve.wait_ge(o_ps, (nv - 1) * QUAD)
                        for r in range(2):
                            rows = slice(64 * r, 64 * r + 64)
                            out = vals[1 - u][rows, 4 * VB * h:4 * VB * h + 4 * VB].rearrange(
                                "p (n g w) -> p n g w", n=4, g=GROUPS)[:, :, :, VW * r:VW * r + DH]
                            src = ps_1[h][rows, :].rearrange("p (n g w) -> p n g w", n=4, g=GROUPS)
                            bias = bv[rows, :].rearrange("p (g w) -> p g w", g=GROUPS)
                            dve.tensor_tensor(out, src[:, :, :, DH * r:DH * r + DH],
                                              bias[:, :, DH * r:DH * r + DH].unsqueeze(1)
                                              .broadcast_to([64, 4, GROUPS, DH]), ALU.add).then_inc(v_sb, 1)
                if there(t, TILES):
                    dve.wait_ge(s_ps, t + 1)
                    if later(t, 4):
                        dve.wait_ge(pt_ps, t * 2 - 6)
                    for h in range(2):
                        dve.scalar_tensor_tensor(
                            out=probs[:, j, :, h, :], in0=ps_s[h][:], scalar=DH ** -0.5,
                            in1=mask[:].unsqueeze(1).broadcast_to([P, GROUPS, SEQ]),
                            op0=ALU.mult, op1=ALU.subtract).then_inc(s_sb, 1)
                    dve.wait_ge(s_sb, t * 2 + 2)
                    dve.tensor_reduce(top[:, j], probs[:, j].rearrange("p g j k -> p (g j) k"),
                                      AX_X, ALU.max).then_inc(top_ready, 1)

        sweep(dve, step)


def sweep(eng, step):
    for s in range(-2, 2):
        step(s, s % 2)
    with eng.Fori(0, (SUPERS - 4) // 2) as i:
        step(i * 2 + 2, 0)
        step(i * 2 + 3, 1)
    for s in range(SUPERS - 2, SUPERS + 2):
        step(s, s % 2)


def there(n, count):
    return not isinstance(n, int) or 0 <= n < count


def later(n, least):
    return not isinstance(n, int) or n >= least


def row(x, tile):
    return x[:, bass.ds(tile, 1), :].rearrange("p a c -> p (a c)")


def layer1_attention(nc, ctx, d, g, sb, sem):
    x_sb, ident, tg = g["x_sb"], g["ident"], g["tanh_gates"]
    stats, mean, rstd = g["stats"], g["mean"], g["rstd"]

    wq, wk, wv = (sb(f"c_w{n}", [P, DM], F32) for n in "qkv")
    bq, bk = (sb(f"c_b{n}", [P, 1], F32) for n in "qk")
    bv = sb("c_bv", [P, DM], F32)
    mask_u8 = sb("c_mask_u8", [1, SUPERS, ST], U8)
    TERMS = 65
    term_k = sb("c_term_k", [TERMS, 2, QUAD, 2, SEQ], BF16)
    term_q = sb("c_term_q", [TERMS, P], BF16)
    ctx_in = sb("c_ctx_in", [P, 2, QUAD, DM], F32)
    xn = sb("c_xn", [P, QUAD, DM], F32)
    xn_t = sb("c_xn_t", [P, ST], F32)
    ctx_t = sb("c_ctx_t", [P, ST], F32)
    qk = sb("c_qk", [P, 2, ST], F32)
    v_raw = sb("c_v_raw", [P, QUAD, DM], F32)
    vals = sb("c_vals", [P, 2, QUAD, DM], F32)
    ntop = sb("c_ntop", [P, 2, QUAD], F32)
    probs = sb("c_probs", [P, 2, QUAD, P], F32)
    rsum = sb("c_rsum", [P, 2, QUAD], F32)
    gain = sb("c_gain", [P, 2, QUAD], F32)
    probs_t = sb("c_probs_t", [P, QUAD, P], F32)

    def bank(name):
        return ctx.enter_context(nc.psum_tensor(name, [P, QUAD, P], F32))

    ps_a, ps_b, ps_v, ps_s, ps_pt, ps_o = (bank(f"c_ps_{n}") for n in ("a", "b", "v", "s", "pt", "o"))

    w_in, m_in, held, loaded, terms, mask_ready = (
        sem(f"c_{n}") for n in ("w_in", "m_in", "held", "loaded", "terms", "mask_ready"))
    xn_ready, xt_ps, ct_ps, xt_sb, ct_sb = (sem(f"c_{n}") for n in ("xn_ready", "xt_ps", "ct_ps", "xt_sb", "ct_sb"))
    q_ps, k_ps, qk_sb = (sem(f"c_{n}") for n in ("q_ps", "k_ps", "qk_sb"))
    v_ps, v_raw_sb, v_sb = (sem(f"c_{n}") for n in ("v_ps", "v_raw_sb", "v_sb"))
    s_ps, top_step, top_ready, p_ready = (sem(f"c_{n}") for n in ("s_ps", "top_step", "top_ready", "p_ready"))
    pt_ps, pt_sb, o_ps, gain_step, x_out, stats_out = (
        sem(f"c_{n}") for n in ("pt_ps", "pt_sb", "o_ps", "gain_step", "x_out", "stats_out"))

    ctx_view = d["ctx_1024"].rearrange("(a b) s c -> (b s) a c", b=2)

    def hold(eng):
        eng.sem_inc(held, 1)

    block = ctx.enter_context(nc.Block())

    @block.sync
    def _(sp):
        for dst, src in ((wq, "Wq"), (wk, "Wk"), (wv, "Wv")):
            sp.dma_start(dst[:], d["L1_xattn_" + src]).then_inc(w_in, 16)
        for dst, src in ((bq, "bq"), (bk, "bk")):
            sp.dma_start(dst[:], d["L1_xattn_" + src].rearrange("(p a) -> p a", a=1)).then_inc(w_in, 16)
        sp.dma_start(bv[:], d["L1_xattn_bv"].partition_broadcast(P)).then_inc(w_in, 16)
        sp.dma_start(mask_u8[:], d["mask_BxS2_bk1"].rearrange("(a s b) k -> a s (b k)", a=1, s=SUPERS)).then_inc(m_in, 16)

        def step(s, u):
            nxt = s + 2
            if there(nxt, SUPERS):
                if later(nxt, 1):
                    sp.wait_ge(loaded, nxt * 16)
                    hold(sp)
                if later(nxt, 2):
                    sp.wait_ge(ct_ps, nxt - 1)
                    hold(sp)
                sp.dma_start(ctx_in[:, u], ctx_view[:, bass.ds(nxt * QUAD, QUAD), :]).then_inc(loaded, 16)

        sweep(sp, step)

    @block.gpsimd
    def _(pool):
        pool.memset(term_k[:], 0.0).then_inc(terms, 1)
        pool.memset(term_q[:], 0.0).then_inc(terms, 1)
        pool.wait_ge(terms, 2)
        for u in range(2):
            pool.memset(term_k[32:33, u, :, 1, :], -1e30).then_inc(terms, 1)
            pool.memset(term_k[64:65, u, :, 0, :], -1e30).then_inc(terms, 1)
        pool.memset(term_q[0:1, :], 1.0).then_inc(terms, 1)
        pool.memset(term_q[32:33, 0:SEQ], 1.0).then_inc(terms, 1)
        pool.memset(term_q[64:65, SEQ:P], 1.0).then_inc(terms, 1)
        pool.wait_ge(m_in, 16)

        def step(s, u):
            if there(s, SUPERS):
                if later(s, 2):
                    pool.wait_ge(s_ps, s - 1)
                    hold(pool)
                pool.tensor_copy(term_k[0:1, u].rearrange("p t b k -> p (t b k)"),
                                 mask_u8[:, bass.ds(s, 1)].rearrange("p a k -> p (a k)")).then_inc(mask_ready, 1)

        sweep(pool, step)

    @block.scalar
    def _(act):
        act.wait_ge(w_in, 96)

        def step(s, u):
            n = s + 1
            if there(n, SUPERS):
                act.wait_ge(xt_ps, n + 1)
                act.activation(xn_t[:], ps_a[:].rearrange("p a b -> p (a b)"), ACT.Copy).then_inc(xt_sb, 1)
                act.wait_ge(ct_ps, n + 1)
                act.activation(ctx_t[:], ps_b[:].rearrange("p a b -> p (a b)"), ACT.Copy).then_inc(ct_sb, 1)
            if there(s - 1, SUPERS):
                act.wait_ge(pt_ps, s)
                act.activation(probs_t[:], ps_pt[:], ACT.Copy).then_inc(pt_sb, 1)
            if there(s, SUPERS):
                act.wait_ge(top_ready, s + 1)
                for k in range(QUAD):
                    act.activation(probs[:, u, k], ps_s[:, k], ACT.Exp, bias=ntop[:, u, k:k + 1],
                                   accum_out=rsum[:, u, k:k + 1]).then_inc(p_ready, 1)
            if there(n, SUPERS):
                for h, (ready, ps, bias) in enumerate(((q_ps, ps_a, bq), (k_ps, ps_b, bk))):
                    act.wait_ge(ready, n + 1)
                    act.activation(qk[:, h], ps[:].rearrange("p a b -> p (a b)"), ACT.Identity,
                                   bias=bias[:, 0:1]).then_inc(qk_sb, 1)
                act.wait_ge(v_raw_sb, n + 1)
                if later(n, 2):
                    act.wait_ge(o_ps, n - 1)
                act.activation(vals[:, 1 - u], v_raw[:], ACT.Tanh).then_inc(v_sb, 1)

        sweep(act, step)

    @block.tensor
    def _(pe):
        pe.wait_ge(w_in, 96)
        pe.wait_ge(terms, 9)

        def step(s, u):
            n = s + 1
            if there(s, SUPERS):
                pe.wait_ge(qk_sb, s * 2 + 2)
                pe.wait_ge(mask_ready, s + 1)
                if later(s, 1):
                    pe.wait_ge(p_ready, s * 4)
                for k in range(QUAD):
                    tok = slice(P * k, P * k + P)
                    pe.matmul(ps_s[:, k], qk[:, 0, tok], qk[:, 1, tok], start=True, stop=False)
                    mm = pe.matmul(ps_s[:, k], term_q[:],
                                   term_k[:, u, k].rearrange("p b k -> p (b k)"),
                                   start=False, stop=True)
                mm.then_inc(s_ps, 1)
            if there(n, SUPERS):
                pe.wait_ge(xn_ready, n * QUAD + QUAD)
                if later(n, 1):
                    pe.wait_ge(qk_sb, n * 2)
                for k in range(QUAD):
                    mm = pe.transpose(ps_a[:, k], xn[:, k], ident[:])
                mm.then_inc(xt_ps, 1)
                pe.wait_ge(loaded, n * 16 + 16)
                for k in range(QUAD):
                    mm = pe.transpose(ps_b[:, k], ctx_in[:, 1 - u, k], ident[:])
                mm.then_inc(ct_ps, 1)
            if there(s - 1, SUPERS):
                pe.wait_ge(p_ready, s * 4)
                if later(s - 1, 1):
                    pe.wait_ge(pt_sb, s - 1)
                for k in range(QUAD):
                    mm = pe.transpose(ps_pt[:, k], probs[:, 1 - u, k], ident[:])
                mm.then_inc(pt_ps, 1)
            if there(n, SUPERS):
                pe.wait_ge(xt_sb, n + 1)
                pe.matmul(ps_a[:].rearrange("p a b -> p (a b)"), wq[:], xn_t[:], start=True, stop=True)\
                    .then_inc(q_ps, 1)
                pe.wait_ge(ct_sb, n + 1)
                pe.matmul(ps_b[:].rearrange("p a b -> p (a b)"), wk[:], ctx_t[:], start=True, stop=True)\
                    .then_inc(k_ps, 1)
                if later(n, 1):
                    pe.wait_ge(v_raw_sb, n)
                for k in range(QUAD):
                    mm = pe.matmul(ps_v[:, k], ctx_t[:, P * k:P * k + P], wv[:], start=True, stop=True)
                mm.then_inc(v_ps, 1)
            if there(s - 1, SUPERS):
                pe.wait_ge(pt_sb, s)
                pe.wait_ge(v_sb, s)
                if later(s - 1, 1):
                    pe.wait_ge(x_out, s * 4 - 4)
                for k in range(QUAD):
                    mm = pe.matmul(ps_o[:, k], probs_t[:, k], vals[:, 1 - u, k], start=True, stop=True)
                mm.then_inc(o_ps, 1)

        sweep(pe, step)

    @block.vector
    def _(dve):
        dve.wait_ge(w_in, 96)

        def step(s, u):
            if there(s, SUPERS):
                dve.wait_ge(s_ps, s + 1)
                dve.tensor_reduce(ntop[:, u], ps_s[:], AX_X, ALU.max).then_inc(top_step, 1)
                dve.wait_ge(top_step, s + 1)
                dve.tensor_scalar(ntop[:, u], ntop[:, u], -1.0, None, ALU.mult).then_inc(top_ready, 1)
            n2 = s + 2
            if there(n2, SUPERS):
                if later(n2, 1):
                    dve.wait_ge(xt_ps, n2)
                for k in range(QUAD):
                    tile = n2 * QUAD + k
                    dve.tensor_scalar(xn[:, k], row(x_sb, tile), mean[:, bass.ds(tile, 1)],
                                      rstd[:, bass.ds(tile, 1)], ALU.subtract, ALU.mult).then_inc(xn_ready, 1)
            n = s + 1
            if there(n, SUPERS):
                dve.wait_ge(v_ps, n + 1)
                if later(n, 1):
                    dve.wait_ge(v_sb, n)
                dve.tensor_tensor(v_raw[:], ps_v[:], bv[:].unsqueeze(1).broadcast_to([P, QUAD, DM]), ALU.add)\
                    .then_inc(v_raw_sb, 1)
            if there(s - 1, SUPERS):
                dve.wait_ge(p_ready, s * 4)
                dve.reciprocal(gain[:, 1 - u], rsum[:, 1 - u]).then_inc(gain_step, 1)
                dve.wait_ge(gain_step, s * 2 - 1)
                dve.tensor_scalar(gain[:, 1 - u], gain[:, 1 - u], tg[:, 2:3], None, ALU.mult).then_inc(gain_step, 1)
                dve.wait_ge(gain_step, s * 2)
                dve.wait_ge(o_ps, s)
                for k in range(QUAD):
                    xs = row(x_sb, (s - 1) * QUAD + k)
                    dve.scalar_tensor_tensor(out=xs, in0=ps_o[:, k], scalar=gain[:, 1 - u, k:k + 1], in1=xs,
                                             op0=ALU.mult, op1=ALU.add).then_inc(x_out, 1)
                for k in range(QUAD):
                    dve.wait_ge(x_out, s * 4 - 3 + k)
                    tile = (s - 1) * QUAD + k
                    dve.bn_stats(row(stats, tile), row(x_sb, tile)).then_inc(stats_out, 1)
                four = bass.ds((s - 1) * QUAD, QUAD)
                for e, op in enumerate((ALU.max, ALU.min)):
                    dve.tensor_reduce(g["ext"][:, e, four], x_sb[:, four, :], AX_X, op).then_inc(stats_out, 1)

        sweep(dve, step)


MAGIC = 12582912.0
QMIN, QMAX = -128.0, 127.0
HID = 512
CHUNKS = HID // P


def layer1_ffn(nc, ctx, d, g, sb, sem):
    x_sb, ident, tg = g["x_sb"], g["ident"], g["tanh_gates"]
    mean, rstd = g["mean"], g["rstd"]

    hid = sb("d_hid", [P, SUPERS, CHUNKS, ST], F32)
    w1 = sb("d_w1", [P, CHUNKS, P], F32)
    w2 = sb("d_w2", [P, CHUNKS, P], F32)
    wq = [sb(f"d_wq{n}", [P, CHUNKS, P], BF16) for n in range(2)]
    wqt = [sb(f"d_wqt{n}", [P, CHUNKS, P], BF16) for n in range(2)]
    b1 = sb("d_b1", [P, CHUNKS], F32)
    b2 = sb("d_b2", [P, DM], F32)
    ident16 = sb("d_ident16", [P, P], BF16)
    ext = g["ext"]
    peak = sb("d_peak", [P, 4], F32)
    peaks = sb("d_peaks", [P, 4], F32)
    hpeak = sb("d_hpeak", [P, 2, SUPERS], F32)
    hp = sb("d_hp", [P, 2], F32)
    hps = sb("d_hps", [P, 2], F32)
    wscale = sb("d_wscale", [P, 2], F32)
    winv = sb("d_winv", [P, 2], F32)
    qs = [sb(f"d_qs{n}", [P, 8], F32) for n in range(2)]
    outscale = sb("d_outscale", [P, 2], F32)
    xq32 = sb("d_xq32", [P, 2, QUAD, DM], F32)
    xq = sb("d_xq", [P, QUAD, DM], BF16)
    xqt = sb("d_xqt", [P, 2, ST], BF16)
    hq = sb("d_hq", [P, 2, CHUNKS, ST], BF16)

    def qscale(dve, q, amax, namin, step, at):
        def then(ins, wait=True):
            nonlocal at
            at += 1
            ins.then_inc(step, 1)
            if wait:
                dve.wait_ge(step, at)

        then(dve.tensor_tensor(q[:, 0:1], amax, namin, ALU.add))
        then(dve.tensor_scalar(q[:, 0:1], q[:, 0:1], 1.0 / 255.0, 1e-8, ALU.mult, ALU.max))
        then(dve.reciprocal(q[:, 1:2], q[:, 0:1]))
        then(dve.tensor_scalar(q[:, 2:3], namin, q[:, 1:2], MAGIC, ALU.mult, ALU.add))
        then(dve.tensor_scalar(q[:, 3:4], q[:, 2:3], MAGIC, QMIN, ALU.subtract, ALU.add))
        then(dve.tensor_scalar(q[:, 4:5], q[:, 3:4], QMIN, QMAX, ALU.max, ALU.min))
        then(dve.tensor_scalar(q[:, 5:6], q[:, 4:5], -1.0, QMIN, ALU.mult, ALU.add))
        then(dve.memset(q[:, 7:8], MAGIC))
        then(dve.tensor_scalar(q[:, 6:7], q[:, 4:5], -1.0, QMAX + MAGIC, ALU.mult, ALU.add))
        return at

    def bank(name, dt=F32):
        return ctx.enter_context(nc.psum_tensor(name, [P, CHUNKS, P], dt))

    ps_t = bank("d_ps_t", BF16)
    ps_h = [bank(f"d_ps_h{n}") for n in range(CHUNKS)]
    ps_y = [bank(f"d_ps_y{n}") for n in range(2)]

    names = ("w_in", "held", "id16", "ext", "peak_ready", "peaks_ready", "step", "x_scale", "wq_sb", "wq32", "wt_ps", "wt_sb",
             "n_ready", "xt_ready", "q_step", "xq_ready", "xt_ps", "xt_sb", "h_ps", "h_sb", "hpeak_ready", "hp_ready", "hps_ready",
             "h_scale", "x_less", "b2_added", "t_ready", "c_ready", "hq_ready", "y_ps", "x_out", "stored")
    (w_in, held, id16, ext_ready, peak_ready, peaks_ready, qstep, x_scale, wq_sb, wq32, wt_ps, wt_sb,
     n_ready, xt_ready, q_step, xq_ready, xt_ps, xt_sb, h_ps, h_sb, hpeak_ready, hp_ready, hps_ready,
     h_scale, x_less, b2_added, t_ready, c_ready, hq_ready, y_ps, x_out, stored) = (sem("d_" + n) for n in names)

    def hold(eng):
        eng.sem_inc(held, 1)

    out_view = d["out"].rearrange("(a b) s c -> (b s) a c", b=2)
    flat_x = x_sb[:].rearrange("p t c -> p (t c)")

    def tokens(s):
        return flat_x[:, bass.ds(s * ST, ST)]

    block = ctx.enter_context(nc.Block())

    @block.sync
    def _(sp):
        sp.dma_start(w1[:], d["L1_ffn_W1"].rearrange("(a p) c -> p a c", p=P)).then_inc(w_in, 16)
        sp.dma_start(w2[:], d["L1_ffn_W2"].rearrange("c (a p) -> c a p", p=P)).then_inc(w_in, 16)
        sp.dma_start(b1[:], d["L1_ffn_b1"].rearrange("(a p) -> p a", p=P), allow_slow_non_contiguous=True).then_inc(w_in, 16)
        sp.dma_start(b2[:], d["L1_ffn_b2"].partition_broadcast(P)).then_inc(w_in, 16)
        with sp.Fori(0, SUPERS) as s:
            sp.wait_ge(x_out, s * 4 + 4)
            hold(sp)
            sp.dma_start(out_view[:, bass.ds(s * QUAD, QUAD), :], x_sb[:, bass.ds(s * QUAD, QUAD), :])\
                .then_inc(stored, 16)
        sp.wait_ge(stored, 16 * SUPERS)

    @block.gpsimd
    def _(pool):
        pool.tensor_copy(ident16[:], ident[:]).then_inc(id16, 1)
        pool.wait_ge(w_in, 64)
        pool.tensor_scalar(b2[:], b2[:], tg[:, 3:4], None, ALU.mult).then_inc(id16, 1)
        pool.wait_ge(peak_ready, 4)
        pool.partition_all_reduce(peaks[:], peak[:], P, bass.bass_isa.ReduceOp.max).then_inc(peaks_ready, 1)

        def step(s, u):
            n = s + 2
            if there(n, SUPERS):
                if later(n, 2):
                    pool.wait_ge(xq_ready, n - 1)
                four = bass.ds(n * QUAD, QUAD)
                pool.tensor_tensor(xq32[:, u], x_sb[:, four, :], mean[:, four].unsqueeze(2).broadcast_to([P, QUAD, DM]),
                                   ALU.subtract).then_inc(x_less, 1)
                pool.wait_ge(x_less, n + 1)
                pool.tensor_tensor(xq32[:, u], xq32[:, u], rstd[:, four].unsqueeze(2).broadcast_to([P, QUAD, DM]),
                                   ALU.mult).then_inc(n_ready, 1)

        sweep(pool, step)
        pool.wait_ge(hp_ready, 2)
        pool.partition_all_reduce(hps[:], hp[:], P, bass.bass_isa.ReduceOp.max).then_inc(hps_ready, 1)
        pool.wait_ge(id16, 2)
        pool.wait_ge(n_ready, SUPERS)
        with pool.Fori(0, SUPERS) as s:
            xs = x_sb[:, bass.ds(s * QUAD, QUAD), :]
            pool.tensor_tensor(xs, xs, b2[:].unsqueeze(1).broadcast_to([P, QUAD, DM]), ALU.add).then_inc(b2_added, 1)

    @block.scalar
    def _(act):
        for n in range(2):
            act.wait_ge(wt_ps, n + 1)
            act.activation(wqt[n][:], ps_t[:], ACT.Copy).then_inc(wt_sb, 1)
        act.wait_ge(x_scale, 1)

        def step(s, u):
            if there(s + 1, SUPERS):
                n = s + 1
                act.wait_ge(xt_ps, n + 1)
                if later(n, 2):
                    act.wait_ge(h_ps, n * 4 - 4)
                act.activation(xqt[:, 1 - u], ps_t[:].rearrange("p a b -> p (a b)"), ACT.Copy).then_inc(xt_sb, 1)
            if there(s, SUPERS):
                for c in range(CHUNKS):
                    act.wait_ge(h_ps, s * 4 + c + 1)
                    act.activation(hid[:, bass.ds(s, 1), c, :].rearrange("p a t -> p (a t)"),
                                   ps_h[c][:].rearrange("p a b -> p (a b)"), ACT.Gelu,
                                   bias=b1[:, c:c + 1], scale=outscale[:, 0:1]).then_inc(h_sb, 1)

            if there(s + 2, SUPERS):
                n = s + 2
                act.wait_ge(n_ready, n + 1)
                act.activation(xq32[:, u], xq32[:, u], ACT.Identity, scale=qs[0][:, 1:2], bias=qs[0][:, 7:8])\
                    .then_inc(xt_ready, 1)

        sweep(act, step)
        act.wait_ge(h_scale, 1)
        with act.Fori(0, SUPERS) as s:
            h = hid[:, bass.ds(s, 1)].rearrange("p a c t -> p (a c t)")
            act.activation(h, h, ACT.Identity, scale=qs[1][:, 1:2], bias=qs[1][:, 7:8]).then_inc(t_ready, 1)

    @block.tensor
    def _(pe):
        pe.wait_ge(id16, 1)
        for n in range(2):
            pe.wait_ge(wq_sb, n + 1)
            if n:
                pe.wait_ge(wt_sb, n)
            for c in range(CHUNKS):
                mm = pe.transpose(ps_t[:, c], wq[n][:, c], ident16[:])
            mm.then_inc(wt_ps, 1)

        pe.wait_ge(wt_sb, 2)

        def step(s, u):
            if there(s + 1, SUPERS):
                n = s + 1
                pe.wait_ge(xq_ready, n + 1)
                if later(n, 1):
                    pe.wait_ge(xt_sb, n)
                for k in range(QUAD):
                    mm = pe.transpose(ps_t[:, k], xq[:, k], ident16[:])
                mm.then_inc(xt_ps, 1)
            if there(s, SUPERS):
                pe.wait_ge(xt_sb, s + 1)
                for c in range(CHUNKS):
                    if later(s, 1):
                        pe.wait_ge(h_sb, s * 4 - 3 + c)
                    pe.matmul(ps_h[c][:].rearrange("p a b -> p (a b)"), wqt[0][:, c], xqt[:, u],
                              start=True, stop=True).then_inc(h_ps, 1)

        sweep(pe, step)

        def second(s, u):
            pe.wait_ge(hq_ready, s + 1)
            if later(s, 2):
                pe.wait_ge(x_out, s * 4 - 4)
            for k in range(QUAD):
                for c in range(CHUNKS):
                    mm = pe.matmul(ps_y[u][:, k], hq[:, u, c, P * k:P * k + P], wqt[1][:, c],
                                   start=(c == 0), stop=(c == CHUNKS - 1))
            mm.then_inc(y_ps, 1)

        for s in range(2):
            second(s, s)
        with pe.Fori(0, SUPERS // 2 - 1) as i:
            for u in range(2):
                second(i * 2 + 2 + u, u)

    @block.vector
    def _(dve):
        for e in range(2):
            dve.tensor_tensor(ext[:, e], ext[:, e], mean[:], ALU.subtract).then_inc(ext_ready, 1)
        dve.wait_ge(ext_ready, 2)
        for e in range(2):
            dve.tensor_tensor(ext[:, e], ext[:, e], rstd[:], ALU.mult).then_inc(ext_ready, 1)
        dve.wait_ge(ext_ready, 4)
        dve.tensor_scalar(ext[:, 1], ext[:, 1], -1.0, None, ALU.mult).then_inc(ext_ready, 1)
        dve.wait_ge(ext_ready, 5)
        for e in range(2):
            dve.tensor_reduce(peak[:, e:e + 1], ext[:, e], AX_X, ALU.max).then_inc(peak_ready, 1)
        dve.wait_ge(w_in, 64)
        for e, w in enumerate((w1, w2)):
            dve.tensor_reduce(peak[:, 2 + e:3 + e], w[:].rearrange("p a b -> p (a b)"), AX_X, ALU.max,
                              apply_absolute_value=True).then_inc(peak_ready, 1)
        dve.wait_ge(peaks_ready, 1)
        at = qscale(dve, qs[0], peaks[:, 0:1], peaks[:, 1:2], qstep, 0)
        dve.tensor_scalar(wscale[:], peaks[:, 2:4], 1.0 / 127.0, 1e-8, ALU.mult, ALU.max).then_inc(qstep, 1)
        dve.wait_ge(qstep, at + 1)
        dve.reciprocal(winv[:], wscale[:]).then_inc(qstep, 1)
        dve.tensor_scalar(outscale[:, 0:1], wscale[:, 0:1], qs[0][:, 0:1], None, ALU.mult).then_inc(x_scale, 1)
        dve.wait_ge(qstep, at + 2)
        at += 2
        for n, w in enumerate((w1, w2)):
            dve.tensor_scalar(w[:], w[:], winv[:, n:n + 1], MAGIC, ALU.mult, ALU.add).then_inc(wq32, 1)
            dve.wait_ge(wq32, 3 * n + 1)
            dve.tensor_scalar(w[:], w[:], MAGIC, -127.0, ALU.subtract, ALU.max).then_inc(wq32, 1)
            dve.wait_ge(wq32, 3 * n + 2)
            dve.tensor_scalar(wq[n][:], w[:], 127.0, None, ALU.min).then_inc(wq_sb, 1)
            dve.sem_inc(wq32, 1)

        def step(s, u):
            n = s + 1
            if there(n, SUPERS):
                dve.wait_ge(xt_ready, n + 1)
                if later(n, 1):
                    dve.wait_ge(xt_ps, n)
                dve.tensor_scalar(xq[:], xq32[:, 1 - u], qs[0][:, 6:7], MAGIC, ALU.min, ALU.subtract).then_inc(q_step, 1)
                dve.wait_ge(q_step, n + 1)
                dve.tensor_scalar(xq[:], xq[:], qs[0][:, 5:6], None, ALU.max).then_inc(xq_ready, 1)
            p = s - 1
            if there(p, SUPERS):
                dve.wait_ge(h_sb, p * 4 + 4)
                h = hid[:, bass.ds(p, 1)].rearrange("p a c t -> p (a c t)")
                for e, op in enumerate((ALU.max, ALU.min)):
                    dve.tensor_reduce(hpeak[:, e, bass.ds(p, 1)], h, AX_X, op).then_inc(hpeak_ready, 1)

        sweep(dve, step)
        dve.wait_ge(hpeak_ready, 2 * SUPERS)
        dve.tensor_reduce(hp[:, 0:1], hpeak[:, 0], AX_X, ALU.max).then_inc(hp_ready, 1)
        dve.tensor_reduce(hp[:, 1:2], hpeak[:, 1], AX_X, ALU.min).then_inc(hpeak_ready, 1)
        dve.wait_ge(hpeak_ready, 2 * SUPERS + 1)
        dve.tensor_scalar(hp[:, 1:2], hp[:, 1:2], -1.0, None, ALU.mult).then_inc(hp_ready, 1)
        dve.wait_ge(hps_ready, 1)
        at = qscale(dve, qs[1], hps[:, 0:1], hps[:, 1:2], qstep, at)
        dve.sem_inc(h_scale, 1)
        dve.tensor_scalar(outscale[:, 1:2], wscale[:, 1:2], qs[1][:, 0:1], tg[:, 3:4], ALU.mult, ALU.mult)\
            .then_inc(qstep, 1)
        dve.wait_ge(qstep, at + 1)

        def second(s, u):
            dve.wait_ge(t_ready, s + 1)
            h = hid[:, bass.ds(s, 1)].rearrange("p a c t -> p (a c t)")
            if later(s, 2):
                dve.wait_ge(y_ps, s - 1)
            q = hq[:, u].rearrange("p c t -> p (c t)")
            dve.tensor_scalar(q, h, qs[1][:, 6:7], MAGIC, ALU.min, ALU.subtract).then_inc(c_ready, 1)
            dve.wait_ge(c_ready, s + 1)
            dve.tensor_scalar(q, q, qs[1][:, 5:6], None, ALU.max).then_inc(hq_ready, 1)

        def finish(s, u):
            dve.wait_ge(y_ps, s + 1)
            dve.wait_ge(b2_added, s + 1)
            for k in range(QUAD):
                xs = row(x_sb, s * QUAD + k)
                dve.scalar_tensor_tensor(out=xs, in0=ps_y[u][:, k], scalar=outscale[:, 1:2], in1=xs,
                                         op0=ALU.mult, op1=ALU.add).then_inc(x_out, 1)

        second(0, 0)
        second(1, 1)
        finish(0, 0)
        with dve.Fori(0, SUPERS // 2 - 1) as i:
            second(i * 2 + 2, 0)
            finish(i * 2 + 1, 1)
            second(i * 2 + 3, 1)
            finish(i * 2 + 2, 0)
        finish(SUPERS - 1, 1)


EXPERTS = 8
RT = ST
REGION = NTOK + RT
ETILES = (2 * NTOK + EXPERTS * (RT - 1)) // RT
RW = DM + 4
SPARE = ETILES - 2 * NTOK // RT
PADDED = EXPERTS + SPARE


def mixture(nc, ctx, d, g, sb, sem):
    tokens_to = nc.dram_tensor("m_rows", (EXPERTS * REGION + SPARE * RT, RW), F32, kind="Internal").ap()
    results = nc.dram_tensor("m_results", (2 * NTOK + PADDED * RT, DM), F32, kind="Internal").ap()
    wall = sb("m_wall", [P, EXPERTS, 4, HID], F32R)
    ball = sb("m_ball", [P, EXPERTS, CHUNKS + 1], F32)
    tables = sb("m_tables", [1, 2, ETILES], U32)
    ends = sb("m_ends", [1, EXPERTS], U32)
    with ExitStack() as inner:
        route(nc, inner, d, g, sem, tokens_to, wall, ball, tables, ends)
    with ExitStack() as inner:
        experts(nc, inner, d, g, sem, tokens_to, results, wall, ball, tables)
    with ExitStack() as inner:
        gather(nc, inner, d, g, sem, results)


def route(nc, ctx, d, g, sem, tokens_to, wall, ball, tables, ends):
    x_sb, ident, tg, mean, rstd = g["x_sb"], g["ident"], g["tanh_gates"], g["mean"], g["rstd"]

    def sb(name, shape, dt):
        return ctx.enter_context(nc.sbuf_tensor(name, shape, dt))

    CT = 2 * QUAD
    NCH = TILES // CT
    rows = sb("r_rows", [P, TILES, 2, RW], F32)
    xn = sb("r_xn", [P, 2, CT, DM], F32)
    xn_t = sb("r_xn_t", [P, 2, QUAD, P], F32)
    rw = sb("r_rw", [EXPERTS, DM], F32)
    rw_t = sb("r_rw_t", [P, EXPERTS], F32)
    raw = sb("r_raw", [P, 2, 2, HID], F32)
    bias_rows = sb("r_bias_rows", [EXPERTS * (CHUNKS + 1), P], F32)
    TE = [P, CT, EXPERTS]
    logits, work, first, second = (sb(f"r_{n}", TE, F32) for n in ("logits", "work", "first", "second"))
    chosen = sb("r_chosen", TE, BF16)
    order = sb("r_order", TE, F32)
    top = sb("r_top", [P, 2, CT], F32)
    pick = sb("r_pick", [P, CT], F32)
    gate = sb("r_gate", [P, 2, CT], F32)
    place = sb("r_place", [P, 2, CT], F32)
    place_u = sb("r_place_u", [P, 2, TILES], U32)
    before = sb("r_before", [P, P], BF16)
    ones = sb("r_ones", [P, P], BF16)
    total = sb("r_total", [P, EXPERTS, CT], F32)
    upto = sb("r_upto", [P, EXPERTS, CT], F32)
    resets = sb("r_resets", [P, EXPERTS, CT], F32)
    base = sb("r_base", [P, EXPERTS], F32)
    end = sb("r_end", [P, EXPERTS], F32)
    count = sb("r_count", [P, EXPERTS], F32)
    ntile = sb("r_ntile", [P, EXPERTS], F32)
    tile_end = sb("r_tile_end", [P, EXPERTS], F32)
    tnum = sb("r_tnum", [P, ETILES], F32)
    trow = sb("r_trow", [P, ETILES], F32)
    texp = sb("r_texp", [P, ETILES], F32)
    past = sb("r_past", [P, ETILES], F32)
    skip = sb("r_skip", [P, EXPERTS], F32)
    PADS = SPARE + 1
    pad = sb("r_pad", [P, PADS, RT // P, RW], F32)

    def bank(name, shape, dt=F32):
        return ctx.enter_context(nc.psum_tensor(name, shape, dt))

    ps_t = [bank(f"r_ps_t{n}", [P, QUAD, P]) for n in range(2)]
    ps_l = [bank(f"r_ps_l{n}", [P, CT, 64]) for n in range(2)]
    ps_c = bank("r_ps_c", [P, CT, 64])
    ps_n = bank("r_ps_n", [P, CT, 64])
    ps_w = bank("r_ps_w", [P, 4, P])

    names = ("w_in", "b_in", "xn_ready", "xt_ps", "xt_sb", "copied", "l_ps", "rwt_ps", "rwt_sb", "bias_ps",
             "bias_sb", "raw_in", "hi", "lo", "consts", "step", "diff", "ratio", "chosen", "cn_ps", "tables_ready",
             "ids", "place_ready", "sent", "padded", "held", "pad_ready", "spare_out")
    (w_in, b_in, xn_ready, xt_ps, xt_sb, copied, l_ps, rwt_ps, rwt_sb, bias_ps,
     bias_sb, raw_in, hi_done, lo_done, consts, step_done, diff, ratio, chosen_ready, cn_ps, tables_ready,
     ids, place_ready, sent, padded, held, pad_ready, spare_out) = (sem("r_" + n) for n in names)

    def hold(eng):
        eng.sem_inc(held, 1)

    def chunks(eng, step):
        step(-1, 1)
        step(0, 0)
        with eng.Fori(0, (NCH - 2) // 2) as i:
            step(i * 2 + 1, 1)
            step(i * 2 + 2, 0)
        step(NCH - 1, 1)

    with nc.Block() as block:
        @block.sync
        def _(sp):
            sp.dma_start(rw[:], d["L0_ffn_router_w"]).then_inc(w_in, 16)
            sp.dma_start(bias_rows[0:EXPERTS * CHUNKS, :], d["L0_ffn_b_fc"].rearrange("e (a p) -> (e a) p", p=P))\
                .then_inc(b_in, 16)
            sp.dma_start(bias_rows[EXPERTS * CHUNKS:, :], d["L0_ffn_b_proj"]).then_inc(b_in, 16)
            def raw_weights(e):
                if e >= 1:
                    sp.wait_ge(raw_in, 32 * e)
                if e >= 2:
                    sp.wait_ge(lo_done, e - 1)
                sp.dma_start(raw[:, e % 2, 0], d["L0_ffn_w_fc"][e]).then_inc(raw_in, 16)
                sp.dma_start(raw[:, e % 2, 1].rearrange("p (a c) -> p a c", c=DM),
                             d["L0_ffn_w_proj"][e].rearrange("(a p) c -> p a c", p=P)).then_inc(raw_in, 16)

            def padding(n, first):
                if n >= PADS:
                    sp.wait_ge(pad_ready, n - PADS + 1)
                else:
                    sp.wait_ge(consts, 5)
                sp.dma_start(tokens_to[bass.ds(first, RT), :].rearrange("(p r) w -> p r w", p=P), pad[:, n % PADS])\
                    .then_inc(spare_out if n < SPARE else padded, 16)

            for e in range(2):
                raw_weights(e)
            for n in range(SPARE):
                padding(n, EXPERTS * REGION + n * RT)
            sp.wait_ge(tables_ready, 3)
            for e in range(EXPERTS):
                padding(SPARE + e, sp.value_load(ends[0:1, e:e + 1], min_val=e * REGION, max_val=e * REGION + NTOK))
            for e in range(2, EXPERTS):
                raw_weights(e)
            sp.wait_ge(spare_out, 16 * SPARE)
            sp.wait_ge(padded, 16 * EXPERTS)

        @block.gpsimd
        def _(pool):
            pool.memset(before[:], 1.0).then_inc(consts, 1)
            pool.memset(ones[:], 1.0).then_inc(consts, 1)
            pool.memset(pad[:], 0.0).then_inc(consts, 1)
            pool.wait_ge(consts, 3)
            pool.affine_select(out=before[:], in_=before[:], compare_op=ALU.is_gt, fill=0.0, base=0,
                               pattern=[[1, P]], channel_multiplier=-1).then_inc(consts, 1)
            pool.iota(pad[:, :, :, DM], pattern=[[RT, PADS], [1, RT // P]], base=2 * NTOK, channel_multiplier=RT // P,
                      allow_small_or_imprecise_dtypes=True).then_inc(consts, 1)
            pool.iota(order[:], pattern=[[0, CT], [-1, EXPERTS]], base=EXPERTS, channel_multiplier=0,
                      allow_small_or_imprecise_dtypes=True).then_inc(consts, 1)
            pool.iota(tnum[:], pattern=[[1, ETILES]], base=0, channel_multiplier=0,
                      allow_small_or_imprecise_dtypes=True).then_inc(consts, 1)
            pool.iota(base[:], pattern=[[REGION, EXPERTS]], base=0, channel_multiplier=0,
                      allow_small_or_imprecise_dtypes=True).then_inc(consts, 1)
            for k in range(2):
                pool.iota(rows[:, :, k, DM], pattern=[[2 * P, TILES]], base=k, channel_multiplier=2,
                          allow_small_or_imprecise_dtypes=True).then_inc(ids, 1)
                pool.memset(rows[:, :, k, DM + 2:RW], 0.0).then_inc(ids, 1)
            pool.wait_ge(ids, 4)
            for t in range(TILES):
                if t % CT == 0:
                    pool.wait_ge(copied, t // CT + 1)
                    pool.wait_ge(place_ready, (t // CT + 1) * 2)
                for k in range(2):
                    pool.indirect_dma_start(
                        tokens_to, bass.IndirectOffsetOnAxis(ap=place_u[:, k, t:t + 1], axis=0),
                        rows[:, t, k, :], None).then_inc(sent, 16)
            pool.wait_ge(sent, 32 * TILES)

        @block.scalar
        def _(act):
            act.wait_ge(rwt_ps, 1)
            act.activation(rw_t[:], ps_w[:, 0, 0:EXPERTS], ACT.Copy).then_inc(rwt_sb, 1)
            act.wait_ge(bias_ps, 1)
            act.activation(ball[:, :, 0:CHUNKS], ps_w[:, 1, 0:EXPERTS * CHUNKS].rearrange("p (e a) -> p e a", e=EXPERTS),
                           ACT.Copy).then_inc(bias_sb, 1)
            act.activation(ball[:, :, CHUNKS], ps_w[:, 1, EXPERTS * CHUNKS:EXPERTS * (CHUNKS + 1)], ACT.Copy)\
                .then_inc(bias_sb, 1)

            def step(c, u):
                n = c + 1
                if there(n, NCH):
                    for half in range(2):
                        act.wait_ge(xt_ps, n * 2 + half + 1)
                        act.activation(xn_t[:, half], ps_t[half][:], ACT.Copy).then_inc(xt_sb, 1)
                if there(c, NCH):
                    act.wait_ge(diff, c + 1)
                    act.activation(gate[:, 1], pick[:], ACT.Exp).then_inc(ratio, 1)
                if there(n, NCH):
                    act.wait_ge(xn_ready, n * CT + CT)
                    act.activation(rows[:, bass.ds(n * CT, CT), :, 0:DM],
                                   xn[:, 1 - u].unsqueeze(2).broadcast_to([P, CT, 2, DM]), ACT.Copy)\
                        .then_inc(copied, 1)

            chunks(act, step)
            for e in range(EXPERTS):
                act.wait_ge(raw_in, 32 * e + 32)
                for k in range(2):
                    act.activation(wall[:, e, 2 * k], raw[:, e % 2, k], ACT.Copy).then_inc(hi_done, 1)

        @block.tensor
        def _(pe):
            pe.wait_ge(w_in, 16)
            pe.transpose(ps_w[:, 0, 0:EXPERTS], rw[:], ident[0:EXPERTS, 0:EXPERTS]).then_inc(rwt_ps, 1)
            pe.wait_ge(b_in, 32)
            pe.wait_ge(rwt_sb, 1)
            n = EXPERTS * (CHUNKS + 1)
            pe.transpose(ps_w[:, 1, 0:n], bias_rows[:], ident[0:n, 0:n]).then_inc(bias_ps, 1)

            pe.wait_ge(consts, 4)

            def step(c, u):
                n = c + 1
                if there(n, NCH):
                    for half in range(2):
                        pe.wait_ge(xn_ready, n * CT + QUAD * half + QUAD)
                        if later(n, 1):
                            pe.wait_ge(xt_sb, n * 2 + half - 1)
                        for k in range(QUAD):
                            mm = pe.transpose(ps_t[half][:, k], xn[:, 1 - u, QUAD * half + k], ident[:])
                        mm.then_inc(xt_ps, 1)
                    for half in range(2):
                        pe.wait_ge(xt_sb, n * 2 + half + 1)
                        for k in range(QUAD):
                            mm = pe.matmul(ps_l[1 - u][:, QUAD * half + k, 0:EXPERTS], xn_t[:, half, k], rw_t[:],
                                           start=True, stop=True)
                    mm.then_inc(l_ps, 1)
                if there(c, NCH):
                    pe.wait_ge(chosen_ready, c + 1)
                    hold(pe)
                    for ps, sums in ((ps_c, before), (ps_n, ones)):
                        pe.matmul(ps[:, 0:1, :].rearrange("p a b -> p (a b)"), sums[:],
                                  chosen[:].rearrange("p t e -> p (t e)"), start=True, stop=True).then_inc(cn_ps, 1)

            chunks(pe, step)

        @block.vector
        def _(dve):
            STEPS = 31

            def wide(x):
                return x.unsqueeze(2).broadcast_to(TE)

            def step(c, u):
                n = c + 1
                if there(n, NCH):
                    if later(n, 2):
                        dve.wait_ge(xt_ps, n * 2 - 2)
                        dve.wait_ge(copied, n - 1)
                    for k in range(CT):
                        tile = n * CT + k
                        dve.tensor_scalar(xn[:, 1 - u, k], row(x_sb, tile), mean[:, bass.ds(tile, 1)],
                                          rstd[:, bass.ds(tile, 1)], ALU.subtract, ALU.mult).then_inc(xn_ready, 1)
                if not there(c, NCH):
                    return
                at = 0

                def then(ins):
                    nonlocal at
                    at += 1
                    ins.then_inc(step_done, 1)
                    dve.wait_ge(step_done, c * STEPS + at)
                    hold(dve)

                dve.wait_ge(l_ps, c + 1)
                hold(dve)
                then(dve.tensor_copy(logits[:], ps_l[u][:, :, 0:EXPERTS]))
                for k, (src, hot) in enumerate(((logits, first), (work, second))):
                    then(dve.tensor_reduce(top[:, k], src[:], AX_X, ALU.max))
                    then(dve.tensor_tensor(hot[:], src[:], wide(top[:, k]), ALU.is_equal))
                    then(dve.tensor_tensor(hot[:], hot[:], order[:], ALU.mult))
                    then(dve.tensor_reduce(pick[:], hot[:], AX_X, ALU.max))
                    then(dve.tensor_tensor(hot[:], order[:], wide(pick[:]), ALU.is_equal))
                    if k == 0:
                        then(dve.scalar_tensor_tensor(out=work[:], in0=first[:], scalar=-FMAX, in1=logits[:],
                                                      op0=ALU.mult, op1=ALU.add))
                then(dve.tensor_tensor(chosen[:], first[:], second[:], ALU.add))
                dve.sem_inc(chosen_ready, 1)
                dve.tensor_tensor(pick[:], top[:, 1], top[:, 0], ALU.subtract).then_inc(diff, 1)
                dve.wait_ge(cn_ps, c * 2 + 2)
                hold(dve)
                counts = [ps[:, 0:1, :].rearrange("p a (t e) -> p (a t) e", e=EXPERTS) for ps in (ps_c, ps_n)]
                then(dve.tensor_copy(total[:].rearrange("p e t -> p t e"), counts[1]))
                then(dve.tensor_tensor_scan(upto[:].rearrange("p e t -> p (e t)"), resets[:].rearrange("p e t -> p (e t)"),
                                            total[:].rearrange("p e t -> p (e t)"), 0.0, ALU.mult, ALU.add))
                then(dve.tensor_tensor(upto[:], upto[:], wide_e(end[:]), ALU.add))
                then(dve.tensor_copy(end[:], upto[:, :, CT - 1]))
                then(dve.tensor_tensor(upto[:], upto[:], total[:], ALU.subtract))
                then(dve.tensor_tensor(work[:], counts[0], upto[:].rearrange("p e t -> p t e"), ALU.add))
                dve.wait_ge(ratio, c + 1)
                hold(dve)
                then(dve.tensor_scalar(gate[:, 0], gate[:, 1], 1.0, None, ALU.add))
                then(dve.reciprocal(gate[:, 0], gate[:, 0]))
                then(dve.tensor_scalar(gate[:, 0], gate[:, 0], tg[:, 1:2], None, ALU.mult))
                then(dve.tensor_tensor(gate[:, 1], gate[:, 1], gate[:, 0], ALU.mult))
                for k, hot in enumerate((first, second)):
                    then(dve.tensor_copy(rows[:, bass.ds(c * CT, CT), k, DM + 1], gate[:, k]))
                    then(dve.tensor_tensor(hot[:], hot[:], work[:], ALU.mult))
                    then(dve.tensor_reduce(place[:, k], hot[:], AX_X, ALU.add))
                    then(dve.tensor_copy(place_u[:, k, bass.ds(c * CT, CT)], place[:, k]))
                    dve.sem_inc(place_ready, 1)
                assert at == STEPS, at

            def wide_e(x):
                return x.unsqueeze(2).broadcast_to([P, EXPERTS, CT])

            dve.wait_ge(consts, 8)
            dve.wait_ge(ids, 4)
            dve.memset(resets[:], 1.0).then_inc(consts, 1)
            dve.wait_ge(consts, 9)
            dve.memset(resets[:, :, 0], 0.0).then_inc(consts, 1)
            dve.tensor_copy(end[:], base[:]).then_inc(consts, 1)
            dve.wait_ge(consts, 11)
            chunks(dve, step)

            at = NCH * STEPS

            def then(ins):
                nonlocal at
                at += 1
                ins.then_inc(step_done, 1)
                dve.wait_ge(step_done, at)

            then(dve.tensor_tensor(count[:], end[:], base[:], ALU.subtract))
            then(dve.tensor_scalar(ntile[:], count[:], 1.0 / RT, (RT - 1.0) / RT - 0.5 + 0.5 / RT, ALU.mult, ALU.add))
            then(dve.tensor_scalar(ntile[:], ntile[:], MAGIC, MAGIC, ALU.add, ALU.subtract))
            then(dve.memset(skip[:], 1.0))
            then(dve.tensor_tensor_scan(tile_end[:], skip[:], ntile[:], 0.0, ALU.mult, ALU.add))
            then(dve.tensor_scalar(skip[:], ntile[:], -float(RT), float(REGION), ALU.mult, ALU.add))
            then(dve.tensor_scalar(trow[:], tnum[:], float(RT), None, ALU.mult))
            then(dve.memset(texp[:], 0.0))
            for e in range(EXPERTS):
                then(dve.tensor_scalar(past[:], tnum[:], tile_end[:, e:e + 1], None, ALU.is_ge))
                then(dve.scalar_tensor_tensor(out=trow[:], in0=past[:], scalar=skip[:, e:e + 1], in1=trow[:],
                                              op0=ALU.mult, op1=ALU.add))
                then(dve.tensor_tensor(texp[:], texp[:], past[:], ALU.add))
            then(dve.tensor_scalar(texp[:], texp[:], EXPERTS - 1.0, None, ALU.min))
            dve.tensor_copy(tables[0:1, 0], trow[0:1, :]).then_inc(tables_ready, 1)
            dve.tensor_copy(tables[0:1, 1], texp[0:1, :]).then_inc(tables_ready, 1)
            dve.tensor_copy(ends[:], end[0:1, :]).then_inc(tables_ready, 1)
            dve.wait_ge(spare_out, 16 * SPARE)
            for n in range(PADS, PADDED):
                dve.tensor_scalar(pad[:, n - PADS, :, DM], pad[:, n - PADS, :, DM], float(PADS * RT), None, ALU.add)\
                    .then_inc(pad_ready, 1)
            for e in range(EXPERTS):
                dve.wait_ge(hi_done, 2 * e + 2)
                dve.tensor_tensor(wall[:, e].rearrange("p (k w) n -> p k w n", w=2)[:, :, 1], raw[:, e % 2],
                                  wall[:, e].bitcast(F32).rearrange("p (k w) n -> p k w n", w=2)[:, :, 0],
                                  ALU.subtract).then_inc(lo_done, 1)


def experts(nc, ctx, d, g, sem, tokens_to, results, wall, ball, tables):
    ident = g["ident"]

    def sb(name, shape, dt):
        return ctx.enter_context(nc.sbuf_tensor(name, shape, dt))

    NR = RT // P
    w_up = sb("e_w_up", [P, 2, 2, HID], F32R)
    w_down = sb("e_w_down", [P, 2, 2, HID], F32R)
    b_up = sb("e_b_up", [P, 2, CHUNKS], F32)
    b_down = sb("e_b_down", [P, 2, 1], F32)
    rows_in = sb("e_rows", [P, 2, NR, RW], F32)
    xt = sb("e_xt", [P, 2, 2, RT], F32R)
    h = sb("e_h", [P, 2, RT], F32)
    hp = sb("e_hp", [P, CHUNKS, 2, RT], F32R)
    yt = sb("e_yt", [P, RT], F32)
    y = sb("e_y", [P, 2, NR, DM], F32)
    to = sb("e_to", [P, 2, NR], U32)
    to_all = sb("e_to_all", [P, ETILES, NR], U32)
    weight = sb("e_weight", [P, ETILES, NR], F32)

    ps_x = ctx.enter_context(nc.psum_tensor("e_ps_x", [P, NR, P], F32))
    ps_h = [ctx.enter_context(nc.psum_tensor(f"e_ps_h{n}", [P, RT], F32)) for n in range(2)]
    ps_y = [ctx.enter_context(nc.psum_tensor(f"e_ps_y{n}", [P, RT], F32)) for n in range(2)]
    ps_r = ctx.enter_context(nc.psum_tensor("e_ps_r", [P, NR, P], F32))

    names = ("held", "up_in", "down_in", "rows_in", "xt_ps", "xt_hi", "xt_lo", "h_ps", "h_sb", "h_hi", "h_lo", "h_used",
             "meta_ready", "yt_sb", "yr_ps", "to_ready", "y_sb")
    (held, up_in, down_in, r_in, xt_ps, xt_hi, xt_lo, h_ps, h_sb, h_hi, h_lo, h_used,
     meta_ready, yt_sb, yr_ps, to_ready, y_sb) = (sem("e_" + n) for n in names)
    sent = [sem(f"e_sent{v}") for v in range(2)]

    def hold(eng):
        eng.sem_inc(held, 1)

    def tiles(eng, step):
        for t in range(-3, 4):
            step(t, t % 2)
        pairs = (ETILES - 7) // 2
        with eng.Fori(0, pairs) as i:
            step(i * 2 + 4, 0)
            step(i * 2 + 5, 1)
        for t in range(4 + 2 * pairs, ETILES + 1):
            step(t, t % 2)

    with nc.Block() as block:
        @block.sync
        def _(sp):
            def step(t, u):
                n = t + 3
                if there(n, ETILES):
                    if later(n, 1):
                        sp.wait_ge(r_in, n * 16)
                        hold(sp)
                    if later(n, 2):
                        sp.wait_ge(xt_ps, n - 1)
                        hold(sp)
                        sp.wait_ge(meta_ready, n * 2 - 2)
                        hold(sp)
                    first = sp.value_load(tables[0:1, 0, bass.ds(n, 1)], min_val=0,
                                          max_val=EXPERTS * REGION + (SPARE - 1) * RT)
                    sp.dma_start(rows_in[:, 1 - u], tokens_to[bass.ds(first, RT), :]
                                 .rearrange("(p r) w -> p r w", p=P)).then_inc(r_in, 16)
                n = t + 2
                if there(n, ETILES):
                    if later(n, 1):
                        sp.wait_ge(up_in, n * 32)
                        hold(sp)
                    if later(n, 2):
                        sp.wait_ge(h_sb, n * 4 - 4)
                        hold(sp)
                    expert = sp.value_load(tables[0:1, 1, bass.ds(n, 1)], min_val=0, max_val=EXPERTS - 1)
                    sp.dma_start(w_up[:, u].bitcast(F32),
                                 wall[:, bass.ds(expert, 1), 0:2].rearrange("p a k n -> p (a k) n").bitcast(F32))\
                        .then_inc(up_in, 16)
                    sp.dma_start(b_up[:, u], ball[:, bass.ds(expert, 1), 0:CHUNKS].rearrange("p a k -> p (a k)"))\
                        .then_inc(up_in, 16)
                n = t + 1
                if there(n, ETILES):
                    v = 1 - u
                    if later(n, 1):
                        sp.wait_ge(down_in, n * 32)
                        hold(sp)
                    if later(n, 2):
                        sp.wait_ge(yt_sb, n - 1)
                        hold(sp)
                    expert = sp.value_load(tables[0:1, 1, bass.ds(n, 1)], min_val=0, max_val=EXPERTS - 1)
                    sp.dma_start(w_down[:, v].bitcast(F32),
                                 wall[:, bass.ds(expert, 1), 2:4].rearrange("p a k n -> p (a k) n").bitcast(F32))\
                        .then_inc(down_in, 16)
                    sp.dma_start(b_down[:, v], ball[:, bass.ds(expert, 1), CHUNKS:].rearrange("p a k -> p (a k)"))\
                        .then_inc(down_in, 16)

            tiles(sp, step)

        @block.gpsimd
        def _(pool):
            def step(t, u):
                n = t - 1
                if there(n, ETILES):
                    v = 1 - u
                    pool.wait_ge(meta_ready, n * 2 + 2)
                    if later(n, 2):
                        pool.wait_ge(sent[v], (n - v) * 32)
                    hold(pool)
                    pool.tensor_copy(to[:, v], to_all[:, bass.ds(n, 1)].rearrange("p a r -> p (a r)"))\
                        .then_inc(to_ready, 1)
                    pool.wait_ge(to_ready, n + 1)
                    for r in range(NR):
                        pool.wait_ge(y_sb, n * NR + r + 1)
                        hold(pool)
                        pool.indirect_dma_start(
                            results, bass.IndirectOffsetOnAxis(ap=to[:, v, r:r + 1], axis=0),
                            y[:, v, r], None).then_inc(sent[v], 16)

            tiles(pool, step)
            for v in range(2):
                pool.wait_ge(sent[v], 16 * NR * ((ETILES + 1 - v) // 2))

        @block.scalar
        def _(act):
            def step(t, u):
                n, m = t + 1, t + 2

                def gelu(c):
                    act.wait_ge(h_ps, n * 4 + c + 1)
                    if c >= 2 or later(n, 1):
                        act.wait_ge(h_lo, n * 4 + c - 1)
                    act.activation(h[:, c % 2], ps_h[c % 2][:], ACT.Gelu_apprx_tanh,
                                   bias=b_up[:, 1 - u, c:c + 1]).then_inc(h_sb, 1)

                if there(t - 1, ETILES):
                    v = 1 - u
                    act.wait_ge(h_used, t * 4)
                    if later(t - 1, 1):
                        act.wait_ge(yr_ps, t - 1)
                    act.activation(yt[:], ps_y[v][:], ACT.Identity, bias=b_down[:, v]).then_inc(yt_sb, 1)
                if there(n, ETILES):
                    act.wait_ge(up_in, n * 32 + 32)
                    gelu(0)
                if there(m, ETILES):
                    act.wait_ge(xt_ps, m + 1)
                    if later(m, 2):
                        act.wait_ge(h_ps, m * 4 - 4)
                    act.activation(xt[:, u, 0], ps_x[:].rearrange("p r t -> p (r t)"), ACT.Copy).then_inc(xt_hi, 1)
                if there(n, ETILES):
                    gelu(1)
                if there(t - 1, ETILES):
                    if later(t - 1, 2):
                        act.wait_ge(sent[v], (t - 1 - v) * 32)
                    act.wait_ge(meta_ready, t * 2)
                    act.wait_ge(yr_ps, t)
                    for r in range(NR):
                        act.activation(y[:, v, r], ps_r[:, r], ACT.Copy,
                                       scale=weight[:, bass.ds(t - 1, 1), r]).then_inc(y_sb, 1)
                if there(n, ETILES):
                    gelu(2)
                    gelu(3)

            tiles(act, step)

        @block.tensor
        def _(pe):
            def step(t, u):
                n, m = t + 1, t + 2

                def up(c):
                    v = 1 - u
                    if c == 0:
                        pe.wait_ge(up_in, n * 32 + 32)
                        pe.wait_ge(xt_hi, n + 1)
                    if later(n, 1) or c >= 2:
                        pe.wait_ge(h_sb, n * 4 + c - 1)
                    at = slice(P * c, P * c + P)
                    pe.matmul(ps_h[c % 2][:], w_up[:, v, 0, at], xt[:, v, 0], start=True, stop=False)
                    pe.matmul(ps_h[c % 2][:], w_up[:, v, 1, at], xt[:, v, 0], start=False, stop=False)
                    if c == 0:
                        pe.wait_ge(xt_lo, n + 1)
                    pe.matmul(ps_h[c % 2][:], w_up[:, v, 0, at], xt[:, v, 1], start=False, stop=True).then_inc(h_ps, 1)

                def down(c):
                    if c == 0:
                        pe.wait_ge(down_in, t * 32 + 32)
                        if later(t, 2):
                            pe.wait_ge(yt_sb, t - 1)
                    pe.wait_ge(h_lo, t * 4 + c + 1)
                    at = slice(P * c, P * c + P)
                    pe.matmul(ps_y[u][:], w_down[:, u, 0, at], hp[:, c, 0], start=(c == 0), stop=False)
                    pe.matmul(ps_y[u][:], w_down[:, u, 1, at], hp[:, c, 0], start=False, stop=False)
                    pe.matmul(ps_y[u][:], w_down[:, u, 0, at], hp[:, c, 1], start=False, stop=(c == CHUNKS - 1))\
                        .then_inc(h_used, 1)

                for c in range(CHUNKS):
                    if there(n, ETILES):
                        up(c)
                    if there(t, ETILES):
                        down(c)
                    if c == 0:
                        if there(m, ETILES):
                            pe.wait_ge(r_in, m * 16 + 16)
                            if later(m, 1):
                                pe.wait_ge(xt_lo, m)
                            for r in range(NR):
                                mm = pe.transpose(ps_x[:, r], rows_in[:, u, r, 0:DM], ident[:])
                            mm.then_inc(xt_ps, 1)
                        if there(t - 1, ETILES):
                            pe.wait_ge(yt_sb, t)
                            if later(t - 1, 1):
                                pe.wait_ge(y_sb, t * 4 - 4)
                            for r in range(NR):
                                mm = pe.transpose(ps_r[:, r], yt[:, P * r:P * r + P], ident[:])
                            mm.then_inc(yr_ps, 1)

            tiles(pe, step)

        @block.vector
        def _(dve):
            def step(t, u):
                n, m = t + 1, t + 2

                def split(c):
                    dve.wait_ge(h_sb, n * 4 + c + 1)
                    if later(n, 1):
                        dve.wait_ge(h_used, t * 4 + c + 1)
                    dve.tensor_copy(hp[:, c, 0], h[:, c % 2]).then_inc(h_hi, 1)
                    dve.wait_ge(h_hi, n * 4 + c + 1)
                    dve.tensor_tensor(hp[:, c, 1], h[:, c % 2], hp[:, c, 0].bitcast(F32),
                                      ALU.subtract).then_inc(h_lo, 1)

                if there(n, ETILES):
                    split(0)
                if there(m, ETILES):
                    dve.wait_ge(r_in, m * 16 + 16)
                    hold(dve)
                    dve.tensor_copy(to_all[:, bass.ds(m, 1)].rearrange("p a r -> p (a r)"), rows_in[:, u, :, DM])\
                        .then_inc(meta_ready, 1)
                    dve.tensor_copy(weight[:, bass.ds(m, 1)].rearrange("p a r -> p (a r)"),
                                    rows_in[:, u, :, DM + 1]).then_inc(meta_ready, 1)
                    dve.wait_ge(xt_hi, m + 1)
                    if later(m, 2):
                        dve.wait_ge(h_ps, m * 4 - 4)
                    dve.tensor_tensor(xt[:, u, 1], ps_x[:].rearrange("p r t -> p (r t)"),
                                      xt[:, u, 0].bitcast(F32), ALU.subtract).then_inc(xt_lo, 1)
                if there(n, ETILES):
                    split(1)
                    split(2)
                    split(3)

            tiles(dve, step)


def gather(nc, ctx, d, g, sem, results):
    x_sb, stats = g["x_sb"], g["stats"]
    SLOTS = 8
    two = ctx.enter_context(nc.sbuf_tensor("f_two", [P, SLOTS, QUAD, 2, DM], F32))
    two_in = [sem(f"f_two_in{u}") for u in range(SLOTS)]
    added, x_out, stats_out, held = sem("f_added"), sem("f_x_out"), sem("f_stats_out"), sem("f_held")
    view = results[0:2 * NTOK, :].rearrange("(t p k) c -> p t k c", p=P, k=2)

    with nc.Block() as block:
        @block.sync
        def _(sp):
            for s in range(SUPERS):
                u = s % SLOTS
                if s >= SLOTS:
                    sp.wait_ge(x_out, s - SLOTS + 1)
                sp.dma_start(two[:, u], view[:, QUAD * s:QUAD * s + QUAD]).then_inc(two_in[u], 16)

        @block.gpsimd
        def _(pool):
            for s in range(SUPERS):
                u = s % SLOTS
                pool.wait_ge(two_in[u], 16 * (s // SLOTS + 1))
                pool.tensor_tensor(two[:, u, :, 0], two[:, u, :, 0], two[:, u, :, 1], ALU.add).then_inc(added, 1)

        @block.vector
        def _(dve):
            with dve.Fori(0, SUPERS // SLOTS) as i:
                for u in range(SLOTS):
                    s = i * SLOTS + u
                    xs = x_sb[:, bass.ds(s * QUAD, QUAD), :]
                    dve.wait_ge(added, s + 1)
                    dve.tensor_tensor(xs, xs, two[:, u, :, 0], ALU.add).then_inc(x_out, 1)
                    dve.wait_ge(x_out, s + 1)
                    for k in range(QUAD):
                        tile = s * QUAD + k
                        dve.bn_stats(row(stats, tile), row(x_sb, tile)).then_inc(stats_out, 1)


def setup(nc, ctx, d, g, sb, sem):
    x_sb, stats, ident, tg = g["x_sb"], g["stats"], g["ident"], g["tanh_gates"]
    CHUNKS = 8
    CT = TILES // CHUNKS
    x_view = d["x"].rearrange("(a b) s c -> (b s) a c", b=2)
    x_in = [sem(f"x_in{n}") for n in range(CHUNKS)]
    gates_in, ident_step, gates_ready = sem("gates_in"), sem("ident_step"), sem("gates_ready")
    stats_out = sem("stats_out")
    block = ctx.enter_context(nc.Block())

    @block.sync
    def _(sp):
        for n in range(CHUNKS):
            sp.dma_start(x_sb[:, CT * n:CT * n + CT, :], x_view[:, CT * n:CT * n + CT, :]).then_inc(x_in[n], 16)
        for n, (name, at) in enumerate((("g_xattn", 0), ("g_ffn", 0), ("g_xattn", 1), ("g_ffn", 1))):
            sp.dma_start(tg[:, n:n + 1], d[name][at:at + 1].partition_broadcast(P)).then_inc(gates_in, 16)

    @block.gpsimd
    def _(pool):
        pool.memset(ident[:], 0.0).then_inc(ident_step, 1)
        pool.wait_ge(ident_step, 1)
        pool.affine_select(out=ident[:], in_=ident[:], compare_op=ALU.not_equal, fill=1.0, base=0,
                           pattern=[[-1, P]], channel_multiplier=1).then_inc(ident_step, 1)

    @block.scalar
    def _(act):
        act.wait_ge(gates_in, 64)
        act.activation(tg[:], tg[:], ACT.Tanh).then_inc(gates_ready, 1)

    @block.vector
    def _(dve):
        for t in range(TILES):
            if t % CT == 0:
                dve.wait_ge(x_in[t // CT], 16)
            dve.bn_stats(stats[:, t], x_sb[:, t]).then_inc(stats_out, 1)


def layernorm_scales(nc, ctx, d, g, sb, sem):
    stats, mean, rstd = g["stats"], g["mean"], g["rstd"]
    uid = g["uid"] = g["uid"] + 1
    diff = sb(f"ln_diff{uid}", [P, TILES], F32)
    var = sb(f"ln_var{uid}", [P, TILES], F32)
    step, var_ready, std_ready = sem(f"ln_step{uid}"), sem(f"ln_var_ready{uid}"), sem(f"ln_std_ready{uid}")
    done = sem(f"ln_done{uid}")
    block = ctx.enter_context(nc.Block())

    @block.vector
    def _(dve):
        dve.tensor_tensor(mean[:], stats[:, :, 1], stats[:, :, 4], ALU.add).then_inc(step, 1)
        dve.tensor_tensor(diff[:], stats[:, :, 1], stats[:, :, 4], ALU.subtract).then_inc(step, 1)
        dve.tensor_tensor(var[:], stats[:, :, 2], stats[:, :, 5], ALU.add).then_inc(step, 1)
        dve.wait_ge(step, 1)
        dve.tensor_scalar(mean[:], mean[:], 0.5, None, ALU.mult).then_inc(step, 1)
        dve.wait_ge(step, 2)
        dve.tensor_tensor(diff[:], diff[:], diff[:], ALU.mult).then_inc(step, 1)
        dve.wait_ge(step, 3)
        dve.tensor_scalar(var[:], var[:], 1.0 / DM, LN_EPS, ALU.mult, ALU.add).then_inc(step, 1)
        dve.wait_ge(step, 6)
        dve.scalar_tensor_tensor(out=var[:], in0=diff[:], scalar=0.25, in1=var[:],
                                 op0=ALU.mult, op1=ALU.add).then_inc(var_ready, 1)
        dve.wait_ge(std_ready, 1)
        dve.reciprocal(rstd[:], var[:]).then_inc(done, 1)

    @block.scalar
    def _(act):
        act.wait_ge(var_ready, 1)
        act.activation(var[:], var[:], ACT.Sqrt).then_inc(std_ready, 1)


def store_x(nc, ctx, d, g, sb, sem):
    stored = sem("stored")
    block = ctx.enter_context(nc.Block())

    @block.sync
    def _(sp):
        sp.dma_start(d["out"].rearrange("(a b) s c -> (b s) a c", b=2), g["x_sb"][:]).then_inc(stored, 16)
        sp.wait_ge(stored, 16)


STAGES = (layernorm_scales, layer0_attention, layernorm_scales, mixture,
          layernorm_scales, layer1_attention, layernorm_scales, layer1_ffn)


def flamingo(nc, d, stages=None):
    with ExitStack() as whole:
        g = {
            "x_sb": whole.enter_context(nc.sbuf_tensor("x_sb", [P, TILES, DM], F32)),
            "stats": whole.enter_context(nc.sbuf_tensor("stats", [P, TILES, 6], F32)),
            "mean": whole.enter_context(nc.sbuf_tensor("mean", [P, TILES], F32)),
            "rstd": whole.enter_context(nc.sbuf_tensor("rstd", [P, TILES], F32)),
            "ext": whole.enter_context(nc.sbuf_tensor("ext", [P, 2, TILES], F32)),
            "uid": 0,
            "ident": whole.enter_context(nc.sbuf_tensor("ident", [P, P], F32)),
            "tanh_gates": whole.enter_context(nc.sbuf_tensor("tanh_gates", [P, 4], F32)),
        }
        for stage in (setup, *(stages or STAGES)):
            with ExitStack() as ctx:
                def sb(name, shape, dt):
                    return ctx.enter_context(nc.sbuf_tensor(name, shape, dt))

                def sem(name):
                    stage_sems.append(nc.alloc_semaphore(name=name))
                    return stage_sems[-1]

                stage_sems = []
                stage(nc, ctx, d, g, sb, sem)
            nc.clear_and_free_semaphores(stage_sems)
            nc.all_engine_barrier()


_INS = ["x", "ctx_1024", "mask_1x1xSxS2_ff0", "mask_BxS2_bk1", "g_xattn", "g_ffn",
        "L0_xattn_Wq", "L0_xattn_bq", "L0_xattn_Wk", "L0_xattn_bk", "L0_xattn_Wv", "L0_xattn_bv",
        "L0_xattn_Wo", "L0_xattn_bo", "L0_ffn_router_w", "L0_ffn_w_fc", "L0_ffn_b_fc", "L0_ffn_w_proj",
        "L0_ffn_b_proj", "L1_xattn_Wq", "L1_xattn_bq", "L1_xattn_Wk", "L1_xattn_bk", "L1_xattn_Wv",
        "L1_xattn_bv", "L1_ffn_W1", "L1_ffn_b1", "L1_ffn_W2", "L1_ffn_b2"]


def kernel(**inputs):
    import numpy as _np
    import concourse.bacc as _bacc
    from concourse import mybir as _mybir
    from concourse.bass_utils import run_bass_kernel_spmd as _run

    nc = _bacc.Bacc("TRN2", target_bir_lowering=False, num_devices=1)
    arrays, d = {}, {}
    for name in _INS:
        a = _np.ascontiguousarray(inputs[name])
        arrays[f"in_{name}_dram"] = a
        d[name] = nc.dram_tensor(f"in_{name}_dram", a.shape, _mybir.dt.from_np(a.dtype), kind="ExternalInput").ap()
    d["out"] = nc.dram_tensor("out_dram", (BATCH, SEQ, DM), F32, kind="ExternalOutput").ap()
    flamingo(nc, d)
    r = _run(nc, [arrays], core_ids=[0])
    return r.results[0]["out_dram"]
```

```python
from contextlib import ExitStack

import concourse.bass as bass
from concourse import mybir

ALU = mybir.AluOpType
ACT = mybir.ActivationFunctionType
AX_X = mybir.AxisListType.X
F32 = mybir.dt.float32
F32R = mybir.dt.float32r
BF16 = mybir.dt.bfloat16
U8 = mybir.dt.uint8
U32 = mybir.dt.uint32

P = 128
BATCH, SEQ, DM = 128, 64, 128
NTOK = BATCH * SEQ
TILES = NTOK // P
QUAD = 4
SUPERS = TILES // QUAD
ST = QUAD * P
HEADS, DH = 16, 8
GROUPS = HEADS // 2
VW = 9
VB = 2 * GROUPS * VW
FMAX = 3.4028234663852886e38
LN_EPS = 1e-5
Q_SLOTS = (0, 0, 1, 1, 0, 2, 1, 2)
K_SLOTS = (0, 1, 0, 1, 2, 0, 2, 1)


def layer0_attention(nc, ctx, d, g, sb, sem):
    x_sb = g["x_sb"]
    ident, tg = g["ident"], g["tanh_gates"]

    wq, wk, wv, wo, bq, bk, bv, bo, mask, ctx_in = (
        g["layer0"][n] for n in ("wq", "wk", "wv", "wo", "bq", "bk", "bv", "bo", "mask", "ctx_in"))
    qk_in, w_in, loaded, x_in = (g["layer0"][n] for n in ("qk_in", "w_in", "loaded", "x_in"))
    scales = g["layer0"]["scales"]
    stats, mean, rstd = g["stats"], g["mean"], g["rstd"]
    xn = sb("a_xn", [P, QUAD, DM], F32)
    xn_t = sb("a_xn_t", [P, ST], F32)
    ctx_t = sb("a_ctx_t", [P, 2, ST // SEQ, 2, SEQ], F32)
    qk = sb("a_qk", [P, 2, 2, ST], F32)
    parts = sb("a_parts", [P, 2, 2, 3, ST], BF16)
    stack = sb("a_stack", [P, 2, 2, GROUPS, ST], BF16)
    VALL = QUAD * 2 * VB
    vals = [sb(f"a_vals{u}", [P, VALL + SEQ], F32) for u in range(2)]
    probs = sb("a_probs", [P, 4, GROUPS, 2, SEQ], F32)
    top = sb("a_top", [P, 4, HEADS], F32)
    probs_t = sb("a_probs_t", [P, 2, GROUPS, P], F32)
    rsum = sb("a_rsum", [P, HEADS], F32)
    heads = sb("a_heads", [P, HEADS, DH], F32)
    heads_t = sb("a_heads_t", [P, P], F32)

    parked = nc.dram_tensor("a_parked", (2, 2, 3, P, ST), BF16, kind="Internal").ap()
    ps_s = [ctx.enter_context(nc.psum_tensor(f"a_ps_s{j}", [P, GROUPS, SEQ], F32)) for j in range(2)]
    ps_pt = [ctx.enter_context(nc.psum_tensor(f"a_ps_pt{j}", [P, 4, P], F32)) for j in range(2)]
    ps_1 = [ctx.enter_context(nc.psum_tensor(f"a_ps_1{j}", [P, ST], F32)) for j in range(2)]
    ps_o = ctx.enter_context(nc.psum_tensor("a_ps_o", [P, 2, 256], F32))
    ps_y = ctx.enter_context(nc.psum_tensor("a_ps_y", [P, 4, P], F32))

    held = sem("a_held")
    consts = sem("a_consts")
    xn_ready = sem("a_xn_ready")
    bo_added = sem("a_bo_added")
    xt_ps, ct_ps = sem("a_xt_ps"), sem("a_ct_ps")
    xt_sb, ct_sb = sem("a_xt_sb"), sem("a_ct_sb")
    q_ps, k_ps, qk_sb = sem("a_q_ps"), sem("a_k_ps"), sem("a_qk_sb")
    hi_cut, hi_off, mid_cut, split = (sem(f"a_{n}") for n in ("hi_cut", "hi_off", "mid_cut", "split"))
    parts_parked = sem("a_parts_parked")
    stacked = sem("a_stacked")
    v_ps, v_sb = sem("a_v_ps"), sem("a_v_sb")
    s_ps, s_sb = sem("a_s_ps"), sem("a_s_sb")
    top_ready, shifted, p_ready = sem("a_top_ready"), sem("a_shifted"), sem("a_p_ready")
    pt_ps, pt_sb = sem("a_pt_ps"), sem("a_pt_sb")
    o_ps, rsum_ready, o_sb = sem("a_o_ps"), sem("a_rsum_ready"), sem("a_o_sb")
    ot_ps, ot_sb = sem("a_ot_ps"), sem("a_ot_sb")
    y_ps, x_out, stats_out = sem("a_y_ps"), sem("a_x_out"), sem("a_stats_out")

    ctx_view = d["ctx_1024"].rearrange("(a b) s c -> (b s) a c", b=2)

    def sweep(eng, step, before_first=None):
        for s in range(-3, 1):
            if s == 0 and before_first:
                before_first()
            step(s, s % 2)
        with eng.Fori(0, (SUPERS - 4) // 2) as i:
            step(i * 2 + 1, 1)
            step(i * 2 + 2, 0)
        for s in range(SUPERS - 3, SUPERS + 1):
            step(s, s % 2)

    def hold(eng):
        eng.sem_inc(held, 1)

    def known(n):
        return isinstance(n, int)

    def there(n, count):
        return not known(n) or 0 <= n < count

    def later(n, least):
        return not known(n) or n >= least

    block = ctx.enter_context(nc.Block())

    @block.sync
    def _(sp):
        def step(s, u):
            nxt = s + 3
            if there(nxt, SUPERS) and later(nxt, 1):
                sp.wait_ge(loaded, nxt * 16)
                hold(sp)
                if later(nxt, 2):
                    sp.wait_ge(ct_ps, nxt - 1)
                    hold(sp)
                sp.dma_start(ctx_in[:, 1 - u], ctx_view[:, bass.ds(nxt * QUAD, QUAD), :]).then_inc(loaded, 16)
            nxt = s + 1
            if there(nxt, SUPERS):
                if later(nxt, 1):
                    sp.wait_ge(stacked, nxt * 512)
                    hold(sp)
                if later(nxt, 2):
                    sp.wait_ge(s_ps, (nxt - 1) * QUAD)
                    hold(sp)
                sp.wait_ge(parts_parked, nxt * 16 + 16)
                hold(sp)
                for x in range(2):
                    for slot, part in enumerate((Q_SLOTS, K_SLOTS)[x]):
                        rows = parked[1 - u, x, part].rearrange("(g j e) t -> j e g t", g=GROUPS, j=2)
                        for j in range(2):
                            sp.dma_start(stack[64 * j + DH * slot:64 * j + DH * slot + DH, 1 - u, x], rows[j])\
                              .then_inc(stacked, 16)
            nxt = s + 2
            if there(nxt, SUPERS):
                sp.wait_ge(split, nxt + 1)
                hold(sp)
                if later(nxt, 2):
                    sp.wait_ge(stacked, nxt * 512 - 512)
                    hold(sp)
                sp.dma_start(parked[u].rearrange("x r p t -> p x r t"), parts[:, u]).then_inc(parts_parked, 16)

        sweep(sp, step)

    @block.gpsimd
    def _(pool):
        for u in range(2):
            pool.memset(vals[u][:], 0.0).then_inc(consts, 1)
        pool.wait_ge(consts, 2)
        for u in range(2):
            for j in range(2):
                ones = vals[u][64 * j:64 * j + 64, 0:VALL].rearrange("p (n w) -> p n w", w=2 * VW)
                pool.memset(ones[:, :, VW * j + DH], 1.0).then_inc(consts, 1)
        pool.wait_ge(consts, 6)
        pool.wait_ge(w_in, 16 * 6)
        pool.tensor_scalar(mask[:], mask[:], FMAX, None, ALU.mult).then_inc(consts, 1)
        pool.tensor_scalar(bo[:], bo[:], tg[:, 0:1], None, ALU.mult).then_inc(consts, 1)
        pool.wait_ge(consts, 8)

        def step(s, u):
            if there(s + 1, SUPERS):
                n = s + 1
                pool.wait_ge(xn_ready, n * QUAD + QUAD)
                xs = x_sb[:, bass.ds(n * QUAD, QUAD), :]
                pool.tensor_tensor(xs, xs, bo[:].unsqueeze(1).broadcast_to([P, QUAD, DM]), ALU.add)\
                    .then_inc(bo_added, 1)
            n = s + 2
            for j in range(QUAD):
                t = s * QUAD + j
                if j == 2 and there(n, SUPERS):
                    pool.wait_ge(hi_cut, n * 2 + 2)
                    pool.tensor_tensor(qk[:, u], qk[:, u], parts[:, u, :, 0, :], ALU.subtract).then_inc(hi_off, 1)
                if j == 3 and there(n, SUPERS):
                    pool.wait_ge(mid_cut, n + 1)
                    pool.tensor_tensor(parts[:, u, :, 2, :], qk[:, u], parts[:, u, :, 1, :],
                                       ALU.subtract).then_inc(split, 1)
                if there(t, TILES):
                    pool.wait_ge(top_ready, t + 1)
                    p = probs[:, j].rearrange("p g j k -> p (g j) k")
                    pool.tensor_tensor(p, p, top[:, j].unsqueeze(2).broadcast_to([P, HEADS, SEQ]),
                                       ALU.subtract).then_inc(shifted, 1)

        sweep(pool, step)

    @block.scalar
    def _(act):
        act.wait_ge(qk_in, 64)

        def step(s, u):
            n = s + 2
            for j in range(QUAD):
                t = s * QUAD + j
                if there(t - 2, TILES):
                    if later(t - 2, 2):
                        act.wait_ge(o_ps, t - 3)
                    for h in range(2):
                        act.wait_ge(pt_ps, t * 2 - 3 + h)
                        act.activation(probs_t[:, j % 2, 4 * h:4 * h + 4, :], ps_pt[h][:], ACT.Copy)\
                            .then_inc(pt_sb, 1)
                if there(n, SUPERS) and j == 3:
                    act.wait_ge(hi_off, n + 1)
                    act.activation(parts[:, u, :, 1, :], qk[:, u], ACT.Copy).then_inc(mid_cut, 1)
                if there(t - 1, TILES):
                    act.wait_ge(shifted, t)
                    act.activation(probs[:, (j + 3) % 4], probs[:, (j + 3) % 4], ACT.Exp).then_inc(p_ready, 1)
                if there(t - 3, TILES):
                    act.wait_ge(ot_ps, t - 2)
                    act.activation(heads_t[:], ps_y[:, 0, :], ACT.Copy).then_inc(ot_sb, 1)
                if there(n, SUPERS) and j == 0:
                    act.wait_ge(xt_ps, n + 1)
                    act.activation(xn_t[:], ps_1[0][:], ACT.Copy).then_inc(xt_sb, 1)
                    act.wait_ge(ct_ps, n + 1)
                    if later(n, 2):
                        act.wait_ge(v_ps, n * 2 - 2)
                    act.activation(ctx_t[:, u], ps_1[1][:].rearrange("p (b k) -> p b k", k=SEQ).unsqueeze(2)
                                   .broadcast_to([P, ST // SEQ, 2, SEQ]), ACT.Copy).then_inc(ct_sb, 1)
                if there(n, SUPERS) and j == 1:
                    if later(n, 2):
                        act.wait_ge(split, n - 1)
                        act.wait_ge(parts_parked, n * 16 - 16)
                    for x, ps, bias in ((0, q_ps, bq), (1, k_ps, bk)):
                        act.wait_ge(ps, n + 1)
                        act.activation(qk[:, u, x], ps_1[x][:], ACT.Identity, bias=bias[:, 0:1]).then_inc(qk_sb, 1)
                        act.activation(parts[:, u, x, 0], ps_1[x][:], ACT.Identity, bias=bias[:, 0:1])\
                            .then_inc(hi_cut, 1)

        sweep(act, step, lambda: scales_on_act(act, scales, 1))

    @block.tensor
    def _(pe):
        pe.wait_ge(qk_in, 64)

        def step(s, u):
            n, nv = s + 2, s + 1
            for j in range(QUAD):
                t = s * QUAD + j
                if there(t - 2, TILES):
                    pe.wait_ge(p_ready, t - 1)
                    for h in range(2):
                        if later(t - 2, 1):
                            pe.wait_ge(pt_sb, t * 2 - 5 + h)
                        for k in range(4):
                            mm = pe.transpose(ps_pt[h][:, k, :],
                                              probs[:, (j + 2) % 4, 4 * h + k].rearrange("p j k -> p (j k)"),
                                              ident[:])
                        mm.then_inc(pt_ps, 1)
                if there(t, TILES):
                    if j == 0:
                        pe.wait_ge(stacked, (s + 1) * 512)
                    if later(t, 1):
                        pe.wait_ge(s_sb, t * 2)
                    hold(pe)
                    for gr in range(GROUPS):
                        for h in range(2):
                            for b in range(2):
                                at = slice(P * j + SEQ * b, P * j + SEQ * b + SEQ)
                                rows = slice(64 * h, 64 * h + 64)
                                mm = pe.matmul(ps_s[h][SEQ * b:SEQ * b + SEQ, gr, :],
                                               stack[rows, u, 0, gr, at], stack[rows, u, 1, gr, at],
                                               start=True, stop=True)
                    mm.then_inc(s_ps, 1)
                if there(t - 3, TILES):
                    if later(t - 3, 1):
                        pe.wait_ge(x_out, t - 3)
                    pe.wait_ge(o_sb, t * 2 - 4)
                    pe.transpose(ps_y[:, 0, :], heads[:].rearrange("p h e -> p (h e)"), ident[:])\
                        .then_inc(ot_ps, 1)
                if there(n, SUPERS) and j == 0:
                    pe.wait_ge(xn_ready, n * QUAD + QUAD)
                    if later(n, 2):
                        pe.wait_ge(v_sb, n * 4 - 4)
                    elif n == 1:
                        pe.wait_ge(hi_cut, 2)
                    for k in range(QUAD):
                        mm = pe.transpose(ps_1[0][:, P * k:P * k + P], xn[:, k, :], ident[:])
                    mm.then_inc(xt_ps, 1)
                    pe.wait_ge(loaded, n * 16 + 16)
                    for k in range(QUAD):
                        mm = pe.transpose(ps_1[1][:, P * k:P * k + P], ctx_in[:, u, k, :], ident[:])
                    mm.then_inc(ct_ps, 1)
                if there(n, SUPERS) and j == 1:
                    pe.wait_ge(xt_sb, n + 1)
                    pe.matmul(ps_1[0][:], wq[:], xn_t[:], start=True, stop=True).then_inc(q_ps, 1)
                    pe.wait_ge(ct_sb, n + 1)
                    pe.matmul(ps_1[1][:], wk[:], ctx_t[:, u, :, 0, :], start=True, stop=True).then_inc(k_ps, 1)
                if there(nv, SUPERS) and j == 2:
                    if not later(nv, 1):
                        pe.wait_ge(w_in, 16 * 6)
                    for h in range(2):
                        if there(n, SUPERS):
                            pe.wait_ge(hi_cut, n * 2 + 1 + h)
                        else:
                            pe.wait_ge(v_sb, nv * 4)
                        for b in range(4):
                            mm = pe.matmul(ps_1[h][:, P * b:P * b + P],
                                           ctx_t[:, 1 - u, 4 * h + b].rearrange("p a k -> p (a k)"), wv[:],
                                           start=True, stop=True)
                        mm.then_inc(v_ps, 1)
                if there(t - 2, TILES):
                    sv = s if j >= 2 else s - 1
                    pe.wait_ge(v_sb, (sv + 1) * 4)
                    if later(t - 2, 1):
                        pe.wait_ge(o_sb, t * 2 - 4)
                    v0 = 2 * VB * ((j + 2) % 4)
                    vv = vals[u if j >= 2 else 1 - u]
                    for gr in range(GROUPS):
                        if gr % 4 == 0:
                            pe.wait_ge(pt_sb, t * 2 - 3 + gr // 4)
                        c = v0 + 2 * VW * gr
                        rhs = vv[:, c:c + 2 * VB].rearrange("p (b w) -> p b w", b=2)[:, :, 0:SEQ] if \
                            c + 2 * VB <= VALL + SEQ else None
                        if rhs is None:
                            rhs = vv[:, c - 2 * VB + VB + SEQ:c + VB + SEQ].rearrange(
                                "p (b w) -> p b w", b=2)[:, :, VB - SEQ:VB]
                        mm = pe.matmul(ps_o[:, :, 2 * VW * gr:2 * VW * gr + SEQ], probs_t[:, j % 2, gr, :],
                                       rhs, start=True, stop=True)
                    mm.then_inc(o_ps, 1)
                if there(t - 3, TILES):
                    pe.wait_ge(ot_sb, t - 2)
                    pe.matmul(ps_y[:, 1, :], heads_t[:], wo[:], start=True, stop=True).then_inc(y_ps, 1)

        sweep(pe, step)

    @block.vector
    def _(dve):
        def other_scales():
            for n, (first, end) in enumerate(X_LOADS):
                for t in range(max(first, FIRST), end):
                    if t == first:
                        dve.wait_ge(x_in[n], 16)
                    dve.bn_stats(stats[:, t], x_sb[:, t]).then_inc(scales["stats_out"], 1)
            scales_on_dve(dve, g, scales, 1, slice(FIRST, TILES))
            dve.wait_ge(scales["done"], 2)
            dve.wait_ge(consts, 8)

        def step(s, u):
            for j in range(QUAD):
                t = s * QUAD + j
                if there(t - 3, TILES):
                    dve.wait_ge(o_ps, t - 2)
                    if later(t - 3, 1):
                        dve.wait_ge(ot_ps, t - 3)
                    for b in range(2):
                        o = ps_o[SEQ * b:SEQ * b + SEQ, b, 0:VB].rearrange("p (h w) -> p h w", w=VW)
                        dve.reciprocal(rsum[SEQ * b:SEQ * b + SEQ, :], o[:, :, DH]).then_inc(rsum_ready, 1)
                    for b in range(2):
                        rows = slice(SEQ * b, SEQ * b + SEQ)
                        o = ps_o[rows, b, 0:VB].rearrange("p (h w) -> p h w", w=VW)
                        dve.wait_ge(rsum_ready, t * 2 - 5 + b)
                        dve.tensor_tensor(heads[rows], o[:, :, 0:DH],
                                          rsum[rows, :].unsqueeze(2).broadcast_to([SEQ, HEADS, DH]),
                                          ALU.mult).then_inc(o_sb, 1)
                if there(t - 4, TILES):
                    dve.wait_ge(y_ps, t - 3)
                    if j == 0:
                        dve.wait_ge(bo_added, s)
                    xs = x_sb[:, bass.ds(t - 4, 1), :].rearrange("p a c -> p (a c)")
                    dve.scalar_tensor_tensor(out=xs, in0=ps_y[:, 1, :], scalar=tg[:, 0:1], in1=xs,
                                             op0=ALU.mult, op1=ALU.add).then_inc(x_out, 1)
                    if j % 2:
                        for k in range(2):
                            dve.wait_ge(x_out, t - 4 + k)
                            tile = t - 5 + k
                            xs = x_sb[:, bass.ds(tile, 1), :].rearrange("p a c -> p (a c)")
                            dve.bn_stats(stats[:, bass.ds(tile, 1), :].rearrange("p a c -> p (a c)"), xs)\
                                .then_inc(stats_out, 1)
                n = s + 3
                if there(n, SUPERS) and j == 1:
                    if later(n, 1):
                        dve.wait_ge(xt_ps, n)
                    for k in range(QUAD):
                        tile = n * QUAD + k
                        xs = x_sb[:, bass.ds(tile, 1), :].rearrange("p a c -> p (a c)")
                        dve.tensor_scalar(xn[:, k, :], xs, mean[:, bass.ds(tile, 1)], rstd[:, bass.ds(tile, 1)],
                                          ALU.subtract, ALU.mult).then_inc(xn_ready, 1)
                nv = s + 1
                if there(nv, SUPERS) and j == 3:
                    if not later(nv, 1):
                        dve.wait_ge(consts, 6)
                        dve.wait_ge(w_in, 16 * 6)
                    for h in range(2):
                        dve.wait_ge(v_ps, nv * 2 + h + 1)
                        if later(nv, 2):
                            dve.wait_ge(o_ps, (nv - 1) * QUAD)
                        for r in range(2):
                            rows = slice(64 * r, 64 * r + 64)
                            out = vals[1 - u][rows, 4 * VB * h:4 * VB * h + 4 * VB].rearrange(
                                "p (n g w) -> p n g w", n=4, g=GROUPS)[:, :, :, VW * r:VW * r + DH]
                            src = ps_1[h][rows, :].rearrange("p (n g w) -> p n g w", n=4, g=GROUPS)
                            bias = bv[rows, :].rearrange("p (g w) -> p g w", g=GROUPS)
                            dve.tensor_tensor(out, src[:, :, :, DH * r:DH * r + DH],
                                              bias[:, :, DH * r:DH * r + DH].unsqueeze(1)
                                              .broadcast_to([64, 4, GROUPS, DH]), ALU.add).then_inc(v_sb, 1)
                if there(t, TILES):
                    dve.wait_ge(s_ps, t + 1)
                    if later(t, 4):
                        dve.wait_ge(pt_ps, t * 2 - 6)
                    for h in range(2):
                        dve.scalar_tensor_tensor(
                            out=probs[:, j, :, h, :], in0=ps_s[h][:], scalar=DH ** -0.5,
                            in1=mask[:].unsqueeze(1).broadcast_to([P, GROUPS, SEQ]),
                            op0=ALU.mult, op1=ALU.subtract).then_inc(s_sb, 1)
                    dve.wait_ge(s_sb, t * 2 + 2)
                    dve.tensor_reduce(top[:, j], probs[:, j].rearrange("p g j k -> p (g j) k"),
                                      AX_X, ALU.max).then_inc(top_ready, 1)

        sweep(dve, step, other_scales)


def sweep(eng, step, peeled=2):
    for s in range(-2, peeled):
        step(s, s % 2)
    with eng.Fori(0, (SUPERS - peeled - 2) // 2) as i:
        step(i * 2 + peeled, 0)
        step(i * 2 + peeled + 1, 1)
    for s in range(SUPERS - 2, SUPERS + 2):
        step(s, s % 2)


def there(n, count):
    return not isinstance(n, int) or 0 <= n < count


def later(n, least):
    return not isinstance(n, int) or n >= least


def row(x, tile):
    return x[:, bass.ds(tile, 1), :].rearrange("p a c -> p (a c)")


def layer1_attention(nc, ctx, d, g, sb, sem):
    x_sb, ident, tg = g["x_sb"], g["ident"], g["tanh_gates"]
    stats, mean, rstd = g["stats"], g["mean"], g["rstd"]
    scales = g["gather"]["scales"]

    early = g["layer1"]
    wq, bq, mask_u8, keys_t, vals = (early[n] for n in ("wq", "bq", "mask_u8", "keys_t", "vals"))
    w_in, m_in, k_in, v_in = (early[n] for n in ("w_in", "m_in", "k_in", "v_in"))
    term_k, term_q, terms = (early[n] for n in ("term_k", "term_q", "terms"))
    xn = sb("c_xn", [P, QUAD, DM], F32)
    xn_t = sb("c_xn_t", [P, ST], F32)
    q = sb("c_q", [P, ST], F32)
    ntop = sb("c_ntop", [P, 2, QUAD], F32)
    probs = sb("c_probs", [P, 2, QUAD, P], F32)
    rsum = sb("c_rsum", [P, 2, QUAD], F32)
    gain = sb("c_gain", [P, 2, QUAD], F32)
    probs_t = sb("c_probs_t", [P, QUAD, P], F32)

    def bank(name):
        return ctx.enter_context(nc.psum_tensor(name, [P, QUAD, P], F32))

    ps_x, ps_q, ps_pt = (bank(f"c_ps_{n}") for n in ("x", "q", "pt"))
    ps_s, ps_o = ([bank(f"c_ps_{n}{u}") for u in range(2)] for n in "so")

    held, mask_ready = (sem(f"c_{n}") for n in ("held", "mask_ready"))
    x_less, xn_ready, xt_ps, xt_sb = (sem(f"c_{n}") for n in ("x_less", "xn_ready", "xt_ps", "xt_sb"))
    q_ps, q_sb = (sem(f"c_{n}") for n in ("q_ps", "q_sb"))
    s_ps, top_step, top_ready, p_ready = (sem(f"c_{n}") for n in ("s_ps", "top_step", "top_ready", "p_ready"))
    pt_ps, pt_sb, o_ps, gain_step, x_out, stats_out = (
        sem(f"c_{n}") for n in ("pt_ps", "pt_sb", "o_ps", "gain_step", "x_out", "stats_out"))

    def hold(eng):
        eng.sem_inc(held, 1)

    block = ctx.enter_context(nc.Block())

    @block.sync
    def _(sp):
        def step(s, u):
            n = s + 2
            if there(n, SUPERS) and later(n, 1):
                sp.wait_ge(k_in, n * 16)
                hold(sp)
                if later(n, 2):
                    sp.wait_ge(s_ps, n - 1)
                    hold(sp)
                sp.dma_start(keys_t[:, u], g["keys_t"][:, bass.ds(n * ST, ST)]).then_inc(k_in, 16)
            n = s + 1
            if there(n, SUPERS) and later(n, 1):
                sp.wait_ge(v_in, n * 16)
                hold(sp)
                if later(n, 2):
                    sp.wait_ge(o_ps, n - 1)
                    hold(sp)
                sp.dma_start(vals[:, 1 - u], g["values"][:, bass.ds(n * QUAD, QUAD), :]).then_inc(v_in, 16)

        sweep(sp, step)

    @block.gpsimd
    def _(pool):
        def normalise(n):
            if later(n, 1):
                pool.wait_ge(xt_ps, n)
            if isinstance(n, int) and n == FIRST // QUAD:
                pool.wait_ge(scales["done"], 2)
            four = bass.ds(n * QUAD, QUAD)
            pool.tensor_tensor(xn[:], x_sb[:, four, :], mean[:, four].unsqueeze(2).broadcast_to([P, QUAD, DM]),
                               ALU.subtract).then_inc(x_less, 1)
            pool.wait_ge(x_less, n + 1)
            pool.tensor_tensor(xn[:], xn[:], rstd[:, four].unsqueeze(2).broadcast_to([P, QUAD, DM]),
                               ALU.mult).then_inc(xn_ready, 1)

        normalise(0)
        g["gather"]["other_sums"](pool)
        pool.wait_ge(m_in, 16)

        def step(s, u):
            n = s + 2
            if there(n, SUPERS):
                if not isinstance(n, int) or n:
                    normalise(n)
                if later(n, 2):
                    pool.wait_ge(s_ps, n - 1)
                    hold(pool)
                pool.tensor_copy(term_k[0:1, u].rearrange("p t b k -> p (t b k)"),
                                 mask_u8[:, bass.ds(n, 1)].rearrange("p a k -> p (a k)")).then_inc(mask_ready, 1)

        sweep(pool, step)

    @block.scalar
    def _(act):
        act.wait_ge(w_in, 32)

        def step(s, u):
            if there(s - 1, SUPERS):
                act.wait_ge(pt_ps, s)
                if later(s - 1, 1):
                    act.wait_ge(o_ps, s - 1)
                act.activation(probs_t[:], ps_pt[:], ACT.Copy).then_inc(pt_sb, 1)
            if isinstance(s, int) and s == 0:
                scales_on_act(act, scales, 1)
            n = s + 1
            if there(n, SUPERS):
                act.wait_ge(q_ps, n + 1)
                if later(n, 1):
                    act.wait_ge(s_ps, n)
                act.activation(q[:], ps_q[:].rearrange("p a b -> p (a b)"), ACT.Identity, bias=bq[:, 0:1]).then_inc(q_sb, 1)
            if there(s, SUPERS):
                act.wait_ge(top_ready, s + 1)
                for k in range(QUAD):
                    act.activation(probs[:, u, k], ps_s[u][:, k], ACT.Exp, bias=ntop[:, u, k:k + 1],
                                   accum_out=rsum[:, u, k:k + 1]).then_inc(p_ready, 1)
            n = s + 2
            if there(n, SUPERS):
                act.wait_ge(xt_ps, n + 1)
                if later(n, 1):
                    act.wait_ge(q_ps, n)
                act.activation(xn_t[:], ps_x[:].rearrange("p a b -> p (a b)"), ACT.Copy).then_inc(xt_sb, 1)

        sweep(act, step)
        act.wait_ge(g["gather"]["wt_out"], 16)

    @block.tensor
    def _(pe):
        pe.wait_ge(w_in, 32)

        def step(s, u):
            if there(s - 1, SUPERS):
                pe.wait_ge(p_ready, s * 4)
                if later(s - 1, 1):
                    pe.wait_ge(pt_sb, s - 1)
                for k in range(QUAD):
                    mm = pe.transpose(ps_pt[:, k], probs[:, 1 - u, k], ident[:])
                mm.then_inc(pt_ps, 1)
            n = s + 1
            if there(n, SUPERS):
                pe.wait_ge(xt_sb, n + 1)
                if later(n, 1):
                    pe.wait_ge(q_sb, n)
                pe.matmul(ps_q[:].rearrange("p a b -> p (a b)"), wq[:], xn_t[:], start=True, stop=True)\
                    .then_inc(q_ps, 1)
            if there(s - 1, SUPERS):
                pe.wait_ge(pt_sb, s)
                pe.wait_ge(v_in, s * 16)
                if later(s - 1, 2):
                    pe.wait_ge(x_out, s * 4 - 8)
                for k in range(QUAD):
                    mm = pe.matmul(ps_o[1 - u][:, k], probs_t[:, k], vals[:, 1 - u, k], start=True, stop=True)
                mm.then_inc(o_ps, 1)
            n = s + 2
            if there(n, SUPERS):
                pe.wait_ge(xn_ready, n + 1)
                if later(n, 1):
                    pe.wait_ge(xt_sb, n)
                for k in range(QUAD):
                    mm = pe.transpose(ps_x[:, k], xn[:, k], ident[:])
                mm.then_inc(xt_ps, 1)
            n = s + 1
            if there(n, SUPERS):
                pe.wait_ge(q_sb, n + 1)
                pe.wait_ge(k_in, n * 16 + 16)
                pe.wait_ge(mask_ready, n + 1)
                if later(n, 2):
                    pe.wait_ge(p_ready, n * 4 - 4)
                for k in range(QUAD):
                    tok = slice(P * k, P * k + P)
                    pe.matmul(ps_s[1 - u][:, k], q[:, tok], keys_t[:, 1 - u, tok], start=True, stop=False)
                    mm = pe.matmul(ps_s[1 - u][:, k], term_q[:],
                                   term_k[:, 1 - u, k].rearrange("p b k -> p (b k)"),
                                   start=False, stop=True)
                mm.then_inc(s_ps, 1)

        sweep(pe, step, peeled=4)

    @block.vector
    def _(dve):
        def step(s, u):
            if there(s - 1, SUPERS):
                dve.wait_ge(p_ready, s * 4)
                dve.reciprocal(gain[:, 1 - u], rsum[:, 1 - u]).then_inc(gain_step, 1)
                dve.wait_ge(gain_step, s * 2 - 1)
                dve.tensor_scalar(gain[:, 1 - u], gain[:, 1 - u], tg[:, 1:2], None, ALU.mult).then_inc(gain_step, 1)
            if there(s, SUPERS):
                dve.wait_ge(s_ps, s + 1)
                if later(s, 2):
                    dve.wait_ge(p_ready, s * 4 - 4)
                dve.tensor_reduce(ntop[:, u], ps_s[u][:], AX_X, ALU.max).then_inc(top_step, 1)
                dve.wait_ge(top_step, s + 1)
                dve.tensor_scalar(ntop[:, u], ntop[:, u], -1.0, None, ALU.mult).then_inc(top_ready, 1)
            p = s - 2
            if there(p, SUPERS):
                dve.wait_ge(gain_step, p * 2 + 2)
                dve.wait_ge(o_ps, p + 1)
                for k in range(QUAD):
                    xs = row(x_sb, p * QUAD + k)
                    dve.scalar_tensor_tensor(out=xs, in0=ps_o[u][:, k], scalar=gain[:, u, k:k + 1], in1=xs,
                                             op0=ALU.mult, op1=ALU.add).then_inc(x_out, 1)
                for k in range(QUAD):
                    dve.wait_ge(x_out, p * 4 + 1 + k)
                    tile = p * QUAD + k
                    dve.bn_stats(row(stats, tile), row(x_sb, tile)).then_inc(stats_out, 1)
                four = bass.ds(p * QUAD, QUAD)
                for e, op in enumerate((ALU.max, ALU.min)):
                    dve.tensor_reduce(g["ext"][:, e, four], x_sb[:, four, :], AX_X, op).then_inc(stats_out, 1)

        g["gather"]["other_rows"](dve)
        sweep(dve, step)


MAGIC = 12582912.0
QMIN, QMAX = -128.0, 127.0
HID = 512
CHUNKS = HID // P


def layer1_ffn(nc, ctx, d, g, sb, sem):
    x_sb, ident, tg = g["x_sb"], g["ident"], g["tanh_gates"]
    mean, rstd = g["mean"], g["rstd"]

    hid = sb("d_hid", [P, SUPERS, CHUNKS, ST], F32)
    wqt = sb("d_wqt", [P, 2, CHUNKS, P], BF16)
    wscale = g["wscale"]
    b1 = sb("d_b1", [P, CHUNKS], F32)
    b2 = sb("d_b2", [P, DM], F32)
    ext = g["ext"]
    peak = sb("d_peak", [P, 2], F32)
    peaks = sb("d_peaks", [P, 2], F32)
    hpeak = sb("d_hpeak", [P, 2, SUPERS], F32)
    hp = sb("d_hp", [P, 2], F32)
    hps = sb("d_hps", [P, 2], F32)
    qs = [sb(f"d_qs{n}", [P, 10], F32) for n in range(2)]
    outscale = sb("d_outscale", [P, 2], F32)
    xq32 = sb("d_xq32", [P, 2, QUAD, DM], F32)
    xqt = sb("d_xqt", [P, 2, ST], BF16)
    hq = sb("d_hq", [P, 2, CHUNKS, ST], BF16)

    def qscale(dve, q, amax, namin, step, at):
        def then(ins, wait=True):
            nonlocal at
            at += 1
            ins.then_inc(step, 1)
            if wait:
                dve.wait_ge(step, at)

        then(dve.memset(q[:, 7:8], MAGIC), wait=False)
        then(dve.memset(q[:, 9:10], -MAGIC), wait=False)
        then(dve.tensor_tensor(q[:, 0:1], amax, namin, ALU.add))
        then(dve.tensor_scalar(q[:, 0:1], q[:, 0:1], 1.0 / 255.0, 1e-8, ALU.mult, ALU.max))
        then(dve.reciprocal(q[:, 1:2], q[:, 0:1]))
        then(dve.tensor_scalar(q[:, 2:3], namin, q[:, 1:2], MAGIC, ALU.mult, ALU.add))
        then(dve.tensor_scalar(q[:, 3:4], q[:, 2:3], MAGIC, QMIN, ALU.subtract, ALU.add))
        then(dve.tensor_scalar(q[:, 4:5], q[:, 3:4], QMIN, QMAX, ALU.max, ALU.min))
        then(dve.tensor_scalar(q[:, 5:6], q[:, 4:5], -1.0, QMIN, ALU.mult, ALU.add), wait=False)
        then(dve.tensor_scalar(q[:, 6:7], q[:, 4:5], -1.0, QMAX + MAGIC, ALU.mult, ALU.add), wait=False)
        then(dve.tensor_scalar(q[:, 8:9], q[:, 4:5], -1.0, QMIN + MAGIC, ALU.mult, ALU.add))
        return at

    def bank(name):
        return ctx.enter_context(nc.psum_tensor(name, [P, CHUNKS, P], F32))

    ps_x = bank("d_ps_x")
    ps_h = [bank(f"d_ps_h{n}") for n in range(CHUNKS)]
    ps_y = [bank(f"d_ps_y{n}") for n in range(2)]

    names = ("w_in", "held", "b2_ready", "ext", "peak_ready", "peaks_ready", "step", "x_scale",
             "n_ready", "xt_ready", "xq_ready", "xt_ps", "xt_sb", "h_ps", "h_sb", "hpeak_ready", "hp_ready", "hps_ready",
             "h_scale", "x_less", "b2_added", "t_ready", "c_ready", "hq_ready", "y_ps", "x_out", "stored")
    (w_in, held, b2_ready, ext_ready, peak_ready, peaks_ready, qstep, x_scale,
     n_ready, xt_ready, xq_ready, xt_ps, xt_sb, h_ps, h_sb, hpeak_ready, hp_ready, hps_ready,
     h_scale, x_less, b2_added, t_ready, c_ready, hq_ready, y_ps, x_out, stored) = (sem("d_" + n) for n in names)

    def hold(eng):
        eng.sem_inc(held, 1)

    out_view = d["out"].rearrange("(a b) s c -> (b s) a c", b=2)
    flat_x = x_sb[:].rearrange("p t c -> p (t c)")

    def tokens(s):
        return flat_x[:, bass.ds(s * ST, ST)]

    block = ctx.enter_context(nc.Block())

    @block.sync
    def _(sp):
        sp.dma_start(wqt[:], g["ffn_weights"]).then_inc(w_in, 16)
        sp.dma_start(b1[:], d["L1_ffn_b1"].rearrange("(a p) -> p a", p=P), allow_slow_non_contiguous=True).then_inc(w_in, 16)
        sp.dma_start(b2[:], d["L1_ffn_b2"].partition_broadcast(P)).then_inc(w_in, 16)
        with sp.Fori(0, SUPERS) as s:
            sp.wait_ge(x_out, s + 1)
            hold(sp)
            sp.dma_start(out_view[:, bass.ds(s * QUAD, QUAD), :], x_sb[:, bass.ds(s * QUAD, QUAD), :])\
                .then_inc(stored, 16)
        sp.wait_ge(stored, 16 * SUPERS)

    @block.gpsimd
    def _(pool):
        pool.wait_ge(peak_ready, 2)
        pool.partition_all_reduce(peaks[:], peak[:], P, bass.bass_isa.ReduceOp.max).then_inc(peaks_ready, 1)
        pool.wait_ge(w_in, 48)
        pool.tensor_scalar(b2[:], b2[:], tg[:, 3:4], None, ALU.mult).then_inc(b2_ready, 1)
        pool.wait_ge(b2_ready, 1)

        def step(s, u):
            n = s + 2
            if there(n, SUPERS):
                if later(n, 2):
                    pool.wait_ge(xt_ps, n - 1)
                four = bass.ds(n * QUAD, QUAD)
                pool.tensor_tensor(xq32[:, u], x_sb[:, four, :], mean[:, four].unsqueeze(2).broadcast_to([P, QUAD, DM]),
                                   ALU.subtract).then_inc(x_less, 1)
                pool.wait_ge(x_less, n + 1)
                pool.tensor_tensor(xq32[:, u], xq32[:, u], rstd[:, four].unsqueeze(2).broadcast_to([P, QUAD, DM]),
                                   ALU.mult).then_inc(n_ready, 1)
                pool.tensor_tensor(x_sb[:, four, :], x_sb[:, four, :], b2[:].unsqueeze(1).broadcast_to([P, QUAD, DM]),
                                   ALU.add).then_inc(b2_added, 1)

        sweep(pool, step)
        pool.wait_ge(hp_ready, 2)
        pool.partition_all_reduce(hps[:], hp[:], P, bass.bass_isa.ReduceOp.max).then_inc(hps_ready, 1)

    @block.scalar
    def _(act):
        act.wait_ge(w_in, 48)
        act.wait_ge(x_scale, 1)

        def step(s, u):
            if there(s + 2, SUPERS):
                n = s + 2
                act.wait_ge(n_ready, n + 1)
                act.activation(xq32[:, u], xq32[:, u], ACT.Identity, scale=qs[0][:, 1:2], bias=qs[0][:, 7:8])\
                    .then_inc(xt_ready, 1)
            if there(s, SUPERS):
                for c in range(CHUNKS):
                    act.wait_ge(h_ps, s * 4 + c + 1)
                    act.activation(hid[:, bass.ds(s, 1), c, :].rearrange("p a t -> p (a t)"),
                                   ps_h[c][:].rearrange("p a b -> p (a b)"), ACT.Gelu,
                                   bias=b1[:, c:c + 1], scale=outscale[:, 0:1]).then_inc(h_sb, 1)
            if there(s + 1, SUPERS):
                n = s + 1
                act.wait_ge(xt_ps, n + 1)
                if later(n, 2):
                    act.wait_ge(h_ps, n * 4 - 4)
                act.activation(xqt[:, 1 - u], ps_x[:].rearrange("p a b -> p (a b)"), ACT.Identity,
                               bias=qs[0][:, 9:10]).then_inc(xt_sb, 1)

        sweep(act, step)
        act.wait_ge(h_scale, 1)
        with act.Fori(0, SUPERS) as s:
            h = hid[:, bass.ds(s, 1)].rearrange("p a c t -> p (a c t)")
            act.activation(h, h, ACT.Identity, scale=qs[1][:, 1:2], bias=qs[1][:, 7:8]).then_inc(t_ready, 1)

    @block.tensor
    def _(pe):
        pe.wait_ge(w_in, 48)

        def step(s, u):
            if there(s, SUPERS):
                pe.wait_ge(xt_sb, s + 1)
                for c in range(CHUNKS):
                    if later(s, 1):
                        pe.wait_ge(h_sb, s * 4 - 3 + c)
                    pe.matmul(ps_h[c][:].rearrange("p a b -> p (a b)"), wqt[:, 0, c], xqt[:, u],
                              start=True, stop=True).then_inc(h_ps, 1)
            if there(s + 1, SUPERS):
                n = s + 1
                pe.wait_ge(xq_ready, n + 1)
                if later(n, 1):
                    pe.wait_ge(xt_sb, n)
                for k in range(QUAD):
                    mm = pe.transpose(ps_x[:, k], xq32[:, 1 - u, k], ident[:])
                mm.then_inc(xt_ps, 1)

        sweep(pe, step)

        def second(s, u):
            pe.wait_ge(hq_ready, s + 1)
            if later(s, 2):
                pe.wait_ge(x_out, s - 1)
            for k in range(QUAD):
                for c in range(CHUNKS):
                    mm = pe.matmul(ps_y[u][:, k], hq[:, u, c, P * k:P * k + P], wqt[:, 1, c],
                                   start=(c == 0), stop=(c == CHUNKS - 1))
            mm.then_inc(y_ps, 1)

        for s in range(2):
            second(s, s)
        with pe.Fori(0, SUPERS // 2 - 1) as i:
            for u in range(2):
                second(i * 2 + 2 + u, u)

    @block.vector
    def _(dve):
        for e in range(2):
            dve.tensor_tensor(ext[:, e], ext[:, e], mean[:], ALU.subtract).then_inc(ext_ready, 1)
        dve.wait_ge(ext_ready, 2)
        for e in range(2):
            dve.tensor_tensor(ext[:, e], ext[:, e], rstd[:], ALU.mult).then_inc(ext_ready, 1)
        dve.wait_ge(ext_ready, 4)
        dve.tensor_scalar(ext[:, 1], ext[:, 1], -1.0, None, ALU.mult).then_inc(ext_ready, 1)
        dve.wait_ge(ext_ready, 5)
        for e in range(2):
            dve.tensor_reduce(peak[:, e:e + 1], ext[:, e], AX_X, ALU.max).then_inc(peak_ready, 1)
        dve.wait_ge(peaks_ready, 1)
        at = qscale(dve, qs[0], peaks[:, 0:1], peaks[:, 1:2], qstep, 0)
        dve.tensor_scalar(outscale[:, 0:1], wscale[:, 0:1], qs[0][:, 0:1], None, ALU.mult).then_inc(x_scale, 1)

        def step(s, u):
            n = s + 1
            if there(n, SUPERS):
                dve.wait_ge(xt_ready, n + 1)
                dve.tensor_scalar(xq32[:, 1 - u], xq32[:, 1 - u], qs[0][:, 8:9], qs[0][:, 6:7], ALU.max, ALU.min)\
                    .then_inc(xq_ready, 1)
            p = s - 1
            if there(p, SUPERS):
                dve.wait_ge(h_sb, p * 4 + 4)
                h = hid[:, bass.ds(p, 1)].rearrange("p a c t -> p (a c t)")
                for e, op in enumerate((ALU.max, ALU.min)):
                    dve.tensor_reduce(hpeak[:, e, bass.ds(p, 1)], h, AX_X, op).then_inc(hpeak_ready, 1)

        sweep(dve, step)
        dve.wait_ge(hpeak_ready, 2 * SUPERS)
        dve.tensor_reduce(hp[:, 0:1], hpeak[:, 0], AX_X, ALU.max).then_inc(hp_ready, 1)
        dve.tensor_reduce(hp[:, 1:2], hpeak[:, 1], AX_X, ALU.min).then_inc(hpeak_ready, 1)
        dve.wait_ge(hpeak_ready, 2 * SUPERS + 1)
        dve.tensor_scalar(hp[:, 1:2], hp[:, 1:2], -1.0, None, ALU.mult).then_inc(hp_ready, 1)
        dve.wait_ge(hps_ready, 1)
        at = qscale(dve, qs[1], hps[:, 0:1], hps[:, 1:2], qstep, at)
        dve.sem_inc(h_scale, 1)
        dve.tensor_scalar(outscale[:, 1:2], wscale[:, 1:2], qs[1][:, 0:1], tg[:, 3:4], ALU.mult, ALU.mult)\
            .then_inc(qstep, 1)
        dve.wait_ge(qstep, at + 1)

        def highest(s, u):
            dve.wait_ge(t_ready, s + 1)
            h = hid[:, bass.ds(s, 1)].rearrange("p a c t -> p (a c t)")
            if later(s, 2):
                dve.wait_ge(y_ps, s - 1)
            dve.tensor_scalar(hq[:, u].rearrange("p c t -> p (c t)"), h, qs[1][:, 6:7], MAGIC, ALU.min, ALU.subtract)\
                .then_inc(c_ready, 1)

        def lowest(s, u):
            q = hq[:, u].rearrange("p c t -> p (c t)")
            dve.wait_ge(c_ready, s + 1)
            dve.tensor_scalar(q, q, qs[1][:, 5:6], None, ALU.max).then_inc(hq_ready, 1)

        def finish(s, u):
            dve.wait_ge(y_ps, s + 1)
            dve.wait_ge(b2_added, s + 1)
            dve.scalar_tensor_tensor(out=tokens(s), in0=ps_y[u][:].rearrange("p a b -> p (a b)"), scalar=outscale[:, 1:2],
                                     in1=tokens(s), op0=ALU.mult, op1=ALU.add).then_inc(x_out, 1)

        for s in range(2):
            highest(s, s)
            lowest(s, s)
        with dve.Fori(0, SUPERS // 2 - 1) as i:
            for u in range(2):
                highest(i * 2 + 2 + u, u)
                finish(i * 2 + u, u)
                lowest(i * 2 + 2 + u, u)
        for s in range(SUPERS - 2, SUPERS):
            finish(s, s % 2)


EXPERTS = 8
RT = ST
REGION = NTOK + RT
ETILES = (2 * NTOK + EXPERTS * (RT - 1)) // RT
RW = DM + 4
SPARE = ETILES - 2 * NTOK // RT
PADDED = EXPERTS + SPARE


def mixture(nc, ctx, d, g, sb, sem):
    tokens_to = nc.dram_tensor("m_rows", (EXPERTS * REGION + SPARE * RT, RW), F32, kind="Internal").ap()
    results = g["results"] = nc.dram_tensor("m_results", (2 * NTOK + PADDED * RT, DM), F32, kind="Internal").ap()
    wall = sb("m_wall", [P, EXPERTS, 4, HID], F32R)
    ball = sb("m_ball", [P, EXPERTS, CHUNKS + 1], F32)
    tables = sb("m_tables", [1, 2, ETILES], U32)
    ends = sb("m_ends", [1, EXPERTS], U32)
    g["keys_t"] = nc.dram_tensor("m_keys_t", (P, NTOK), F32, kind="Internal").ap()
    g["values"] = nc.dram_tensor("m_values", (P, TILES, DM), F32, kind="Internal").ap()
    with ExitStack() as inner:
        route(nc, inner, d, g, sem, tokens_to, wall, ball, tables, ends)
    with ExitStack() as inner:
        experts(nc, inner, d, g, sem, tokens_to, results, wall, ball, tables)


def route(nc, ctx, d, g, sem, tokens_to, wall, ball, tables, ends):
    x_sb, ident, tg, mean, rstd = g["x_sb"], g["ident"], g["tanh_gates"], g["mean"], g["rstd"]

    def sb(name, shape, dt):
        return ctx.enter_context(nc.sbuf_tensor(name, shape, dt))

    CT = 2 * QUAD
    NCH = TILES // CT
    rows = sb("r_rows", [P, TILES, 2, RW], F32)
    xn = sb("r_xn", [P, 2, CT, DM], F32)
    xn_t = sb("r_xn_t", [P, 2, QUAD, P], F32)
    rw = sb("r_rw", [EXPERTS, DM], F32)
    rw_t = sb("r_rw_t", [P, EXPERTS], F32)
    raw = sb("r_raw", [P, 2, 2, HID], F32)
    bias_rows = sb("r_bias_rows", [EXPERTS * (CHUNKS + 1), P], F32)
    TE = [P, CT, EXPERTS]
    logits, work, first, second = (sb(f"r_{n}", TE, F32) for n in ("logits", "work", "first", "second"))
    chosen = sb("r_chosen", TE, BF16)
    order = sb("r_order", TE, F32)
    top = sb("r_top", [P, 2, CT], F32)
    pick = sb("r_pick", [P, CT], F32)
    gate = sb("r_gate", [P, 2, CT], F32)
    place = sb("r_place", [P, 2, CT], F32)
    place_u = sb("r_place_u", [P, 2, TILES], U32)
    before = sb("r_before", [P, P], BF16)
    ones = sb("r_ones", [P, P], BF16)
    total = sb("r_total", [P, EXPERTS, CT], F32)
    upto = sb("r_upto", [P, EXPERTS, CT], F32)
    resets = sb("r_resets", [P, EXPERTS, CT], F32)
    base = sb("r_base", [P, EXPERTS], F32)
    end = sb("r_end", [P, EXPERTS], F32)
    count = sb("r_count", [P, EXPERTS], F32)
    ntile = sb("r_ntile", [P, EXPERTS], F32)
    tile_end = sb("r_tile_end", [P, EXPERTS], F32)
    tnum = sb("r_tnum", [P, ETILES], F32)
    trow = sb("r_trow", [P, ETILES], F32)
    texp = sb("r_texp", [P, ETILES], F32)
    past = sb("r_past", [P, ETILES], F32)
    skip = sb("r_skip", [P, EXPERTS], F32)
    zeros = sb("r_zeros", [P, DM], F32)
    pad = sb("r_pad", [P, PADDED, RT // P, RW - DM], F32)

    wk, wv = (sb(f"r_w{n}", [P, DM], F32) for n in "kv")
    bk = sb("r_bk", [P, 1], F32)
    bv = sb("r_bv", [P, DM], F32)
    ctx_in = sb("r_ctx_in", [P, 2, QUAD, DM], F32)
    ctx_t = sb("r_ctx_t", [P, ST], F32)
    keys_t = sb("r_keys_t", [P, 2, ST], F32)
    values = sb("r_values", [P, 2, QUAD, DM], F32)

    def bank(name, shape, dt=F32):
        return ctx.enter_context(nc.psum_tensor(name, shape, dt))

    ps_t = [bank(f"r_ps_t{n}", [P, QUAD, P]) for n in range(2)]
    ps_l = bank("r_ps_l", [P, CT, 64])
    ps_cn = bank("r_ps_cn", [P, CT, 64])
    ps_w = bank("r_ps_w", [P, 4, P])
    ps_x, ps_k, ps_v0 = (bank(f"r_ps_{n}", [P, QUAD, P]) for n in ("x", "k", "v"))
    ps_v = (ps_v0, ps_w)

    names = ("w_in", "b_in", "xn_ready", "xt_ps", "xt_sb", "copied", "l_ps", "l_sb", "rwt_ps", "rwt_sb", "bias_ps",
             "bias_sb", "hi", "lo", "consts", "step", "diff", "ratio", "chosen", "cn_ps", "ends_ready", "tables_ready",
             "ids", "place_ready", "sent", "padded", "held", "kv_in",
             "ctx_in", "ct_ps", "ct_sb", "k_ps", "k_sb", "v_ps", "v_raw", "v_sb", "kv_out")
    (w_in, b_in, xn_ready, xt_ps, xt_sb, copied, l_ps, l_sb, rwt_ps, rwt_sb, bias_ps,
     bias_sb, hi_done, lo_done, consts, step_done, diff, ratio, chosen_ready, cn_ps, ends_ready, tables_ready,
     ids, place_ready, sent, padded, held, kv_in,
     ctx_ready, ct_ps, ct_sb, k_ps, k_sb, v_ps, v_raw, v_sb, kv_out) = (sem("r_" + n) for n in names)

    raw_in = [sem(f"r_raw_in{u}") for u in range(2)]

    def hold(eng):
        eng.sem_inc(held, 1)

    def padding(eng, n, first):
        for columns, src in ((slice(0, DM), zeros[:].unsqueeze(1).broadcast_to([P, RT // P, DM])),
                             (slice(DM, RW), pad[:, n])):
            eng.dma_start(tokens_to[bass.ds(first, RT), columns].rearrange("(p r) w -> p r w", p=P), src)\
                .then_inc(padded, 16)

    def padding_of(eng, e):
        end = eng.value_load(ends[0:1, e:e + 1], min_val=e * REGION, max_val=e * REGION + NTOK)
        padding(eng, SPARE + e, end)

    def chunks(eng, step):
        for c in range(-1, 3):
            step(c, c % 2)
        with eng.Fori(0, (NCH - 6) // 2) as i:
            step(i * 2 + 3, 1)
            step(i * 2 + 4, 0)
        for c in range(NCH - 3, NCH + 1):
            step(c, c % 2)

    with nc.Block() as block:
        @block.sync
        def _(sp):
            sp.dma_start(rw[:], d["L0_ffn_router_w"]).then_inc(w_in, 16)
            sp.dma_start(bias_rows[0:EXPERTS * CHUNKS, :], d["L0_ffn_b_fc"].rearrange("e (a p) -> (e a) p", p=P))\
                .then_inc(b_in, 16)
            sp.dma_start(bias_rows[EXPERTS * CHUNKS:, :], d["L0_ffn_b_proj"]).then_inc(b_in, 16)
            def load_context(n, u):
                if later(n, 1):
                    sp.wait_ge(ctx_ready, n * 16)
                    hold(sp)
                if later(n, 2):
                    sp.wait_ge(ct_ps, n - 1)
                    hold(sp)
                sp.dma_start(ctx_in[:, u], ctx_view[:, bass.ds(n * QUAD, QUAD), :]).then_inc(ctx_ready, 16)

            def store_keys_values(n, u):
                if later(n, 1):
                    sp.wait_ge(kv_out, n * 32)
                    hold(sp)
                sp.wait_ge(k_sb, n + 1)
                hold(sp)
                sp.dma_start(g["keys_t"][:, bass.ds(n * ST, ST)], keys_t[:, u]).then_inc(kv_out, 16)
                sp.wait_ge(v_sb, n + 1)
                hold(sp)
                sp.dma_start(g["values"][:, bass.ds(n * QUAD, QUAD), :], values[:, u]).then_inc(kv_out, 16)

            ctx_view = d["ctx_1024"].rearrange("(a b) s c -> (b s) a c", b=2)
            for dst, src in ((wk, "Wk"), (wv, "Wv")):
                sp.dma_start(dst[:], d["L1_xattn_" + src]).then_inc(kv_in, 16)
            sp.dma_start(bk[:], d["L1_xattn_bk"].rearrange("(p a) -> p a", a=1)).then_inc(kv_in, 16)
            sp.dma_start(bv[:], d["L1_xattn_bv"].partition_broadcast(P)).then_inc(kv_in, 16)
            for n in range(2):
                load_context(n, n)
            sp.wait_ge(consts, 6)
            for n in range(SPARE):
                padding(sp, n, EXPERTS * REGION + n * RT)
            with sp.Fori(0, SUPERS // 2 - 1) as i:
                for u in range(2):
                    store_keys_values(i * 2 + u, u)
                    load_context(i * 2 + 2 + u, u)
            for n in range(SUPERS - 2, SUPERS):
                store_keys_values(n, n % 2)
            sp.wait_ge(ends_ready, 1)
            for e in range(0, EXPERTS, 2):
                padding_of(sp, e)
            sp.wait_ge(padded, 32 * PADDED)
            sp.wait_ge(kv_out, 32 * SUPERS)

        @block.gpsimd
        def _(pool):
            pool.memset(before[:], 1.0).then_inc(consts, 1)
            pool.memset(ones[:], 1.0).then_inc(consts, 1)
            pool.memset(pad[:], 0.0).then_inc(consts, 1)
            pool.memset(zeros[:], 0.0).then_inc(consts, 1)
            pool.wait_ge(consts, 4)
            pool.affine_select(out=before[:], in_=before[:], compare_op=ALU.is_gt, fill=0.0, base=0,
                               pattern=[[1, P]], channel_multiplier=-1).then_inc(consts, 1)
            pool.iota(pad[:, :, :, 0], pattern=[[RT, PADDED], [1, RT // P]], base=2 * NTOK, channel_multiplier=RT // P,
                      allow_small_or_imprecise_dtypes=True).then_inc(consts, 1)
            pool.iota(order[:], pattern=[[0, CT], [-1, EXPERTS]], base=EXPERTS, channel_multiplier=0,
                      allow_small_or_imprecise_dtypes=True).then_inc(consts, 1)
            pool.iota(tnum[:], pattern=[[1, ETILES]], base=0, channel_multiplier=0,
                      allow_small_or_imprecise_dtypes=True).then_inc(consts, 1)
            pool.iota(base[:], pattern=[[REGION, EXPERTS]], base=0, channel_multiplier=0,
                      allow_small_or_imprecise_dtypes=True).then_inc(consts, 1)
            for k in range(2):
                pool.iota(rows[:, :, k, DM], pattern=[[2 * P, TILES]], base=k, channel_multiplier=2,
                          allow_small_or_imprecise_dtypes=True).then_inc(ids, 1)
                pool.memset(rows[:, :, k, DM + 2:RW], 0.0).then_inc(ids, 1)
            pool.wait_ge(ids, 4)
            for t in range(TILES):
                if t % CT == 0:
                    pool.wait_ge(copied, t // CT + 1)
                    pool.wait_ge(place_ready, (t // CT + 1) * 2)
                for k in range(2):
                    pool.indirect_dma_start(
                        tokens_to, bass.IndirectOffsetOnAxis(ap=place_u[:, k, t:t + 1], axis=0),
                        rows[:, t, k, :], None).then_inc(sent, 16)
            pool.wait_ge(sent, 32 * TILES)

        @block.scalar
        def _(act):
            act.wait_ge(rwt_ps, 1)
            act.activation(rw_t[:], ps_w[:, 0, 0:EXPERTS], ACT.Copy).then_inc(rwt_sb, 1)

            def raw_weights(e, u):
                if later(e, 2):
                    act.wait_ge(lo_done, e - 1)
                one = bass.ds(e, 1)
                act.dma_start(raw[:, u, 0], d["L0_ffn_w_fc"][one].rearrange("a p n -> p (a n)")).then_inc(raw_in[u], 16)
                act.dma_start(raw[:, u, 1].rearrange("p (a c) -> p a c", c=DM),
                              d["L0_ffn_w_proj"][one].rearrange("e (a p) c -> p (e a) c", p=P)).then_inc(raw_in[u], 16)

            def step(c, u):
                n = c + 1

                def keys(half):
                    s = c * 2 + half
                    act.wait_ge(ct_ps, s + 1)
                    if later(s, 1):
                        act.wait_ge(v_ps, s)
                    act.activation(ctx_t[:], ps_x[:].rearrange("p a b -> p (a b)"), ACT.Copy).then_inc(ct_sb, 1)
                    act.wait_ge(k_ps, s + 1)
                    if later(s, 2):
                        act.wait_ge(kv_out, s * 32 - 32)
                    act.activation(keys_t[:, half], ps_k[:].rearrange("p a b -> p (a b)"), ACT.Identity,
                                   bias=bk[:, 0:1]).then_inc(k_sb, 1)

                if there(n, NCH):
                    for half in range(2):
                        act.wait_ge(xt_ps, n * 2 + half + 1)
                        act.activation(xn_t[:, half], ps_t[half][:], ACT.Copy).then_inc(xt_sb, 1)
                if isinstance(c, int) and c == 0:
                    act.wait_ge(bias_ps, 1)
                    act.activation(ball[:, :, 0:CHUNKS], ps_w[:, 1, 0:EXPERTS * CHUNKS]
                                   .rearrange("p (e a) -> p e a", e=EXPERTS), ACT.Copy).then_inc(bias_sb, 1)
                    act.activation(ball[:, :, CHUNKS], ps_w[:, 1, EXPERTS * CHUNKS:EXPERTS * (CHUNKS + 1)], ACT.Copy)\
                        .then_inc(bias_sb, 1)
                    act.wait_ge(kv_in, 64)
                if there(c, NCH):
                    act.wait_ge(diff, c + 1)
                    act.activation(gate[:, 1], pick[:], ACT.Exp).then_inc(ratio, 1)
                if there(c - 1, NCH):
                    for half in range(2):
                        act.wait_ge(v_raw, c * 2 - 1 + half)
                        act.activation(values[:, half], values[:, half], ACT.Tanh).then_inc(v_sb, 1)
                if there(n, NCH):
                    act.wait_ge(xn_ready, n * CT + CT)
                    act.activation(rows[:, bass.ds(n * CT, CT), :, 0:DM],
                                   xn[:, 1 - u].unsqueeze(2).broadcast_to([P, CT, 2, DM]), ACT.Copy)\
                        .then_inc(copied, 1)
                if isinstance(c, int) and c == -1:
                    for e in range(2):
                        raw_weights(e, e)
                if there(c, NCH):
                    act.wait_ge(raw_in[u], (c - u) * 16 + 32)
                    hi = wall[:, bass.ds(c, 1)].rearrange("p a (k w) n -> p (a k) w n", w=2)[:, :, 0]
                    act.activation(hi, raw[:, u], ACT.Copy).then_inc(hi_done, 1)
                    for half in range(2):
                        keys(half)
                    if there(c + 2, EXPERTS):
                        raw_weights(c + 2, u)

            chunks(act, step)
            act.wait_ge(ends_ready, 1)
            for e in range(1, EXPERTS, 2):
                padding_of(act, e)

        @block.tensor
        def _(pe):
            pe.wait_ge(w_in, 16)
            pe.transpose(ps_w[:, 0, 0:EXPERTS], rw[:], ident[0:EXPERTS, 0:EXPERTS]).then_inc(rwt_ps, 1)
            pe.wait_ge(rwt_sb, 1)

            def step(c, u):
                n = c + 1

                def keys_values(half):
                    s = c * 2 + half
                    pe.wait_ge(ctx_ready, s * 16 + 16)
                    if later(s, 1):
                        pe.wait_ge(ct_sb, s)
                    for k in range(QUAD):
                        mm = pe.transpose(ps_x[:, k], ctx_in[:, half, k], ident[:])
                    mm.then_inc(ct_ps, 1)
                    pe.wait_ge(ct_sb, s + 1)
                    if later(s, 1):
                        pe.wait_ge(k_sb, s)
                    pe.matmul(ps_k[:].rearrange("p a b -> p (a b)"), wk[:], ctx_t[:], start=True, stop=True)\
                        .then_inc(k_ps, 1)
                    if later(s, 2):
                        pe.wait_ge(v_raw, s - 1)
                    for k in range(QUAD):
                        mm = pe.matmul(ps_v[half][:, k], ctx_t[:, P * k:P * k + P], wv[:], start=True, stop=True)
                    mm.then_inc(v_ps, 1)

                if there(n, NCH):
                    for half in range(2):
                        pe.wait_ge(xn_ready, n * CT + QUAD * half + QUAD)
                        if later(n, 1):
                            pe.wait_ge(xt_sb, n * 2 + half - 1)
                        for k in range(QUAD):
                            mm = pe.transpose(ps_t[half][:, k], xn[:, 1 - u, QUAD * half + k], ident[:])
                        mm.then_inc(xt_ps, 1)
                    for half in range(2):
                        pe.wait_ge(xt_sb, n * 2 + half + 1)
                        if half == 0 and later(n, 1):
                            pe.wait_ge(l_sb, n)
                        for k in range(QUAD):
                            mm = pe.matmul(ps_l[:, QUAD * half + k, 0:EXPERTS], xn_t[:, half, k], rw_t[:],
                                           start=True, stop=True)
                    mm.then_inc(l_ps, 1)
                if isinstance(c, int) and c == 0:
                    pe.wait_ge(b_in, 32)
                    rows_of_bias = EXPERTS * (CHUNKS + 1)
                    pe.transpose(ps_w[:, 1, 0:rows_of_bias], bias_rows[:], ident[0:rows_of_bias, 0:rows_of_bias])\
                        .then_inc(bias_ps, 1)
                    pe.wait_ge(consts, 5)
                    pe.wait_ge(kv_in, 64)
                    pe.wait_ge(bias_sb, 2)
                if there(c, NCH):
                    pe.wait_ge(chosen_ready, c + 1)
                    hold(pe)
                    for at, sums in ((0, before), (1, ones)):
                        pe.matmul(ps_cn[:, at:at + 1, :].rearrange("p a b -> p (a b)"), sums[:],
                                  chosen[:].rearrange("p t e -> p (t e)"), start=True, stop=True).then_inc(cn_ps, 1)
                    for half in range(2):
                        keys_values(half)

            chunks(pe, step)

        @block.vector
        def _(dve):
            STEPS = 31

            def wide(x):
                return x.unsqueeze(2).broadcast_to(TE)

            def step(c, u):
                n = c + 1
                if there(n, NCH):
                    if later(n, 2):
                        dve.wait_ge(xt_ps, n * 2 - 2)
                        dve.wait_ge(copied, n - 1)
                    for k in range(CT):
                        tile = n * CT + k
                        dve.tensor_scalar(xn[:, 1 - u, k], row(x_sb, tile), mean[:, bass.ds(tile, 1)],
                                          rstd[:, bass.ds(tile, 1)], ALU.subtract, ALU.mult).then_inc(xn_ready, 1)
                def values_of(half):
                    s = c * 2 - 2 + half
                    if not later(s, 1):
                        dve.wait_ge(kv_in, 64)
                    dve.wait_ge(v_ps, s + 1)
                    if later(s, 2):
                        dve.wait_ge(kv_out, s * 32 - 32)
                    dve.tensor_tensor(values[:, half], ps_v[half][:], bv[:].unsqueeze(1).broadcast_to([P, QUAD, DM]),
                                      ALU.add).then_inc(v_raw, 1)

                if isinstance(c, int) and c == NCH:
                    for half in range(2):
                        values_of(half)
                if not there(c, NCH):
                    return
                if isinstance(c, int) and c == 0:
                    dve.wait_ge(consts, 9)
                    dve.wait_ge(ids, 4)
                    dve.memset(resets[:], 1.0).then_inc(consts, 1)
                    dve.wait_ge(consts, 10)
                    dve.memset(resets[:, :, 0], 0.0).then_inc(consts, 1)
                    dve.tensor_copy(end[:], base[:]).then_inc(consts, 1)
                    dve.wait_ge(consts, 12)
                at = 0

                def then(ins):
                    nonlocal at
                    at += 1
                    ins.then_inc(step_done, 1)
                    dve.wait_ge(step_done, c * STEPS + at)
                    hold(dve)

                dve.wait_ge(l_ps, c + 1)
                hold(dve)
                then(dve.tensor_copy(logits[:], ps_l[:, :, 0:EXPERTS]))
                dve.sem_inc(l_sb, 1)
                for k, (src, hot) in enumerate(((logits, first), (work, second))):
                    then(dve.tensor_reduce(top[:, k], src[:], AX_X, ALU.max))
                    then(dve.tensor_tensor(hot[:], src[:], wide(top[:, k]), ALU.is_equal))
                    then(dve.tensor_tensor(hot[:], hot[:], order[:], ALU.mult))
                    then(dve.tensor_reduce(pick[:], hot[:], AX_X, ALU.max))
                    then(dve.tensor_tensor(hot[:], order[:], wide(pick[:]), ALU.is_equal))
                    if k == 0:
                        then(dve.scalar_tensor_tensor(out=work[:], in0=first[:], scalar=-FMAX, in1=logits[:],
                                                      op0=ALU.mult, op1=ALU.add))
                then(dve.tensor_tensor(chosen[:], first[:], second[:], ALU.add))
                dve.sem_inc(chosen_ready, 1)
                dve.tensor_tensor(pick[:], top[:, 1], top[:, 0], ALU.subtract).then_inc(diff, 1)
                if there(c - 1, NCH):
                    for half in range(2):
                        values_of(half)
                dve.wait_ge(cn_ps, c * 2 + 2)
                hold(dve)
                counts = [ps_cn[:, a:a + 1, :].rearrange("p a (t e) -> p (a t) e", e=EXPERTS) for a in range(2)]
                then(dve.tensor_copy(total[:].rearrange("p e t -> p t e"), counts[1]))
                then(dve.tensor_tensor_scan(upto[:].rearrange("p e t -> p (e t)"), resets[:].rearrange("p e t -> p (e t)"),
                                            total[:].rearrange("p e t -> p (e t)"), 0.0, ALU.mult, ALU.add))
                then(dve.tensor_tensor(upto[:], upto[:], wide_e(end[:]), ALU.add))
                then(dve.tensor_copy(end[:], upto[:, :, CT - 1]))
                then(dve.tensor_tensor(upto[:], upto[:], total[:], ALU.subtract))
                then(dve.tensor_tensor(work[:], counts[0], upto[:].rearrange("p e t -> p t e"), ALU.add))
                dve.wait_ge(ratio, c + 1)
                hold(dve)
                then(dve.tensor_scalar(gate[:, 0], gate[:, 1], 1.0, None, ALU.add))
                then(dve.reciprocal(gate[:, 0], gate[:, 0]))
                then(dve.tensor_scalar(gate[:, 0], gate[:, 0], tg[:, 2:3], None, ALU.mult))
                then(dve.tensor_tensor(gate[:, 1], gate[:, 1], gate[:, 0], ALU.mult))
                for k, hot in enumerate((first, second)):
                    then(dve.tensor_copy(rows[:, bass.ds(c * CT, CT), k, DM + 1], gate[:, k]))
                    then(dve.tensor_tensor(hot[:], hot[:], work[:], ALU.mult))
                    then(dve.tensor_reduce(place[:, k], hot[:], AX_X, ALU.add))
                    then(dve.tensor_copy(place_u[:, k, bass.ds(c * CT, CT)], place[:, k]))
                    dve.sem_inc(place_ready, 1)
                assert at == STEPS, at
                dve.wait_ge(hi_done, c + 1)
                parts = wall[:, bass.ds(c, 1)].rearrange("p a (k w) n -> p (a k) w n", w=2)
                dve.tensor_tensor(parts[:, :, 1], raw[:, u], parts[:, :, 0].bitcast(F32), ALU.subtract).then_inc(lo_done, 1)

            def wide_e(x):
                return x.unsqueeze(2).broadcast_to([P, EXPERTS, CT])

            chunks(dve, step)

            at = NCH * STEPS

            def then(ins):
                nonlocal at
                at += 1
                ins.then_inc(step_done, 1)
                dve.wait_ge(step_done, at)

            dve.tensor_copy(ends[:], end[0:1, :]).then_inc(ends_ready, 1)
            then(dve.tensor_tensor(count[:], end[:], base[:], ALU.subtract))
            then(dve.tensor_scalar(ntile[:], count[:], 1.0 / RT, (RT - 1.0) / RT - 0.5 + 0.5 / RT, ALU.mult, ALU.add))
            then(dve.tensor_scalar(ntile[:], ntile[:], MAGIC, MAGIC, ALU.add, ALU.subtract))
            then(dve.memset(skip[:], 1.0))
            then(dve.tensor_tensor_scan(tile_end[:], skip[:], ntile[:], 0.0, ALU.mult, ALU.add))
            then(dve.tensor_scalar(skip[:], ntile[:], -float(RT), float(REGION), ALU.mult, ALU.add))
            then(dve.tensor_scalar(trow[:], tnum[:], float(RT), None, ALU.mult))
            then(dve.memset(texp[:], 0.0))
            for e in range(EXPERTS):
                then(dve.tensor_scalar(past[:], tnum[:], tile_end[:, e:e + 1], None, ALU.is_ge))
                then(dve.scalar_tensor_tensor(out=trow[:], in0=past[:], scalar=skip[:, e:e + 1], in1=trow[:],
                                              op0=ALU.mult, op1=ALU.add))
                then(dve.tensor_tensor(texp[:], texp[:], past[:], ALU.add))
            then(dve.tensor_scalar(texp[:], texp[:], EXPERTS - 1.0, None, ALU.min))
            dve.tensor_copy(tables[0:1, 0], trow[0:1, :]).then_inc(tables_ready, 1)
            dve.tensor_copy(tables[0:1, 1], texp[0:1, :]).then_inc(tables_ready, 1)


def experts(nc, ctx, d, g, sem, tokens_to, results, wall, ball, tables):
    ident = g["ident"]

    def sb(name, shape, dt):
        return ctx.enter_context(nc.sbuf_tensor(name, shape, dt))

    NR = RT // P
    w_up = sb("e_w_up", [P, 2, 2, HID], F32R)
    w_down = sb("e_w_down", [P, 2, 2, HID], F32R)
    b_up = sb("e_b_up", [P, 2, CHUNKS], F32)
    b_down = sb("e_b_down", [P, 2, 1], F32)
    rows_in = sb("e_rows", [P, 2, NR, RW], F32)
    xt = sb("e_xt", [P, 2, 2, RT], F32R)
    h = sb("e_h", [P, 2, RT], F32)
    hp = sb("e_hp", [P, CHUNKS, 2, RT], F32R)
    yt = sb("e_yt", [P, RT], F32)
    y = sb("e_y", [P, 2, NR, DM], F32)
    to = sb("e_to", [P, 2, NR], U32)
    to_all = sb("e_to_all", [P, ETILES, NR], U32)
    weight = sb("e_weight", [P, ETILES, NR], F32)

    ps_x = ctx.enter_context(nc.psum_tensor("e_ps_x", [P, NR, P], F32))
    ps_h = [ctx.enter_context(nc.psum_tensor(f"e_ps_h{n}", [P, RT], F32)) for n in range(2)]
    ps_y = [ctx.enter_context(nc.psum_tensor(f"e_ps_y{n}", [P, RT], F32)) for n in range(2)]
    ps_r = ctx.enter_context(nc.psum_tensor("e_ps_r", [P, NR, P], F32))

    names = ("held", "up_in", "down_in", "rows_in", "xt_ps", "xt_hi", "xt_lo", "h_ps", "h_sb", "h_hi", "h_lo", "h_used",
             "meta_ready", "yt_sb", "yr_ps", "to_ready", "y_sb")
    (held, up_in, down_in, r_in, xt_ps, xt_hi, xt_lo, h_ps, h_sb, h_hi, h_lo, h_used,
     meta_ready, yt_sb, yr_ps, to_ready, y_sb) = (sem("e_" + n) for n in names)
    sent = [sem(f"e_sent{v}") for v in range(2)]

    def hold(eng):
        eng.sem_inc(held, 1)

    def tiles(eng, step):
        for t in range(-3, 4):
            step(t, t % 2)
        pairs = (ETILES - 7) // 2
        with eng.Fori(0, pairs) as i:
            step(i * 2 + 4, 0)
            step(i * 2 + 5, 1)
        for t in range(4 + 2 * pairs, ETILES + 1):
            step(t, t % 2)

    with nc.Block() as block:
        @block.sync
        def _(sp):
            def up_weights(n, v):
                expert = sp.value_load(tables[0:1, 1, bass.ds(n, 1)], min_val=0, max_val=EXPERTS - 1)
                sp.dma_start(w_up[:, v].bitcast(F32),
                             wall[:, bass.ds(expert, 1), 0:2].rearrange("p a k n -> p (a k) n").bitcast(F32))\
                    .then_inc(up_in, 16)
                sp.dma_start(b_up[:, v], ball[:, bass.ds(expert, 1), 0:CHUNKS].rearrange("p a k -> p (a k)"))\
                    .then_inc(up_in, 16)

            def step(t, u):
                n = t + 3
                if there(n, ETILES):
                    if later(n, 1):
                        sp.wait_ge(r_in, n * 16)
                        hold(sp)
                    if later(n, 2):
                        sp.wait_ge(xt_ps, n - 1)
                        hold(sp)
                        sp.wait_ge(meta_ready, n * 2 - 2)
                        hold(sp)
                    first = sp.value_load(tables[0:1, 0, bass.ds(n, 1)], min_val=0,
                                          max_val=EXPERTS * REGION + (SPARE - 1) * RT)
                    sp.dma_start(rows_in[:, 1 - u], tokens_to[bass.ds(first, RT), :]
                                 .rearrange("(p r) w -> p r w", p=P)).then_inc(r_in, 16)
                if isinstance(t, int) and t == -3:
                    up_weights(0, 0)
                n = t + 2
                if there(n, ETILES) and later(n, 1):
                    sp.wait_ge(up_in, n * 32)
                    hold(sp)
                    if later(n, 2):
                        sp.wait_ge(h_sb, n * 4 - 4)
                        hold(sp)
                    up_weights(n, u)
                n = t + 1
                if there(n, ETILES):
                    v = 1 - u
                    if later(n, 1):
                        sp.wait_ge(down_in, n * 32)
                        hold(sp)
                    if later(n, 2):
                        sp.wait_ge(yt_sb, n - 1)
                        hold(sp)
                    expert = sp.value_load(tables[0:1, 1, bass.ds(n, 1)], min_val=0, max_val=EXPERTS - 1)
                    sp.dma_start(w_down[:, v].bitcast(F32),
                                 wall[:, bass.ds(expert, 1), 2:4].rearrange("p a k n -> p (a k) n").bitcast(F32))\
                        .then_inc(down_in, 16)
                    sp.dma_start(b_down[:, v], ball[:, bass.ds(expert, 1), CHUNKS:].rearrange("p a k -> p (a k)"))\
                        .then_inc(down_in, 16)

            tiles(sp, step)

        @block.gpsimd
        def _(pool):
            def step(t, u):
                n = t - 1
                if there(n, ETILES):
                    v = 1 - u
                    pool.wait_ge(meta_ready, n * 2 + 2)
                    if later(n, 2):
                        pool.wait_ge(sent[v], (n - v) * 32)
                    hold(pool)
                    pool.tensor_copy(to[:, v], to_all[:, bass.ds(n, 1)].rearrange("p a r -> p (a r)"))\
                        .then_inc(to_ready, 1)
                    pool.wait_ge(to_ready, n + 1)
                    for r in range(NR):
                        pool.wait_ge(y_sb, n * NR + r + 1)
                        hold(pool)
                        pool.indirect_dma_start(
                            results, bass.IndirectOffsetOnAxis(ap=to[:, v, r:r + 1], axis=0),
                            y[:, v, r], None).then_inc(sent[v], 16)

            tiles(pool, step)
            for v in range(2):
                pool.wait_ge(sent[v], 16 * NR * ((ETILES + 1 - v) // 2))

        @block.scalar
        def _(act):
            def step(t, u):
                n, m = t + 1, t + 2

                def gelu(c):
                    act.wait_ge(h_ps, n * 4 + c + 1)
                    if c >= 2 or later(n, 1):
                        act.wait_ge(h_lo, n * 4 + c - 1)
                    act.activation(h[:, c % 2], ps_h[c % 2][:], ACT.Gelu_apprx_tanh,
                                   bias=b_up[:, 1 - u, c:c + 1]).then_inc(h_sb, 1)

                if there(t - 1, ETILES):
                    v = 1 - u
                    act.wait_ge(h_used, t * 4)
                    if later(t - 1, 1):
                        act.wait_ge(yr_ps, t - 1)
                    act.activation(yt[:], ps_y[v][:], ACT.Identity, bias=b_down[:, v]).then_inc(yt_sb, 1)
                if there(n, ETILES):
                    act.wait_ge(up_in, n * 32 + 32)
                    gelu(0)
                if there(m, ETILES):
                    act.wait_ge(xt_ps, m + 1)
                    if later(m, 2):
                        act.wait_ge(h_ps, m * 4 - 4)
                    act.activation(xt[:, u, 0], ps_x[:].rearrange("p r t -> p (r t)"), ACT.Copy).then_inc(xt_hi, 1)
                if there(n, ETILES):
                    gelu(1)
                if there(t - 1, ETILES):
                    if later(t - 1, 2):
                        act.wait_ge(sent[v], (t - 1 - v) * 32)
                    act.wait_ge(meta_ready, t * 2)
                    act.wait_ge(yr_ps, t)
                    for r in range(NR):
                        act.activation(y[:, v, r], ps_r[:, r], ACT.Copy,
                                       scale=weight[:, bass.ds(t - 1, 1), r]).then_inc(y_sb, 1)
                if there(n, ETILES):
                    gelu(2)
                    gelu(3)

            tiles(act, step)

        @block.tensor
        def _(pe):
            def step(t, u):
                n, m = t + 1, t + 2

                def up(c):
                    v = 1 - u
                    if c == 0:
                        pe.wait_ge(up_in, n * 32 + 32)
                        pe.wait_ge(xt_hi, n + 1)
                    if later(n, 1) or c >= 2:
                        pe.wait_ge(h_sb, n * 4 + c - 1)
                    at = slice(P * c, P * c + P)
                    pe.matmul(ps_h[c % 2][:], w_up[:, v, 0, at], xt[:, v, 0], start=True, stop=False)
                    pe.matmul(ps_h[c % 2][:], w_up[:, v, 1, at], xt[:, v, 0], start=False, stop=False)
                    if c == 0:
                        pe.wait_ge(xt_lo, n + 1)
                    pe.matmul(ps_h[c % 2][:], w_up[:, v, 0, at], xt[:, v, 1], start=False, stop=True).then_inc(h_ps, 1)

                def down(c):
                    if c == 0:
                        pe.wait_ge(down_in, t * 32 + 32)
                        if later(t, 2):
                            pe.wait_ge(yt_sb, t - 1)
                    pe.wait_ge(h_lo, t * 4 + c + 1)
                    at = slice(P * c, P * c + P)
                    pe.matmul(ps_y[u][:], w_down[:, u, 0, at], hp[:, c, 0], start=(c == 0), stop=False)
                    pe.matmul(ps_y[u][:], w_down[:, u, 1, at], hp[:, c, 0], start=False, stop=False)
                    pe.matmul(ps_y[u][:], w_down[:, u, 0, at], hp[:, c, 1], start=False, stop=(c == CHUNKS - 1))\
                        .then_inc(h_used, 1)

                for c in range(CHUNKS):
                    if there(n, ETILES):
                        up(c)
                    if there(t, ETILES):
                        down(c)
                    if c == 0:
                        if there(m, ETILES):
                            pe.wait_ge(r_in, m * 16 + 16)
                            if later(m, 1):
                                pe.wait_ge(xt_lo, m)
                            for r in range(NR):
                                mm = pe.transpose(ps_x[:, r], rows_in[:, u, r, 0:DM], ident[:])
                            mm.then_inc(xt_ps, 1)
                        if there(t - 1, ETILES):
                            pe.wait_ge(yt_sb, t)
                            if later(t - 1, 1):
                                pe.wait_ge(y_sb, t * 4 - 4)
                            for r in range(NR):
                                mm = pe.transpose(ps_r[:, r], yt[:, P * r:P * r + P], ident[:])
                            mm.then_inc(yr_ps, 1)

            tiles(pe, step)

        @block.vector
        def _(dve):
            def step(t, u):
                n, m = t + 1, t + 2

                def split(c):
                    dve.wait_ge(h_sb, n * 4 + c + 1)
                    if later(n, 1):
                        dve.wait_ge(h_used, t * 4 + c + 1)
                    dve.tensor_copy(hp[:, c, 0], h[:, c % 2]).then_inc(h_hi, 1)
                    dve.wait_ge(h_hi, n * 4 + c + 1)
                    dve.tensor_tensor(hp[:, c, 1], h[:, c % 2], hp[:, c, 0].bitcast(F32),
                                      ALU.subtract).then_inc(h_lo, 1)

                if there(n, ETILES):
                    split(0)
                if there(m, ETILES):
                    dve.wait_ge(r_in, m * 16 + 16)
                    hold(dve)
                    dve.tensor_copy(to_all[:, bass.ds(m, 1)].rearrange("p a r -> p (a r)"), rows_in[:, u, :, DM])\
                        .then_inc(meta_ready, 1)
                    dve.tensor_copy(weight[:, bass.ds(m, 1)].rearrange("p a r -> p (a r)"),
                                    rows_in[:, u, :, DM + 1]).then_inc(meta_ready, 1)
                    dve.wait_ge(xt_hi, m + 1)
                    if later(m, 2):
                        dve.wait_ge(h_ps, m * 4 - 4)
                    dve.tensor_tensor(xt[:, u, 1], ps_x[:].rearrange("p r t -> p (r t)"),
                                      xt[:, u, 0].bitcast(F32), ALU.subtract).then_inc(xt_lo, 1)
                if there(n, ETILES):
                    split(1)
                    split(2)
                    split(3)

            tiles(dve, step)


TWO_LOADS = ((0, 1), (1, 2), (2, 3), (3, 6), (6, 9), (9, 12), (12, 14), (14, 16))


def gather(nc, ctx, d, g, sb, sem):
    x_sb, stats, ident, wscale = g["x_sb"], g["stats"], g["ident"], g["wscale"]
    two = sb("f_two", [P, SUPERS, QUAD, 2, DM], F32)
    w = sb("f_w", [P, 2, CHUNKS, P], F32)
    wt = sb("f_wt", [P, 2, CHUNKS, P], BF16)
    wpeak = sb("f_wpeak", [P, 2], F32)
    wpeaks = sb("f_wpeaks", [P, 2], F32)
    winv = sb("f_winv", [P, 2], F32)
    magic = sb("f_magic", [P, 2], F32)
    two_in = [sem(f"f_two_in{n}") for n in range(len(TWO_LOADS))]
    added, summed, x_out = sem("f_added"), sem("f_summed"), sem("f_x_out")
    w_in, consts, wpeak_ready, wpeaks_ready, scaled, w_ready, clamped, wt_ps, wt_sb, wt_out = (
        sem("f_" + n) for n in ("w_in", "consts", "wpeak_ready", "wpeaks_ready", "scaled", "w_ready", "clamped",
                                "wt_ps", "wt_sb", "wt_out"))
    scales = scale_buffers(sb, sem, "mid")
    ps_w = [ctx.enter_context(nc.psum_tensor(f"f_ps_w{n}", [P, CHUNKS, P], F32)) for n in range(2)]
    view = g["results"][0:2 * NTOK, :].rearrange("(t p k) c -> p t k c", p=P, k=2)
    wt_dram = g["ffn_weights"] = nc.dram_tensor("f_wt_dram", (P, 2, CHUNKS, P), BF16, kind="Internal").ap()

    early = g["layer1"] = {
        "wq": sb("c_wq", [P, DM], F32), "bq": sb("c_bq", [P, 1], F32),
        "mask_u8": sb("c_mask_u8", [1, SUPERS, ST], U8),
        "keys_t": sb("c_keys_t", [P, 2, ST], F32), "vals": sb("c_vals", [P, 2, QUAD, DM], F32),
        "term_k": sb("c_term_k", [65, 2, QUAD, 2, SEQ], BF16), "term_q": sb("c_term_q", [65, P], BF16)}
    early.update({n: sem(f"c_{n}") for n in ("w_in", "m_in", "k_in", "v_in", "terms")})

    def sum_two(pool, n):
        four = slice(*TWO_LOADS[n])
        pool.wait_ge(two_in[n], 16)
        pool.tensor_tensor(two[:, four, :, 0], two[:, four, :, 0], two[:, four, :, 1], ALU.add).then_inc(added, 1)

    def add_to_x(dve, n):
        first, end = TWO_LOADS[n]
        xs = x_sb[:, first * QUAD:end * QUAD, :].rearrange("p (s t) c -> p s t c", t=QUAD)
        if n == FIRST_LOADS:
            dve.wait_ge(two_in[n], 16)
            dve.tensor_tensor(two[:, first:end, :, 0], two[:, first:end, :, 0], two[:, first:end, :, 1], ALU.add)\
                .then_inc(summed, 1)
            dve.wait_ge(summed, 1)
        else:
            dve.wait_ge(added, n + 1 if n < FIRST_LOADS else n)
        dve.tensor_tensor(xs, xs, two[:, first:end, :, 0], ALU.add).then_inc(x_out, 1)

    def row_stats(dve, n):
        first, end = TWO_LOADS[n]
        dve.wait_ge(x_out, n + 1)
        for t in range(first * QUAD, end * QUAD):
            dve.bn_stats(stats[:, t], x_sb[:, t]).then_inc(scales["stats_out"], 1)

    FIRST_LOADS = FIRST // QUAD
    assert TWO_LOADS[FIRST_LOADS][0] == FIRST_LOADS

    def other_sums(pool):
        for n in range(FIRST_LOADS + 1, len(TWO_LOADS)):
            sum_two(pool, n)

    def other_rows(dve):
        for n in range(FIRST_LOADS, len(TWO_LOADS)):
            add_to_x(dve, n)
            if n > FIRST_LOADS:
                row_stats(dve, n - 1)
        row_stats(dve, len(TWO_LOADS) - 1)
        scales_on_dve(dve, g, scales, 1, slice(FIRST, TILES))

    g["gather"] = {"other_sums": other_sums, "other_rows": other_rows, "scales": scales, "wt_out": wt_out}
    block = ctx.enter_context(nc.Block())

    @block.sync
    def _(sp):
        sp.dma_start(w[:, 0], d["L1_ffn_W1"].rearrange("(a p) c -> p a c", p=P)).then_inc(w_in, 16)
        sp.dma_start(w[:, 1], d["L1_ffn_W2"].rearrange("c (a p) -> c a p", p=P)).then_inc(w_in, 16)
        for n, (first, end) in enumerate(TWO_LOADS):
            if n == FIRST_LOADS:
                sp.dma_start(early["wq"][:], d["L1_xattn_Wq"]).then_inc(early["w_in"], 16)
                sp.dma_start(early["bq"][:], d["L1_xattn_bq"].rearrange("(p a) -> p a", a=1)).then_inc(early["w_in"], 16)
                sp.dma_start(early["mask_u8"][:], d["mask_BxS2_bk1"].rearrange("(a s b) k -> a s (b k)", a=1, s=SUPERS))\
                    .then_inc(early["m_in"], 16)
                sp.dma_start(early["keys_t"][:, 0], g["keys_t"][:, 0:ST]).then_inc(early["k_in"], 16)
                sp.dma_start(early["vals"][:, 0], g["values"][:, 0:QUAD, :]).then_inc(early["v_in"], 16)
            sp.dma_start(two[:, first:end].rearrange("p s t k c -> p (s t) k c"), view[:, QUAD * first:QUAD * end])\
                .then_inc(two_in[n], 16)

    @block.gpsimd
    def _(pool):
        pool.memset(magic[:, 0:1], MAGIC).then_inc(consts, 1)
        pool.memset(magic[:, 1:2], -MAGIC).then_inc(consts, 1)
        pool.wait_ge(consts, 2)
        term_k, term_q, terms = early["term_k"], early["term_q"], early["terms"]
        pool.memset(term_k[:], 0.0).then_inc(terms, 1)
        pool.memset(term_q[:], 0.0).then_inc(terms, 1)
        pool.wait_ge(terms, 2)
        for u in range(2):
            pool.memset(term_k[32:33, u, :, 1, :], -1e30).then_inc(terms, 1)
            pool.memset(term_k[64:65, u, :, 0, :], -1e30).then_inc(terms, 1)
        pool.memset(term_q[0:1, :], 1.0).then_inc(terms, 1)
        pool.memset(term_q[32:33, 0:SEQ], 1.0).then_inc(terms, 1)
        pool.memset(term_q[64:65, SEQ:P], 1.0).then_inc(terms, 1)
        pool.wait_ge(terms, 9)
        pool.wait_ge(wpeak_ready, 2)
        pool.partition_all_reduce(wpeaks[:], wpeak[:], P, bass.bass_isa.ReduceOp.max).then_inc(wpeaks_ready, 1)
        for n in range(FIRST_LOADS):
            sum_two(pool, n)

    @block.scalar
    def _(act):
        act.wait_ge(consts, 2)
        for n in range(2):
            act.wait_ge(scaled, 2)
            act.activation(w[:, n], w[:, n], ACT.Identity, scale=winv[:, n:n + 1], bias=magic[:, 0:1]).then_inc(w_ready, 1)
        scales_on_act(act, scales, 0)
        for n in range(2):
            act.wait_ge(wt_ps, n + 1)
            act.activation(wt[:, n], ps_w[n][:], ACT.Identity, bias=magic[:, 1:2]).then_inc(wt_sb, 1)
        act.wait_ge(wt_sb, 2)
        act.dma_start(wt_dram, wt[:]).then_inc(wt_out, 16)

    @block.tensor
    def _(pe):
        for n in range(2):
            pe.wait_ge(clamped, n + 1)
            for c in range(CHUNKS):
                mm = pe.transpose(ps_w[n][:, c], w[:, n, c], ident[:])
            mm.then_inc(wt_ps, 1)

    @block.vector
    def _(dve):
        dve.wait_ge(w_in, 32)
        for n in range(2):
            dve.tensor_reduce(wpeak[:, n:n + 1], w[:, n].rearrange("p a b -> p (a b)"), AX_X, ALU.max,
                              apply_absolute_value=True).then_inc(wpeak_ready, 1)
        dve.wait_ge(wpeaks_ready, 1)
        dve.tensor_scalar(wscale[:], wpeaks[:], 1.0 / 127.0, 1e-8, ALU.mult, ALU.max).then_inc(scaled, 1)
        dve.wait_ge(scaled, 1)
        dve.reciprocal(winv[:], wscale[:]).then_inc(scaled, 1)
        for n in range(FIRST_LOADS):
            add_to_x(dve, n)
            if n:
                row_stats(dve, n - 1)
        row_stats(dve, FIRST_LOADS - 1)
        scales_on_dve(dve, g, scales, 0, slice(0, FIRST))
        for n in range(2):
            dve.wait_ge(w_ready, n + 1)
            dve.tensor_scalar(w[:, n], w[:, n], MAGIC - 127.0, MAGIC + 127.0, ALU.max, ALU.min).then_inc(clamped, 1)


FIRST = 3 * QUAD
X_LOADS = [(t, t + QUAD) for t in range(0, FIRST, QUAD)] + [(t, t + 13) for t in range(FIRST, TILES, 13)]


def setup(nc, ctx, d, g, sb, sem):
    x_sb, stats, ident, tg = g["x_sb"], g["stats"], g["ident"], g["tanh_gates"]
    w = g["layer0"] = {n: sb(f"a_{n}", [P, DM], F32) for n in ("wq", "wk", "wv", "wo", "bv", "bo")}
    w.update({n: sb(f"a_{n}", [P, 1], F32) for n in ("bq", "bk")})
    w["mask"] = sb("a_mask", [P, SEQ], F32)
    w["ctx_in"] = sb("a_ctx_in", [P, 2, QUAD, DM], F32)
    w.update({n: sem(f"a_{n}") for n in ("qk_in", "w_in", "loaded")})
    x_in = w["x_in"] = [sem(f"x_in{n}") for n in range(len(X_LOADS))]
    scales = w["scales"] = scale_buffers(sb, sem, "first")
    gates_in, ident_step, gates_ready = sem("gates_in"), sem("ident_step"), sem("gates_ready")
    x_view = d["x"].rearrange("(a b) s c -> (b s) a c", b=2)
    ctx_view = d["ctx_1024"].rearrange("(a b) s c -> (b s) a c", b=2)
    block = ctx.enter_context(nc.Block())

    @block.sync
    def _(sp):
        def load_x(n):
            first, end = X_LOADS[n]
            sp.dma_start(x_sb[:, first:end, :], x_view[:, first:end, :]).then_inc(x_in[n], 16)

        for n in range(FIRST // QUAD):
            load_x(n)
        sp.dma_start(w["ctx_in"][:, 0], ctx_view[:, 0:QUAD, :]).then_inc(w["loaded"], 16)
        for n, name in enumerate(("g_xattn", "g_ffn")):
            sp.dma_start(tg[:, 2 * n:2 * n + 2], d[name].partition_broadcast(P))\
                .then_inc(gates_in, 16)
        for n in "qk":
            sp.dma_start(w["w" + n][:], d["L0_xattn_W" + n]).then_inc(w["qk_in"], 16)
            sp.dma_start(w["b" + n][:], d["L0_xattn_b" + n].rearrange("(p a) -> p a", a=1)).then_inc(w["qk_in"], 16)
        for n in "vo":
            sp.dma_start(w["w" + n][:], d["L0_xattn_W" + n]).then_inc(w["w_in"], 16)
            sp.dma_start(w["b" + n][:], d["L0_xattn_b" + n].partition_broadcast(P)).then_inc(w["w_in"], 16)
        for b in range(2):
            sp.dma_start(w["mask"][SEQ * b:SEQ * b + SEQ, :],
                         d["mask_1x1xSxS2_ff0"].rearrange("a b q k -> (a b q) k")).then_inc(w["w_in"], 16)
        for n in range(FIRST // QUAD, len(X_LOADS)):
            load_x(n)

    @block.gpsimd
    def _(pool):
        pool.memset(ident[:], 0.0).then_inc(ident_step, 1)
        pool.wait_ge(ident_step, 1)
        pool.affine_select(out=ident[:], in_=ident[:], compare_op=ALU.not_equal, fill=1.0, base=0,
                           pattern=[[-1, P]], channel_multiplier=1).then_inc(ident_step, 1)

    @block.scalar
    def _(act):
        scales_on_act(act, scales, 0)
        act.wait_ge(gates_in, 32)
        act.activation(tg[:], tg[:], ACT.Tanh).then_inc(gates_ready, 1)

    @block.vector
    def _(dve):
        for n in range(FIRST // QUAD):
            dve.wait_ge(x_in[n], 16)
            for t in range(*X_LOADS[n]):
                dve.bn_stats(stats[:, t], x_sb[:, t]).then_inc(scales["stats_out"], 1)
        scales_on_dve(dve, g, scales, 0, slice(0, FIRST))


def scale_buffers(sb, sem, name):
    room = {n: sb(f"ln_{n}_{name}", [P, TILES], F32) for n in ("diff", "var")}
    room.update({n: sem(f"ln_{n}_{name}") for n in ("stats_out", "step", "var_ready", "std_ready", "done")})
    return room


def scales_on_dve(dve, g, room, nth, tiles):
    stats, mean, rstd = (g[n][:, tiles] for n in ("stats", "mean", "rstd"))
    diff, var = room["diff"][:, tiles], room["var"][:, tiles]
    step = room["step"]
    if nth or tiles.stop < TILES:
        dve.wait_ge(room["stats_out"], tiles.stop)
    dve.tensor_tensor(mean, stats[:, :, 1], stats[:, :, 4], ALU.add).then_inc(step, 1)
    dve.tensor_tensor(diff, stats[:, :, 1], stats[:, :, 4], ALU.subtract).then_inc(step, 1)
    dve.tensor_tensor(var, stats[:, :, 2], stats[:, :, 5], ALU.add).then_inc(step, 1)
    dve.wait_ge(step, nth * 6 + 1)
    dve.tensor_scalar(mean, mean, 0.5, None, ALU.mult).then_inc(step, 1)
    dve.wait_ge(step, nth * 6 + 2)
    dve.tensor_tensor(diff, diff, diff, ALU.mult).then_inc(step, 1)
    dve.wait_ge(step, nth * 6 + 3)
    dve.tensor_scalar(var, var, 1.0 / DM, LN_EPS, ALU.mult, ALU.add).then_inc(step, 1)
    dve.wait_ge(step, nth * 6 + 6)
    dve.scalar_tensor_tensor(out=var, in0=diff, scalar=0.25, in1=var,
                             op0=ALU.mult, op1=ALU.add).then_inc(room["var_ready"], 1)
    dve.wait_ge(room["std_ready"], nth + 1)
    dve.reciprocal(rstd, var).then_inc(room["done"], 1)


def scales_on_act(act, room, nth, tiles=None):
    tiles = tiles or (slice(0, FIRST), slice(FIRST, TILES))[nth]
    act.wait_ge(room["var_ready"], nth + 1)
    act.activation(room["var"][:, tiles], room["var"][:, tiles], ACT.Sqrt).then_inc(room["std_ready"], 1)


def layernorm_scales(nc, ctx, d, g, sb, sem):
    g["uid"] = g["uid"] + 1
    room = scale_buffers(sb, sem, g["uid"])
    every = slice(0, TILES)
    block = ctx.enter_context(nc.Block())

    @block.vector
    def _(dve):
        scales_on_dve(dve, g, room, 0, every)

    @block.scalar
    def _(act):
        scales_on_act(act, room, 0, every)


def store_x(nc, ctx, d, g, sb, sem):
    stored = sem("stored")
    block = ctx.enter_context(nc.Block())

    @block.sync
    def _(sp):
        sp.dma_start(d["out"].rearrange("(a b) s c -> (b s) a c", b=2), g["x_sb"][:]).then_inc(stored, 16)
        sp.wait_ge(stored, 16)


STAGES = ((setup, layer0_attention), (layernorm_scales,), (mixture,),
          (gather, layer1_attention), (layernorm_scales, layer1_ffn))


def flamingo(nc, d, stages=None):
    with ExitStack() as whole:
        g = {
            "x_sb": whole.enter_context(nc.sbuf_tensor("x_sb", [P, TILES, DM], F32)),
            "stats": whole.enter_context(nc.sbuf_tensor("stats", [P, TILES, 6], F32)),
            "mean": whole.enter_context(nc.sbuf_tensor("mean", [P, TILES], F32)),
            "rstd": whole.enter_context(nc.sbuf_tensor("rstd", [P, TILES], F32)),
            "ext": whole.enter_context(nc.sbuf_tensor("ext", [P, 2, TILES], F32)),
            "wscale": whole.enter_context(nc.sbuf_tensor("wscale", [P, 2], F32)),
            "uid": 0,
            "ident": whole.enter_context(nc.sbuf_tensor("ident", [P, P], F32)),
            "tanh_gates": whole.enter_context(nc.sbuf_tensor("tanh_gates", [P, 4], F32)),
        }
        for group in stages or STAGES:
            with ExitStack() as shared:
                def sb(name, shape, dt):
                    return shared.enter_context(nc.sbuf_tensor(name, shape, dt))

                def sem(name):
                    group_sems.append(nc.alloc_semaphore(name=name))
                    return group_sems[-1]

                group_sems = []
                for stage in group:
                    with ExitStack() as ctx:
                        stage(nc, ctx, d, g, sb, sem)
            nc.clear_and_free_semaphores(group_sems)
            nc.all_engine_barrier()


_INS = ["x", "ctx_1024", "mask_1x1xSxS2_ff0", "mask_BxS2_bk1", "g_xattn", "g_ffn",
        "L0_xattn_Wq", "L0_xattn_bq", "L0_xattn_Wk", "L0_xattn_bk", "L0_xattn_Wv", "L0_xattn_bv",
        "L0_xattn_Wo", "L0_xattn_bo", "L0_ffn_router_w", "L0_ffn_w_fc", "L0_ffn_b_fc", "L0_ffn_w_proj",
        "L0_ffn_b_proj", "L1_xattn_Wq", "L1_xattn_bq", "L1_xattn_Wk", "L1_xattn_bk", "L1_xattn_Wv",
        "L1_xattn_bv", "L1_ffn_W1", "L1_ffn_b1", "L1_ffn_W2", "L1_ffn_b2"]


def kernel(**inputs):
    import numpy as _np
    import concourse.bacc as _bacc
    from concourse import mybir as _mybir
    from concourse.bass_utils import run_bass_kernel_spmd as _run

    nc = _bacc.Bacc("TRN2", target_bir_lowering=False, num_devices=1)
    arrays, d = {}, {}
    for name in _INS:
        a = _np.ascontiguousarray(inputs[name])
        arrays[f"in_{name}_dram"] = a
        d[name] = nc.dram_tensor(f"in_{name}_dram", a.shape, _mybir.dt.from_np(a.dtype), kind="ExternalInput").ap()
    d["out"] = nc.dram_tensor("out_dram", (BATCH, SEQ, DM), F32, kind="ExternalOutput").ap()
    flamingo(nc, d)
    r = _run(nc, [arrays], core_ids=[0])
    return r.results[0]["out_dram"]
```
